# Optimizing a Trainium2 kernel written in Bass

```python
import numpy as np
import jax
import jax.numpy as jnp

def _softmax(x, axis=-1):
    return jax.nn.softmax(x, axis=axis)

def _gelu(x):
    return jax.nn.gelu(x, approximate=True)

def _silu(x):
    return jax.nn.silu(x)

def _sigmoid(x):
    return jax.nn.sigmoid(x)

def _layernorm(x, axis=-1, eps=1e-05):
    m = jnp.mean(x, axis=axis, keepdims=True)
    v = jnp.var(x, axis=axis, keepdims=True)
    return (x - m) / jnp.sqrt(v + eps)

def _scatter_add(tgt, idx, src, axis=0):
    return tgt.at[idx].add(src)

def _segment_sum(src, seg, n):
    return jax.ops.segment_sum(src, seg, n)
kernel_name = 'mk_gnn_ffn_d2_gnn_r32_db640d'

def setup_inputs(seed: int=0):
    np.random.seed(seed)
    _w = jnp.asarray

    def _rec_inputs():
        import jax
        import jax.numpy as jnp
        _gk = jax.random.key(seed)
        x = -0.0003713 + 1 * jax.random.normal(jax.random.fold_in(_gk, 1), (3125, 256), jnp.float32)
        _s = jax.random.randint(jax.random.fold_in(_gk, 2), (25000,), 0, 3125, jnp.int32)
        _d = jax.random.randint(jax.random.fold_in(_gk, 3), (25000,), 0, 3125, jnp.int32)
        _loop = jnp.arange(3125, dtype=jnp.int32)
        src = jnp.concatenate([_s, _d, _loop])
        dst = jnp.concatenate([_d, _s, _loop])
        _o = jnp.argsort(dst, stable=True)
        src = src[_o]
        dst = dst[_o]
        edge_attr_128 = -5.16925e-05 + 1.00005 * jax.random.normal(jax.random.fold_in(_gk, 11), (53125, 128), jnp.float32)
        edge_weight = jax.random.uniform(jax.random.fold_in(_gk, 13), (53125,), jnp.float32, 0.0, 1)
        return (x, src, dst, edge_attr_128, edge_weight)
    x, src, dst, edge_attr_128, edge_weight = _rec_inputs()

    def _L0_gnn_setup():
        import jax, jax.numpy as jnp
        import numpy as np
        N_NODES = 50000
        N_EDGES = 25000
        IN_DIM = 256
        OUT_DIM = 256
        HEADS = 1
        EDGE_DIM = 128
        NEG_SLOPE = 0.01
        key = jax.random.key(seed)
        ks = jax.random.split(key, 8)
        x = jax.random.normal(ks[0], (N_NODES, IN_DIM), dtype=jnp.float32)
        edge_index = jax.random.randint(ks[1], (2, N_EDGES), 0, N_NODES, dtype=jnp.int64)
        edge_attr = jax.random.normal(ks[2], (N_EDGES, EDGE_DIM), dtype=jnp.float32)
        hc = HEADS * OUT_DIM
        Wn = jax.random.normal(ks[3], (hc, IN_DIM), dtype=jnp.float32) / np.sqrt(IN_DIM)
        bn = jnp.zeros((hc,), dtype=jnp.float32)
        We = jax.random.normal(ks[4], (hc, EDGE_DIM), dtype=jnp.float32) / np.sqrt(EDGE_DIM)
        be = jnp.zeros((hc,), dtype=jnp.float32)
        attn = jax.random.normal(ks[5], (1, HEADS, OUT_DIM), dtype=jnp.float32) * np.sqrt(2.0 / (HEADS * OUT_DIM + 1))
        return {'x': x, 'edge_index': edge_index, 'edge_attr': edge_attr, 'Wn': Wn, 'bn': bn, 'We': We, 'be': be, 'attn': attn}
    _L0_gnn_all = _L0_gnn_setup()
    _L0_gnn_in = {k: v for k, v in _L0_gnn_all.items() if k in ('Wn', 'bn', 'We', 'be', 'attn')}
    del _L0_gnn_all

    def _L0_ffn_setup():
        import jax, jax.numpy as jnp
        import numpy as np
        B, S, D, E, H, K = (4, 128, 256, 8, 512, 2)
        key = jax.random.key(seed)
        ks = jax.random.split(key, 6)
        x = jax.random.normal(ks[0], (B, S, D), jnp.float32)
        Wg = jax.random.normal(ks[1], (D, E), jnp.float32) * 0.02
        bg = jnp.zeros((E,), jnp.float32)
        W1 = jax.random.normal(ks[2], (E, D, H), jnp.float32) * 0.02
        b1 = jnp.zeros((E, H), jnp.float32)
        W2 = jax.random.normal(ks[3], (E, H, D), jnp.float32) * 0.02
        b2 = jnp.zeros((E, D), jnp.float32)
        return {'x': x, 'Wg': Wg, 'bg': bg, 'W1': W1, 'b1': b1, 'W2': W2, 'b2': b2}
    _L0_ffn_all = _L0_ffn_setup()
    _L0_ffn_in = {k: v for k, v in _L0_ffn_all.items() if k in ('Wg', 'bg', 'W1', 'b1', 'W2', 'b2')}
    del _L0_ffn_all

    def _L1_gnn_setup():
        import jax, jax.numpy as jnp
        import numpy as np
        N = 3125
        NNZ = 100000
        IN_DIM = 256
        OUT_DIM = 256
        BN_EPS = 1e-05
        key = jax.random.key(seed)
        ks = jax.random.split(key, 6)
        x = jax.random.normal(ks[0], (N, IN_DIM), dtype=jnp.float32)
        A_indices = jax.random.randint(ks[1], (2, NNZ), 0, N, dtype=jnp.int64)
        A_values = jax.random.uniform(ks[2], (NNZ,), dtype=jnp.float32)
        W = jax.random.normal(ks[3], (IN_DIM, OUT_DIM), dtype=jnp.float32) / np.sqrt(IN_DIM)
        bias = jax.random.normal(ks[4], (OUT_DIM,), dtype=jnp.float32) * 0.02
        gamma = jnp.ones((OUT_DIM,), dtype=jnp.float32)
        beta = jnp.zeros((OUT_DIM,), dtype=jnp.float32)
        return {'x': x, 'A_indices': A_indices, 'A_values': A_values, 'A_shape': N, 'W': W, 'bias': bias, 'gamma': gamma, 'beta': beta}
    _L1_gnn_all = _L1_gnn_setup()
    _L1_gnn_in = {k: v for k, v in _L1_gnn_all.items() if k in ('W', 'bias', 'gamma', 'beta')}
    del _L1_gnn_all

    def _L1_ffn_setup():
        import jax, jax.numpy as jnp
        import numpy as np
        B, N, D = (16, 128, 256)
        NUM_EXPERTS, TOP_K, HEADS = (4, 2, 4)
        N_EDGES = 32768
        LN_EPS = 1e-05

        def _layernorm(x, g, b):
            mu = x.mean(-1, keepdims=True)
            var = ((x - mu) ** 2).mean(-1, keepdims=True)
            return (x - mu) * jax.lax.rsqrt(var + LN_EPS) * g + b

        def _forward(x, edge_index, W_gat, att_src, att_dst, b_gat, ln_gamma, ln_beta, W1, b1, W2, b2):
            Bc, Nc, Dc = x.shape
            M = Bc * Nc
            x_flat = x.reshape(M, Dc)
            h = (x_flat @ W_gat).reshape(M, HEADS, NUM_EXPERTS)
            loops = jnp.arange(M, dtype=edge_index.dtype)
            src = jnp.concatenate([edge_index[0], loops])
            dst = jnp.concatenate([edge_index[1], loops])
            a_src = (h * att_src).sum(-1)
            a_dst = (h * att_dst).sum(-1)
            e = jax.nn.leaky_relu(a_src[src] + a_dst[dst], negative_slope=0.2)
            e_max = jax.ops.segment_max(e, dst, num_segments=M)
            ee = jnp.exp(e - e_max[dst])
            denom = jax.ops.segment_sum(ee, dst, num_segments=M)
            alpha = ee / (denom[dst] + 1e-16)
            msg = h[src] * alpha[:, :, None]
            agg = jax.ops.segment_sum(msg, dst, num_segments=M).reshape(M, HEADS * NUM_EXPERTS) + b_gat
            scores = _layernorm(agg, ln_gamma, ln_beta).reshape(M, HEADS, NUM_EXPERTS).mean(1)
            scores = scores.reshape(Bc, Nc, NUM_EXPERTS)
            topk_s, topk_i = jax.lax.top_k(scores, TOP_K)
            w = jax.nn.softmax(topk_s, axis=-1)
            out = jnp.zeros_like(x)
            for ei in range(NUM_EXPERTS):
                g = jnp.where(topk_i == ei, w, 0.0).sum(-1)
                hh = jax.nn.gelu(x @ W1[ei] + b1[ei], approximate=False)
                out = out + g[..., None] * (hh @ W2[ei] + b2[ei])
            return out
        key = jax.random.key(seed)
        ks = jax.random.split(key, 8)
        s = 0.05
        return {'x': jax.random.normal(ks[0], (B, N, D), jnp.float32), 'W_gat': jax.random.normal(ks[1], (D, HEADS * NUM_EXPERTS), jnp.float32) * s, 'att_src': jax.random.normal(ks[2], (HEADS, NUM_EXPERTS), jnp.float32) * s, 'att_dst': jax.random.normal(ks[3], (HEADS, NUM_EXPERTS), jnp.float32) * s, 'b_gat': jnp.zeros((HEADS * NUM_EXPERTS,), jnp.float32), 'ln_gamma': jnp.ones((HEADS * NUM_EXPERTS,), jnp.float32), 'ln_beta': jnp.zeros((HEADS * NUM_EXPERTS,), jnp.float32), 'W1': jax.random.normal(ks[4], (NUM_EXPERTS, D, 2 * D), jnp.float32) * s, 'b1': jnp.zeros((NUM_EXPERTS, 2 * D), jnp.float32), 'W2': jax.random.normal(ks[5], (NUM_EXPERTS, 2 * D, D), jnp.float32) * s, 'b2': jnp.zeros((NUM_EXPERTS, D), jnp.float32), 'edge_index': jax.random.randint(ks[6], (2, N_EDGES), 0, B * N, jnp.int32)}
    _L1_ffn_all = _L1_ffn_setup()
    _L1_ffn_in = {k: v for k, v in _L1_ffn_all.items() if k in ('W_gat', 'att_src', 'att_dst', 'b_gat', 'ln_gamma', 'ln_beta', 'W1', 'b1', 'W2', 'b2', 'edge_index')}
    del _L1_ffn_all
    return {'x': x, 'src': src, 'dst': dst, 'edge_attr_128': edge_attr_128, 'edge_weight': edge_weight, 'L0_gnn_Wn': _L0_gnn_in['Wn'], 'L0_gnn_bn': _L0_gnn_in['bn'], 'L0_gnn_We': _L0_gnn_in['We'], 'L0_gnn_be': _L0_gnn_in['be'], 'L0_gnn_attn': _L0_gnn_in['attn'], 'L0_ffn_Wg': _L0_ffn_in['Wg'], 'L0_ffn_bg': _L0_ffn_in['bg'], 'L0_ffn_W1': _L0_ffn_in['W1'], 'L0_ffn_b1': _L0_ffn_in['b1'], 'L0_ffn_W2': _L0_ffn_in['W2'], 'L0_ffn_b2': _L0_ffn_in['b2'], 'L1_gnn_W': _L1_gnn_in['W'], 'L1_gnn_bias': _L1_gnn_in['bias'], 'L1_gnn_gamma': _L1_gnn_in['gamma'], 'L1_gnn_beta': _L1_gnn_in['beta'], 'L1_ffn_W_gat': _L1_ffn_in['W_gat'], 'L1_ffn_att_src': _L1_ffn_in['att_src'], 'L1_ffn_att_dst': _L1_ffn_in['att_dst'], 'L1_ffn_b_gat': _L1_ffn_in['b_gat'], 'L1_ffn_ln_gamma': _L1_ffn_in['ln_gamma'], 'L1_ffn_ln_beta': _L1_ffn_in['ln_beta'], 'L1_ffn_W1': _L1_ffn_in['W1'], 'L1_ffn_b1': _L1_ffn_in['b1'], 'L1_ffn_W2': _L1_ffn_in['W2'], 'L1_ffn_b2': _L1_ffn_in['b2'], 'L1_ffn_edge_index': _L1_ffn_in['edge_index']}

def reference(x, src, dst, edge_attr_128, edge_weight, L0_gnn_Wn, L0_gnn_bn, L0_gnn_We, L0_gnn_be, L0_gnn_attn, L0_ffn_Wg, L0_ffn_bg, L0_ffn_W1, L0_ffn_b1, L0_ffn_W2, L0_ffn_b2, L1_gnn_W, L1_gnn_bias, L1_gnn_gamma, L1_gnn_beta, L1_ffn_W_gat, L1_ffn_att_src, L1_ffn_att_dst, L1_ffn_b_gat, L1_ffn_ln_gamma, L1_ffn_ln_beta, L1_ffn_W1, L1_ffn_b1, L1_ffn_W2, L1_ffn_b2, L1_ffn_edge_index):
    import jax
    import jax.numpy as jnp

    def _L0_gnn_ref(x, edge_index, edge_attr, Wn, bn, We, be, attn):
        import jax, jax.numpy as jnp
        import numpy as np
        N_NODES = 50000
        N_EDGES = 25000
        IN_DIM = 256
        OUT_DIM = 256
        HEADS = 1
        EDGE_DIM = 128
        NEG_SLOPE = 0.01
        N = x.shape[0]
        H, C = (attn.shape[1], attn.shape[2])
        src, dst = (edge_index[0], edge_index[1])
        h = x @ Wn.T + bn
        e = edge_attr @ We.T + be
        xj = h[src].reshape(-1, H, C)
        ee = e.reshape(-1, H, C)
        a = jax.nn.leaky_relu(jnp.sum((xj + ee) * attn, axis=-1), NEG_SLOPE)
        m = jax.ops.segment_max(a, dst, num_segments=N)
        a = jnp.exp(a - m[dst])
        denom = jax.ops.segment_sum(a, dst, num_segments=N)
        a = a / (denom[dst] + 1e-16)
        msg = (xj * a[..., None]).reshape(-1, H * C)
        out = jax.ops.segment_sum(msg, dst, num_segments=N)
        return jax.nn.relu(out)

    def _L0_ffn_ref(x, Wg, bg, W1, b1, W2, b2):
        import jax, jax.numpy as jnp
        import numpy as np
        B, S, D, E, H, K = (4, 128, 256, 8, 512, 2)
        Bv, Sv, Dv = x.shape
        gate_scores = x @ Wg + bg
        _, idx = jax.lax.top_k(gate_scores, K)
        mask = jax.nn.one_hot(idx, E, dtype=x.dtype).sum(axis=-2)
        xf = x.reshape(-1, Dv)
        mf = mask.reshape(-1, E)
        h = jax.nn.gelu(jnp.einsum('td,edh->teh', xf, W1) + b1[None], approximate=False)
        y = jnp.einsum('teh,ehd->ted', h, W2) + b2[None]
        out = jnp.einsum('ted,te->td', y, mf)
        return out.reshape(Bv, Sv, Dv)

    def _L1_gnn_ref(x, A_indices, A_values, A_shape, W, bias, gamma, beta):
        import jax, jax.numpy as jnp
        import numpy as np
        N = 3125
        NNZ = 100000
        IN_DIM = 256
        OUT_DIM = 256
        BN_EPS = 1e-05
        h = jnp.einsum('nd,df->nf', x, W)
        row, col = (A_indices[0], A_indices[1])
        gathered = A_values[:, None] * h[col]
        agg = jax.ops.segment_sum(gathered, row, num_segments=A_shape)
        h = agg + bias
        mean = jnp.mean(h, axis=0)
        var = jnp.mean(jnp.square(h - mean), axis=0)
        h = (h - mean) * jax.lax.rsqrt(var + BN_EPS) * gamma + beta
        return jax.nn.relu(h)

    def _L1_ffn_ref(x, W_gat, att_src, att_dst, b_gat, ln_gamma, ln_beta, W1, b1, W2, b2, edge_index):
        import jax, jax.numpy as jnp
        import numpy as np
        B, N, D = (16, 128, 256)
        NUM_EXPERTS, TOP_K, HEADS = (4, 2, 4)
        N_EDGES = 32768
        LN_EPS = 1e-05

        def _layernorm(x, g, b):
            mu = x.mean(-1, keepdims=True)
            var = ((x - mu) ** 2).mean(-1, keepdims=True)
            return (x - mu) * jax.lax.rsqrt(var + LN_EPS) * g + b

        def _forward(x, edge_index, W_gat, att_src, att_dst, b_gat, ln_gamma, ln_beta, W1, b1, W2, b2):
            Bc, Nc, Dc = x.shape
            M = Bc * Nc
            x_flat = x.reshape(M, Dc)
            h = (x_flat @ W_gat).reshape(M, HEADS, NUM_EXPERTS)
            loops = jnp.arange(M, dtype=edge_index.dtype)
            src = jnp.concatenate([edge_index[0], loops])
            dst = jnp.concatenate([edge_index[1], loops])
            a_src = (h * att_src).sum(-1)
            a_dst = (h * att_dst).sum(-1)
            e = jax.nn.leaky_relu(a_src[src] + a_dst[dst], negative_slope=0.2)
            e_max = jax.ops.segment_max(e, dst, num_segments=M)
            ee = jnp.exp(e - e_max[dst])
            denom = jax.ops.segment_sum(ee, dst, num_segments=M)
            alpha = ee / (denom[dst] + 1e-16)
            msg = h[src] * alpha[:, :, None]
            agg = jax.ops.segment_sum(msg, dst, num_segments=M).reshape(M, HEADS * NUM_EXPERTS) + b_gat
            scores = _layernorm(agg, ln_gamma, ln_beta).reshape(M, HEADS, NUM_EXPERTS).mean(1)
            scores = scores.reshape(Bc, Nc, NUM_EXPERTS)
            topk_s, topk_i = jax.lax.top_k(scores, TOP_K)
            w = jax.nn.softmax(topk_s, axis=-1)
            out = jnp.zeros_like(x)
            for ei in range(NUM_EXPERTS):
                g = jnp.where(topk_i == ei, w, 0.0).sum(-1)
                hh = jax.nn.gelu(x @ W1[ei] + b1[ei], approximate=False)
                out = out + g[..., None] * (hh @ W2[ei] + b2[ei])
            return out
        return _forward(x, edge_index, W_gat, att_src, att_dst, b_gat, ln_gamma, ln_beta, W1, b1, W2, b2)
    edge_index = jnp.stack([src, dst])
    x = x + _L0_gnn_ref(_layernorm(x, axis=-1), edge_index, edge_attr_128, L0_gnn_Wn, L0_gnn_bn, L0_gnn_We, L0_gnn_be, L0_gnn_attn)
    x = x + _L0_ffn_ref(_layernorm(x, axis=-1)[None], L0_ffn_Wg, L0_ffn_bg, L0_ffn_W1, L0_ffn_b1, L0_ffn_W2, L0_ffn_b2)[0]
    x = x + _L1_gnn_ref(_layernorm(x, axis=-1), edge_index, edge_weight, 3125, L1_gnn_W, L1_gnn_bias, L1_gnn_gamma, L1_gnn_beta)
    x = x + _L1_ffn_ref(_layernorm(x, axis=-1)[None], L1_ffn_W_gat, L1_ffn_att_src, L1_ffn_att_dst, L1_ffn_b_gat, L1_ffn_ln_gamma, L1_ffn_ln_beta, L1_ffn_W1, L1_ffn_b1, L1_ffn_W2, L1_ffn_b2, L1_ffn_edge_index)[0]
    return x

_drawn_inputs = setup_inputs


def setup_inputs(seed=0):
    import zlib

    import numpy as np

    out = dict(_drawn_inputs(seed))
    spreads = {'L0_gnn_bn': (0.0, 0.1),
     'L0_gnn_be': (0.0, 0.453),
     'L0_ffn_bg': (0.0, 0.1),
     'L0_ffn_b1': (0.0, 0.1),
     'L0_ffn_b2': (0.0, 0.1),
     'L1_gnn_gamma': (1.0, 0.2),
     'L1_gnn_beta': (0.0, 0.1),
     'L1_ffn_b_gat': (0.0, 0.1),
     'L1_ffn_ln_gamma': (1.0, 0.2),
     'L1_ffn_ln_beta': (0.0, 0.1),
     'L1_ffn_b1': (0.0, 0.1),
     'L1_ffn_b2': (0.0, 0.1)}
    factors = {'L1_gnn_bias': 8.0, 'L1_ffn_att_dst': 2.937}
    for name, (base, spread) in spreads.items():
        noise = np.random.default_rng([zlib.crc32(name.encode()), seed]).standard_normal(out[name].shape)
        drawn = base * np.exp(spread * noise) if base else spread * noise
        out[name] = jnp.asarray(drawn.astype(out[name].dtype))
    for name, factor in factors.items():
        out[name] = (out[name] * factor).astype(out[name].dtype)
    return out
```

```python
from contextlib import ExitStack

import concourse.bass as bass
import concourse.mybir as mybir
import numpy as np

F32, BF16, I32, U32 = mybir.dt.float32, mybir.dt.bfloat16, mybir.dt.int32, mybir.dt.uint32
ALU = mybir.AluOpType
ACT = mybir.ActivationFunctionType
AX = mybir.AxisListType

P = 128
N = 3125
NT = -(-N // P)
NP = NT * P
D = 256
KD = D // P
U = 5
SLOTS = 4
OUT = NT // U
E = 53125
NC = -(-E // P)
BL = 4
NCP = NC + BL
ED = 128
PIECE = 26
NPIECE = NC // PIECE
BIG = 1.0e30
LNEPS = 1e-5
TW = 260
H0 = 512
KH = H0 // P
NE0, NE1 = 8, 4
GE = 32768
GC = GE // P
GB = BL * P
GBLOCKS = GE // GB + NT
GS = GBLOCKS * BL
EBLOCKS = NC * P // GB + NT
ES = EBLOCKS * BL
HEADS, HC = 4, NE1
HW = HEADS * HC
GW = HW + HEADS


def emit_layernorm_project(nc, S, tag, w, n_out, keep_xT, sink, table=None, table_sb=None, before=None):
    sem, x = S.sem, S.x
    stats_ready, rstd_root = sem(tag + "_stats"), sem(tag + "_root")
    xn_ready, transposed = sem(tag + "_xn"), sem(tag + "_tp")
    xt_ready, projected, sunk, stored = sem(tag + "_xt"), sem(tag + "_pj"), sem(tag + "_sunk"), sem(tag + "_st")
    with ExitStack() as ctx:
        sb = lambda n, s, d: ctx.enter_context(nc.sbuf_tensor(tag + n, s, d))
        st = sb("st", [P, U, 6], F32)
        mv = sb("mv", [P, U, 2], F32)
        root = sb("root", [P, U], F32)
        xn = sb("xn", [P, U, D], F32)
        xT = sb("xT", [P, U, D], F32)
        tp = ctx.enter_context(nc.psum_tensor(tag + "tp", [P, SLOTS, 512], F32))
        pj = ctx.enter_context(nc.psum_tensor(tag + "pj", [P, SLOTS, 512], F32))
        block = ctx.enter_context(nc.Block())

        @block.vector
        def _(v):
            if before is not None:
                before(v)
            with v.Fori(0, OUT) as o:
                for i in range(U):
                    nc.vector.bn_stats(st[:, i, :], x[:, bass.ds(o * (U * D) + i * D, D)])
                v.drain()
                for i in range(U):
                    nc.vector.bn_aggr(mv[:, i, :], st[:, i, :])
                v.drain()
                nc.vector.tensor_scalar(root[:], mv[:, :, 1], LNEPS, None, ALU.add).then_inc(stats_ready, 1)
                v.wait_ge(rstd_root, o + 1)
                nc.vector.reciprocal(root[:], root[:])
                v.drain()
                v.wait_ge(transposed, o * U)
                for i in range(U):
                    nc.vector.tensor_scalar(xn[:, i, :], x[:, bass.ds(o * (U * D) + i * D, D)], mv[:, i, 0:1],
                                            root[:, i:i + 1], ALU.subtract, ALU.mult).then_inc(xn_ready, 1)
                for i in range(U):
                    v.wait_ge(projected, o * U + i + 1)
                    sink(v, o, i, pj[:, i % SLOTS, 0:n_out])
                    v.drain().then_inc(sunk, 1)

        @block.scalar
        def _(act):
            nc.scalar.preload_act_table(ACT.Sqrt)
            with act.Fori(0, OUT) as o:
                act.wait_ge(stats_ready, o + 1)
                nc.scalar.activation(root[:], root[:], ACT.Sqrt).then_inc(rstd_root, 1)
                act.wait_ge(projected, o * U)
                for i in range(U):
                    act.wait_ge(transposed, o * U + i + 1)
                    ins = nc.scalar.copy(xT[:, i, :], tp[:, i % SLOTS, 0:D])
                    if keep_xT:
                        ins = nc.scalar.copy(S.xnT[:, :, bass.ds(o * (U * P) + i * P, P)],
                                             tp[:, i % SLOTS, 0:D].rearrange("p (k n) -> p k n", k=KD))
                    ins.then_inc(xt_ready, 1)

        @block.tensor
        def _(pe):
            with pe.Fori(0, OUT) as o:
                pe.wait_ge(xt_ready, o * U)
                for i in range(U):
                    if i >= SLOTS:
                        pe.wait_ge(xt_ready, o * U + i - SLOTS + 1)
                    pe.wait_ge(xn_ready, o * U + i + 1)
                    for k in range(KD):
                        ins = nc.tensor.transpose(tp[:, i % SLOTS, k * P:(k + 1) * P], xn[:, i, k * P:(k + 1) * P], S.ident[:])
                    ins.then_inc(transposed, 1)
                pe.wait_ge(sunk, o * U)
                for i in range(U):
                    if i >= SLOTS:
                        pe.wait_ge(sunk, o * U + i - SLOTS + 1)
                    pe.wait_ge(xt_ready, o * U + i + 1)
                    for k in range(KD):
                        ins = nc.tensor.matmul(pj[:, i % SLOTS, 0:n_out], xT[:, i, k * P:(k + 1) * P], w[:, k, 0:n_out],
                                               start=(k == 0), stop=(k == KD - 1))
                    ins.then_inc(projected, 1)

        if table is not None:
            @block.sync
            def _(sp):
                rows = table.rearrange("(t p) d -> p t d", p=P)
                width = table.shape[1]
                with sp.Fori(0, OUT) as o:
                    sp.wait_ge(sunk, (o + 1) * U)
                    sp.dma_start(rows[:, bass.ds(o * U, U), :],
                                 table_sb[:, bass.ds(o * U, U), :]).then_inc(stored, 16)
                sp.wait_ge(stored, 16 * OUT)


def emit_setup(nc, S, A):
    sem = S.sem
    made, loaded, tables, wide, prods, dve1, cols, small = (sem("su_" + n) for n in (
        "made", "loaded", "tables", "wide", "prods", "dve1", "cols", "small"))
    laned = sem("su_laned")
    with ExitStack() as ctx:
        sb = lambda n, s, d: ctx.enter_context(nc.sbuf_tensor("su_" + n, s, d))
        wn = sb("wn", [P, KD, D], F32)
        we = sb("we", [P, KD, ED], F32)
        attn = sb("attn", [P, KD], F32)
        attn_wide = sb("attnw", [P, KD, P], F32)
        bsum = sb("bsum", [P, KD], F32)
        be = sb("be", [P, KD], F32)
        dsti = sb("dsti", [P, NCP], I32)
        tilei = sb("tilei", [P, NCP], I32)
        span = sb("span", [P, 2, NC], F32)
        spanmax = sb("spanmax", [P, 2, NC], F32)
        has = sb("has", [P, 2, NC], F32)
        key = sb("key", [P, 2, NC], F32)
        ends = sb("ends", [P, 2], F32)
        cnt = sb("cnt", [P, 2], F32)
        cnti = sb("cnti", [P, 2], I32)
        spj = sb("spj", [P, NC], I32)
        lane = sb("lane", [P, NC], BF16)
        ps = ctx.enter_context(nc.psum_tensor("su_ps", [P, 512], F32))
        block = ctx.enter_context(nc.Block())

        @block.gpsimd
        def _(pool):
            nc.gpsimd.iota(S.iota[:], [[1, NP]], base=0, channel_multiplier=0,
                           allow_small_or_imprecise_dtypes=True).then_inc(made, 1)
            nc.gpsimd.iota(S.lane[:], [[1, 1]], base=0, channel_multiplier=1,
                           allow_small_or_imprecise_dtypes=True).then_inc(made, 1)
            pool.wait_ge(tables, 2)
            nc.gpsimd.partition_all_reduce(spanmax[:].rearrange("p a c -> p (a c)"),
                                           span[:].rearrange("p a c -> p (a c)"), P, bass.bass_isa.ReduceOp.max).then_inc(wide, 1)

        @block.sync
        def _(sp):
            for dst, src in ((dsti[:], A["dst_pc"]), (S.src[:], A["src_pc"]), (spj[:], A["src_pj"]),
                             (attn[:], A["attn"].rearrange("(k p) -> p k", p=P)), (bsum[:], A["bn"].rearrange("(k p) -> p k", p=P)),
                             (be[:], A["be"].rearrange("(k p) -> p k", p=P)),
                             (wn[:], A["Wn"].rearrange("(k p) i -> p k i", p=P)), (we[:], A["We"].rearrange("(k p) i -> p k i", p=P)),
                             (S.w_aug[:, :, 0:D], A["WnT"].rearrange("(k p) o -> p k o", p=P)),
                             (S.bn_row[:], A["bn"].rearrange("(a d) -> a d", a=1).to_broadcast([P, D])),
                             (S.x[:].rearrange("p (t d) -> p t d", d=D), A["x"].rearrange("(t p) d -> p t d", p=P)),
                             (S.ew[:], A["ew_pc"])):
                with nc.allow_non_contiguous_dma(reason="a few vectors, one element to a partition"):
                    sp.dma_start(dst, src).then_inc(loaded, 16)
            sp.wait_ge(laned, 1)
            sp.dma_start(S.lane_row.rearrange("(p j) -> p j", p=P), lane[:]).then_inc(loaded, 16)
            sp.wait_ge(loaded, 16 * 13)

        @block.vector
        def _(v):
            v.wait_ge(made, 2)
            nc.vector.tensor_scalar(S.ident[:], S.iota[:, 0:P], S.lane[:, 0:1], None, ALU.is_equal)
            nc.vector.tensor_scalar(S.identb[:], S.iota[:, 0:P], S.lane[:, 0:1], None, ALU.is_equal)
            nc.vector.tensor_scalar(S.tri[:], S.iota[:, 0:P], S.lane[:, 0:1], None, ALU.is_gt)
            nc.vector.memset(S.zeros[:], 0.0)
            nc.vector.memset(S.ones[:], 1.0)
            nc.vector.memset(S.table_sb[:], 1.0)
            nc.vector.tensor_scalar(S.countdown[:], S.iota[:, 0:NE0], -1.0, float(NE0), ALU.mult, ALU.add)
            v.drain()
            v.wait_ge(loaded, 16 * 12)
            nc.vector.tensor_scalar(tilei[:], dsti[:], 7, None, ALU.logical_shift_right)
            nc.vector.tensor_copy(S.dstf[:], dsti[:])
            v.drain()
            nc.vector.tensor_copy(span[:, 0, :], tilei[:, 0:NC])
            v.drain()
            nc.vector.tensor_scalar(span[:, 1, :], span[:, 0, :], -1.0, None, ALU.mult)
            v.drain().then_inc(tables, 2)
            nc.vector.tensor_scalar(spj[:], spj[:], P - 1, None, ALU.bitwise_and)
            nc.vector.tensor_scalar(tilei[:], S.src[:], 7, None, ALU.logical_shift_right)
            v.drain()
            nc.vector.tensor_copy(lane[:], spj[:])
            nc.vector.tensor_copy(S.srct[:], tilei[:])
            v.drain().then_inc(laned, 1)
            nc.vector.tensor_tensor(S.src_tile[:], S.srct[:, 0:NC].unsqueeze(2).to_broadcast([P, NC, NT]),
                                    S.iota[:, 0:NT].unsqueeze(1).to_broadcast([P, NC, NT]), ALU.is_equal)
            nc.vector.tensor_tensor(bsum[:], bsum[:], be[:], ALU.add)
            for k in range(KD):
                nc.vector.tensor_scalar(attn_wide[:, k, :], S.ones[:, 0:P], attn[:, k:k + 1], None, ALU.mult)
            v.drain().then_inc(dve1, 1)
            v.wait_ge(prods, 1)
            nc.vector.tensor_copy(S.w_aug[:, :, D:D + 1], ps[:, 0:KD].unsqueeze(2))
            nc.vector.tensor_copy(S.we_attn[:], ps[:, 2:3])
            nc.vector.tensor_copy(S.bias_attn[:], ps[:, 3:4])
            v.wait_ge(wide, 1)
            nc.vector.tensor_scalar(has[:, 0, :], spanmax[:, 0, :], S.lane[:, 0:1], None, ALU.is_ge)
            nc.vector.tensor_scalar(has[:, 1, :], spanmax[:, 1, :], -1.0, S.lane[:, 0:1], ALU.mult, ALU.is_le)
            nc.vector.tensor_scalar(key[:, 0, :], S.iota[:, 0:NC], 1.0, None, ALU.add)
            nc.vector.tensor_scalar(key[:, 1, :], S.iota[:, 0:NC], -1.0, float(NC), ALU.mult, ALU.add)
            v.drain()
            nc.vector.tensor_tensor(has[:, 0, :], has[:, 0, :], has[:, 1, :], ALU.mult)
            v.drain()
            nc.vector.tensor_tensor(key[:], key[:], has[:, 0, :].unsqueeze(1).to_broadcast([P, 2, NC]), ALU.mult)
            v.drain()
            nc.vector.tensor_reduce(ends[:], key[:], AX.X, ALU.max)
            v.drain()
            nc.vector.tensor_scalar(cnt[:, 1:2], ends[:, 1:2], -1.0, float(NC), ALU.mult, ALU.add)
            v.drain()
            nc.vector.tensor_scalar(cnt[:, 1:2], cnt[:, 1:2], float(NC - BL), None, ALU.min)
            v.drain()
            nc.vector.tensor_tensor(cnt[:, 0:1], ends[:, 0:1], cnt[:, 1:2], ALU.subtract)
            v.drain()
            nc.vector.tensor_scalar(cnt[:, 0:1], cnt[:, 0:1], 1.0, float(BL - 1), ALU.max, ALU.add)
            v.drain()
            nc.vector.tensor_copy(cnti[:], cnt[:])
            v.drain()
            nc.vector.tensor_scalar(cnti[:, 0:1], cnti[:, 0:1], 2, None, ALU.logical_shift_right)
            v.drain()
            nc.vector.tensor_copy(cnt[:], cnti[:])
            v.drain().then_inc(cols, 1)
            v.wait_ge(small, 1)
            nc.vector.tensor_copy(S.ranges[0:1, :], ps[0:1, 8:8 + 64])
            v.drain()

        @block.tensor
        def _(pe):
            pe.wait_ge(dve1, 1)
            for i in range(KD):
                for k in range(KD):
                    nc.tensor.matmul(ps[:, i:i + 1], wn[:, k, i * P:(i + 1) * P], attn[:, k:k + 1],
                                     start=(k == 0), stop=(k == KD - 1))
            for k in range(KD):
                nc.tensor.matmul(ps[:, 2:3], we[:, k, :], attn[:, k:k + 1], start=(k == 0), stop=(k == KD - 1))
            for k in range(KD):
                ins = nc.tensor.matmul(ps[:, 3:4], attn_wide[:, k, :], bsum[:, k:k + 1],
                                       start=(k == 0), stop=(k == KD - 1))
            ins.then_inc(prods, 1)
            pe.wait_ge(cols, 1)
            nc.tensor.matmul(ps[0:1, 8:8 + 32], cnt[0:NT, 0:1], S.tri[0:NT, 0:32], start=True, stop=True)
            nc.tensor.matmul(ps[0:1, 8 + 32:8 + 64], cnt[0:NT, 1:2], S.ident[0:NT, 0:32],
                             start=True, stop=True).then_inc(small, 1)


def emit_edge_scores(nc, S, A):
    sem = S.sem
    arrived = [sem(f"es_in{i}") for i in range(2)]
    split, hot, mm, used, read = sem("es_split"), sem("es_hot"), sem("es_mm"), sem("es_used"), sem("es_read")
    HALF = PIECE // 2
    with ExitStack() as ctx:
        sb = lambda n, s, d: ctx.enter_context(nc.sbuf_tensor("es_" + n, s, d))
        ea = sb("ea", [P, 2, PIECE * P], F32)
        lane = sb("lane", [P, 2, PIECE * P], BF16)
        onehot = sb("hot", [P, 2, PIECE * P], BF16)
        parts = sb("parts", [P, 3, NT], BF16)
        rest = sb("rest", [P, 2, NT], F32)
        picked = sb("picked", [P, PIECE, NT], F32)
        ps = [ctx.enter_context(nc.psum_tensor(f"es_ps{i}", [P, 3, 512], F32)) for i in range(2)]
        block = ctx.enter_context(nc.Block())
        lane_row = S.lane_row.rearrange("(a n) -> a n", a=1)

        @block.sync
        def _(sp):
            with sp.Fori(0, NPIECE // 2) as o:
                for i in range(2):
                    sp.wait_ge(read, 2 * o + i + 1)
                    col = o * (2 * PIECE * P) + i * PIECE * P
                    sp.dma_start(ea[:, i, :], A["eaT"][:, bass.ds(col, PIECE * P)]).then_inc(arrived[i], 16)
                    sp.dma_start(lane[:, i, :], lane_row[:, bass.ds(col, PIECE * P)].to_broadcast([P, PIECE * P])
                                 ).then_inc(arrived[i], 16)

        @block.vector
        def _(v):
            nc.vector.tensor_copy(parts[:, 0, :], S.hs[:])
            v.drain()
            nc.vector.tensor_tensor(rest[:, 0, :], S.hs[:], parts[:, 0, :], ALU.subtract)
            v.drain()
            nc.vector.tensor_copy(parts[:, 1, :], rest[:, 0, :])
            v.drain()
            nc.vector.tensor_tensor(rest[:, 1, :], rest[:, 0, :], parts[:, 1, :], ALU.subtract)
            v.drain()
            nc.vector.tensor_copy(parts[:, 2, :], rest[:, 1, :])
            v.drain().then_inc(split, 1)
            v.sem_inc(read, 2)
            with v.Fori(0, NPIECE // 2) as o:
                for i in range(2):
                    v.wait_ge(arrived[i], 32 * o + 32)
                    nc.vector.tensor_scalar(onehot[:, i, :], lane[:, i, :], S.lane[:, 0:1], None, ALU.is_equal
                                            ).then_inc(hot, 1)
                    v.wait_ge(mm, 2 * o + i + 1)
                    c = o * (2 * PIECE) + i * PIECE
                    nc.vector.tensor_tensor(
                        picked[:].rearrange("p (a c) t -> p a (c t)", a=2), ps[i][:, 0:2, 0:HALF * NT],
                        S.src_tile[:, bass.ds(c, PIECE), :].rearrange("p (a c) t -> p a (c t)", a=2), ALU.mult)
                    v.drain()
                    nc.vector.tensor_reduce(S.score[:, bass.ds(c, PIECE)], picked[:], AX.X, ALU.add)
                    v.drain()
                    nc.vector.tensor_tensor(S.score[:, bass.ds(c, PIECE)], S.score[:, bass.ds(c, PIECE)],
                                            ps[i][:, 2, 0:PIECE], ALU.add)
                    v.drain().then_inc(read, 1)
            nc.vector.memset(S.score[:, NC:NCP], 0.0)
            nc.vector.tensor_scalar(S.score[:, 0:NC], S.score[:, 0:NC], S.bias_attn[:, 0:1], None, ALU.add)
            v.drain()
            nc.vector.tensor_scalar(picked[:, 0:17, :].rearrange("p c t -> p (c t)")[:, 0:NC], S.score[:, 0:NC], 0.01, None, ALU.mult)
            v.drain()
            nc.vector.tensor_tensor(S.score[:, 0:NC], S.score[:, 0:NC],
                                    picked[:, 0:17, :].rearrange("p c t -> p (c t)")[:, 0:NC], ALU.max)
            v.drain()

        @block.tensor
        def _(pe):
            pe.wait_ge(split, 1)
            with pe.Fori(0, NPIECE // 2) as o:
                for i in range(2):
                    pe.wait_ge(read, 2 * o + i + 1)
                    pe.wait_ge(arrived[i], 32 * o + 32)
                    for c in range(PIECE):
                        nc.tensor.matmul(ps[i][:, 2, c:c + 1], ea[:, i, c * P:(c + 1) * P], S.we_attn[:, 0:1],
                                         start=True, stop=True)
                    pe.wait_ge(hot, 2 * o + i + 1)
                    for c in range(PIECE):
                        for k in range(3):
                            ins = nc.tensor.matmul(ps[i][:, c // HALF, (c % HALF) * NT:(c % HALF + 1) * NT],
                                                   onehot[:, i, c * P:(c + 1) * P], parts[:, k, :],
                                                   start=(k == 0), stop=(k == 2))
                    ins.then_inc(mm, 1)


def tile_range(eng, S, t):
    g0 = eng.value_load(S.ranges[0:1, bass.ds(t, 1)], min_val=0, max_val=NT * NC // BL)
    g1 = eng.value_load(S.ranges[0:1, bass.ds(t + 1, 1)], min_val=0, max_val=NT * NC // BL)
    c0 = eng.value_load(S.ranges[0:1, bass.ds(t + 32, 1)], min_val=0, max_val=NC - BL)
    return g0, g1, c0


def chunk_of(nc, eng, g, g0, c0):
    return eng.snap(nc.s_assert_within(c0 + (g - g0) * BL, 0, NC, skip_runtime_bounds_check_because=
                                       "a tile's blocks end within a block of its last chunk"))


def sorted_range(eng, ranges, t, most):
    g0 = eng.value_load(ranges[0:1, bass.ds(t, 1)], min_val=0, max_val=most)
    g1 = eng.value_load(ranges[0:1, bass.ds(t + 1, 1)], min_val=0, max_val=most)
    return g0, g1


def slot_of(nc, eng, g, blocks):
    return eng.snap(nc.s_assert_within(g * BL, 0, (blocks - 1) * BL, skip_runtime_bounds_check_because=
                                       "whole blocks of all tiles are at most so many"))


def emit_aggregate(nc, S, tag, table, softmax):
    sem = S.sem
    gathered = [sem(f"{tag}_g{i}") for i in range(BL)]
    indexed, agg_done, masked, weighed = sem(tag + "_idx"), sem(tag + "_agg"), sem(tag + "_msk"), sem(tag + "_w")
    best, best_t, negs, negs_w, closed, evac = (sem(f"{tag}_{n}") for n in ("best", "bestT", "negs", "negsW", "closed", "evac"))
    relud, recip = sem(tag + "_relu"), sem(tag + "_rcp")
    width = D + 1 if softmax else D
    with ExitStack() as ctx:
        sb = lambda n, s, d: ctx.enter_context(nc.sbuf_tensor(tag + n, s, d))
        idx = sb("idx", [P, BL], I32)
        rows = sb("rows", [P, BL, TW], F32)
        w = sb("w", [P, BL, P], F32)
        nb = sb("nb", [P, BL, P], F32)
        top = sb("top", [P, BL, P], F32)
        top1 = sb("top1", [P, P], F32)
        m = sb("m", [P, 1], F32)
        diag = sb("diag", [P, P], F32)
        negm = sb("negm", [P, P], F32)
        rden = sb("rden", [P, 1], F32)
        relu = sb("relu", [P, D], F32)
        ps = ctx.enter_context(nc.psum_tensor(tag + "ps", [P, 512], F32))
        psT = ctx.enter_context(nc.psum_tensor(tag + "psT", [P, P], F32))
        psM = ctx.enter_context(nc.psum_tensor(tag + "psM", [P, P], F32))
        block = ctx.enter_context(nc.Block())

        source = S.src if softmax else S.esource

        def blocks_of(eng, t):
            if softmax:
                g0, g1, c0 = tile_range(eng, S, t)
                return g0, g1, lambda g: chunk_of(nc, eng, g, g0, c0)
            g0, g1 = sorted_range(eng, S.eranges, t, EBLOCKS)
            return g0, g1, lambda g: slot_of(nc, eng, g, EBLOCKS)

        def mask(v, t, c, i):
            nc.vector.tensor_scalar(nb[:, i, :], S.iota[:, bass.ds(t * P, P)], S.dstf[:, bass.ds(c + i, 1)], -BIG,
                                    ALU.not_equal, ALU.mult)

        @block.gpsimd
        def _(pool):
            with pool.Fori(0, NT) as t:
                g0, g1, chunk = blocks_of(pool, t)
                with pool.Fori(g0, g1) as g:
                    c = chunk(g)
                    for i in range(BL):
                        pool.wait_ge(agg_done, g * BL + i + 1)
                        nc.gpsimd.tensor_copy(idx[:, i:i + 1], source[:, bass.ds(c + i, 1)]).then_inc(indexed, 1)
                        count = pool.snap(g * BL + i + 1)
                        pool.wait_ge(indexed, 1)
                        pool.wait_ge(indexed, count)
                        pool.indirect_dma_start(rows[:, i, 0:TW], None, table,
                                                bass.IndirectOffsetOnAxis(ap=idx[:, i:i + 1], axis=0)
                                                ).then_inc(gathered[i], 16)

        @block.tensor
        def _(pe):
            pe.sem_inc(agg_done, BL)
            with pe.Fori(0, NT) as t:
                g0, g1, _ = blocks_of(pe, t)
                if softmax:
                    pe.wait_ge(best, t + 1)
                    nc.tensor.transpose(psT[:], top1[:], S.ident[:]).then_inc(best_t, 1)
                    pe.wait_ge(negs, t + 1)
                    nc.tensor.matmul(psM[:], S.ones[:, 0:P], diag[:], start=True, stop=True).then_inc(negs_w, 1)
                pe.wait_ge(evac, t)
                nc.tensor.matmul(ps[:, 0:width], S.zeros[0:1, 0:P], S.iota[0:1, 0:width], start=True, stop=False)
                with pe.Fori(g0, g1) as g:
                    for i in range(BL):
                        pe.wait_ge(gathered[i], g * 16 + 16)
                        if i == 0 or not softmax:
                            pe.wait_ge(weighed, g + 1 if softmax else g * BL + i + 1)
                        nc.tensor.matmul(ps[:, 0:width], w[:, i, :], rows[:, i, 0:width],
                                         start=False, stop=False).then_inc(agg_done, 1)
                nc.tensor.matmul(ps[:, 0:width], S.zeros[0:1, 0:P], S.iota[0:1, 0:width],
                                 start=False, stop=True).then_inc(closed, 1)

        if not softmax:
            @block.vector
            def _(v):
                with v.Fori(0, NT) as t:
                    g0, g1, chunk = blocks_of(v, t)
                    with v.Fori(g0, g1) as g:
                        c = chunk(g)
                        for i in range(BL):
                            v.wait_ge(agg_done, g * BL + i + 1)
                            nc.vector.tensor_scalar(w[:, i, :], S.iota[:, 0:P], S.elane[:, bass.ds(c + i, 1)],
                                                    S.eweight[:, bass.ds(c + i, 1)], ALU.is_equal, ALU.mult).then_inc(weighed, 1)
                    v.wait_ge(closed, t + 1)
                    nc.vector.tensor_tensor(S.agg[:, bass.ds(t * D, D)], ps[:, 0:D], S.bias_row[:], ALU.add).then_inc(evac, 1)
            return

        @block.vector
        def _(v):
            with v.Fori(0, NT) as t:
                g0, g1, c0 = tile_range(v, S, t)
                nc.vector.memset(top[:], -BIG)
                v.drain()
                with v.Fori(g0, g1) as g:
                    c = chunk_of(nc, v, g, g0, c0)
                    for i in range(BL):
                        mask(v, t, c, i)
                    v.drain()
                    for i in range(BL):
                        nc.vector.scalar_tensor_tensor(top[:, i, :], nb[:, i, :], S.score[:, bass.ds(c + i, 1)], top[:, i, :],
                                                       ALU.add, ALU.max)
                    v.drain()
                nc.vector.tensor_reduce(top1[:], top[:].rearrange("p i n -> p n i"), AX.X, ALU.max).then_inc(best, 1)
                v.wait_ge(best_t, t + 1)
                nc.vector.tensor_reduce(m[:], psT[:], AX.X, ALU.max)
                v.drain()
                nc.vector.tensor_scalar(m[:], m[:], -0.1 * BIG, -1.0, ALU.max, ALU.mult)
                v.drain()
                nc.vector.tensor_scalar(diag[:], S.ident[:], m[:, 0:1], None, ALU.mult).then_inc(negs, 1)
                v.wait_ge(negs_w, t + 1)
                nc.vector.tensor_copy(negm[:], psM[:])
                v.drain()
                with v.Fori(g0, g1) as g:
                    c = chunk_of(nc, v, g, g0, c0)
                    v.wait_ge(weighed, g)
                    for i in range(BL):
                        mask(v, t, c, i)
                    v.drain()
                    nc.vector.tensor_tensor(nb[:], nb[:], negm[:].unsqueeze(1).to_broadcast([P, BL, P]), ALU.add
                                            ).then_inc(masked, 1)
                v.wait_ge(closed, t + 1)
                nc.vector.tensor_scalar(rden[:], ps[:, D:D + 1], 1e-16, None, ALU.add)
                v.drain()
                nc.vector.reciprocal(rden[:], rden[:]).then_inc(recip, 1)
                v.wait_ge(relud, t + 1)
                nc.vector.tensor_tensor(S.x[:, bass.ds(t * D, D)], S.x[:, bass.ds(t * D, D)], relu[:], ALU.add).then_inc(evac, 1)

        @block.scalar
        def _(act):
            nc.scalar.preload_act_table(ACT.Exp)
            with act.Fori(0, NT) as t:
                g0, g1, c0 = tile_range(act, S, t)
                with act.Fori(g0, g1) as g:
                    c = chunk_of(nc, act, g, g0, c0)
                    act.wait_ge(masked, g + 1)
                    act.wait_ge(agg_done, g * BL + BL)
                    for i in range(BL):
                        ins = nc.scalar.activation(w[:, i, :], nb[:, i, :], ACT.Exp, bias=S.score[:, bass.ds(c + i, 1)])
                    ins.then_inc(weighed, 1)
                act.wait_ge(recip, t + 1)
                act.wait_ge(evac, t)
                nc.scalar.activation(relu[:], ps[:, 0:D], ACT.Relu, scale=rden[:, 0:1]).then_inc(relud, 1)


def emit_experts(nc, S, tag, A, n_experts, gate):
    sem = S.sem
    STEPS, HALF = 2 * OUT, U * P // 2
    arrived = [sem(f"{tag}_w{i}") for i in range(2)]
    up_done, hid_ready, down_done, added, b2_in = (sem(f"{tag}_{n}") for n in ("up", "hid", "down", "add", "b2"))
    W1, b1, W2, b2 = A[tag + "_W1"], A[tag + "_b1"], A[tag + "_W2"], A[tag + "_b2"]
    with ExitStack() as ctx:
        sb = lambda n, s, d: ctx.enter_context(nc.sbuf_tensor(tag + n, s, d))
        w1 = [sb(f"w1_{i}", [P, KD, H0], F32) for i in range(2)]
        w2 = [sb(f"w2_{i}", [P, KH, D], F32) for i in range(2)]
        bias1 = [sb(f"b1_{i}", [P, KH], F32) for i in range(2)]
        hid = [sb(f"hid{i}", [P, KH, 2, HALF], F32) for i in range(2)]
        b2_rows = sb("b2", [P, n_experts, D], F32)
        up = [ctx.enter_context(nc.psum_tensor(f"{tag}up{i}", [P, 2, 512], F32)) for i in range(2)]
        down = [ctx.enter_context(nc.psum_tensor(f"{tag}dn{i}", [P, 512], F32)) for i in range(4)]
        block = ctx.enter_context(nc.Block())

        @block.sync
        def _(sp):
            def load(e, i):
                sp.dma_start(w1[i][:], W1[bass.ds(e, 1), :, :].rearrange("a (k p) h -> p (a k) h", p=P)).then_inc(arrived[i], 16)
                sp.dma_start(w2[i][:], W2[bass.ds(e, 1), :, :].rearrange("a (k p) d -> p (a k) d", p=P)).then_inc(arrived[i], 16)
                with nc.allow_non_contiguous_dma(reason="biases, one element to a partition"):
                    sp.dma_start(bias1[i][:], b1[bass.ds(e, 1), :].rearrange("a (k p) -> p (a k)", p=P)).then_inc(arrived[i], 16)

            load(0, 0)
            sp.dma_start(b2_rows[:], b2.unsqueeze(0).to_broadcast([P, n_experts, D])).then_inc(b2_in, 16)
            load(1, 1)
            with sp.Fori(0, n_experts // 2 - 1) as o:
                for i in range(2):
                    sp.wait_ge(down_done, o * (STEPS * U) + (i + 1) * (OUT * U))
                    load(o * 2 + 2 + i, i)

        @block.tensor
        def _(pe):
            with pe.Fori(0, n_experts // 2) as o:
                def down_step(s):
                    pe.wait_ge(hid_ready, o * (STEPS * KH) + (s + 1) * KH)
                    for j in range(U):
                        r = s * U + j
                        pe.wait_ge(added, o * (STEPS * U) + max(r - 3, 0))
                        for k in range(KH):
                            ins = nc.tensor.matmul(down[r % 4][:, 0:D],
                                                   hid[s % 2][:, k, :, :].rearrange("p a n -> p (a n)")[:, j * P:(j + 1) * P],
                                                   w2[s // OUT][:, k, :], start=(k == 0), stop=(k == KH - 1))
                        ins.then_inc(down_done, 1)

                for s in range(STEPS):
                    e, grp = s // OUT, s % OUT
                    if grp == 0:
                        pe.wait_ge(arrived[e], o * 48 + 48)
                    for m in range(KH):
                        q = s * KH + m
                        pe.wait_ge(hid_ready, o * (STEPS * KH) + max(q - 1, 0))
                        for k in range(KD):
                            for a in range(2):
                                col = grp * U * P + a * HALF
                                ins = nc.tensor.matmul(up[q % 2][:, a, 0:HALF], w1[e][:, k, m * P:(m + 1) * P],
                                                       S.xnT[:, k, col:col + HALF], start=(k == 0), stop=(k == KD - 1))
                        ins.then_inc(up_done, 1)
                    if s >= 1:
                        down_step(s - 1)
                down_step(STEPS - 1)

        @block.scalar
        def _(act):
            nc.scalar.preload_act_table(ACT.Gelu)
            with act.Fori(0, n_experts // 2) as o:
                for s in range(STEPS):
                    act.wait_ge(down_done, o * (STEPS * U) + max(s - 1, 0) * U)
                    for m in range(KH):
                        act.wait_ge(up_done, o * (STEPS * KH) + s * KH + m + 1)
                        nc.scalar.activation(hid[s % 2][:, m, :, :], up[m % 2][:, :, 0:HALF], ACT.Gelu,
                                             bias=bias1[s // OUT][:, m:m + 1]).then_inc(hid_ready, 1)

        @block.vector
        def _(v):
            v.wait_ge(b2_in, 16)
            with v.Fori(0, n_experts) as e:
                for t in range(NT):
                    nc.vector.scalar_tensor_tensor(S.x[:, t * D:(t + 1) * D], b2_rows[:, bass.ds(e, 1), :].rearrange("p a d -> p (a d)"),
                                                   gate[:, t, bass.ds(e, 1)], S.x[:, t * D:(t + 1) * D], ALU.mult, ALU.add)
                v.drain()
            with v.Fori(0, n_experts // 2) as o:
                for s in range(STEPS):
                    for j in range(U):
                        r, t = s * U + j, (s % OUT) * U + j
                        v.wait_ge(down_done, o * (STEPS * U) + r + 1)
                        nc.vector.scalar_tensor_tensor(S.x[:, t * D:(t + 1) * D], down[r % 4][:, 0:D],
                                                       gate[:, t, bass.ds(o * 2 + s // OUT, 1)], S.x[:, t * D:(t + 1) * D],
                                                       ALU.mult, ALU.add).then_inc(added, 1)
                    if s % OUT == OUT - 1:
                        v.drain()


def choose_two(nc, v, S, score, n, first, second, tmp, top):
    for r, pick in enumerate((first, second)):
        nc.vector.tensor_reduce(top[:, :, r], score[:], AX.X, ALU.max)
        v.drain()
        nc.vector.tensor_tensor(pick[:], score[:], top[:, :, r:r + 1].to_broadcast([P, NT, n]), ALU.is_equal)
        v.drain()
        nc.vector.tensor_tensor(pick[:], pick[:], S.countdown[:, 0:n].unsqueeze(1).to_broadcast([P, NT, n]), ALU.mult)
        v.drain()
        nc.vector.tensor_reduce(tmp[:], pick[:], AX.X, ALU.max)
        v.drain()
        nc.vector.tensor_tensor(pick[:], pick[:], tmp[:].unsqueeze(2).to_broadcast([P, NT, n]), ALU.is_equal)
        v.drain()
        if r == 0:
            nc.vector.scalar_tensor_tensor(score[:], pick[:], -BIG, score[:], ALU.mult, ALU.add)
            v.drain()


def emit_top2_mask(nc, S):
    with ExitStack() as ctx:
        sb = lambda n, s, d: ctx.enter_context(nc.sbuf_tensor("t2" + n, s, d))
        first, second = sb("a", [P, NT, NE0], F32), sb("b", [P, NT, NE0], F32)
        tmp, top = sb("c", [P, NT], F32), sb("d", [P, NT, 2], F32)
        block = ctx.enter_context(nc.Block())

        @block.vector
        def _(v):
            choose_two(nc, v, S, S.gate0, NE0, first, second, tmp, top)
            nc.vector.tensor_tensor(S.gate0[:], first[:], second[:], ALU.add)
            v.drain()


def emit_batchnorm(nc, S, A):
    sem = S.sem
    loaded, summed, centred, squared, sq_summed, var_in, rooted = (sem("bn_" + n) for n in (
        "in", "sum", "cen", "sq", "sqsum", "var", "root"))
    LAST = N - (NT - 1) * P
    with ExitStack() as ctx:
        sb = lambda n, s, d: ctx.enter_context(nc.sbuf_tensor("bn" + n, s, d))
        gamma, beta, mean, root = (sb(n, [P, D], F32) for n in ("gamma", "beta", "mean", "root"))
        sq = sb("sq", [P, NT * D], F32)
        ps = [ctx.enter_context(nc.psum_tensor(f"bnps{i}", [P, 512], F32)) for i in range(2)]
        block = ctx.enter_context(nc.Block())

        @block.sync
        def _(sp):
            sp.dma_start(gamma[:], A["bn_gamma"].unsqueeze(0).to_broadcast([P, D])).then_inc(loaded, 16)
            sp.dma_start(beta[:], A["bn_beta"].unsqueeze(0).to_broadcast([P, D])).then_inc(loaded, 16)

        @block.tensor
        def _(pe):
            def sum_over_nodes(ps, a):
                for t in range(NT):
                    k = P if t < NT - 1 else LAST
                    ins = nc.tensor.matmul(ps[:, 0:D], S.ones[0:k, 0:P], a[0:k, t * D:(t + 1) * D],
                                           start=(t == 0), stop=(t == NT - 1))
                return ins

            sum_over_nodes(ps[0], S.agg).then_inc(summed, 1)
            pe.wait_ge(squared, 1)
            sum_over_nodes(ps[1], sq).then_inc(sq_summed, 1)

        @block.scalar
        def _(act):
            nc.scalar.preload_act_table(ACT.Sqrt)
            act.wait_ge(centred, 1)
            nc.scalar.activation(sq[:], S.agg[:], ACT.Square).then_inc(squared, 1)
            act.wait_ge(var_in, 1)
            nc.scalar.activation(root[:], root[:], ACT.Sqrt).then_inc(rooted, 1)

        @block.vector
        def _(v):
            agg3 = S.agg[:].rearrange("p (t d) -> p t d", d=D)
            x3 = S.x[:].rearrange("p (t d) -> p t d", d=D)
            bc = lambda row: row[:].unsqueeze(1).to_broadcast([P, NT, D])
            v.wait_ge(summed, 1)
            nc.vector.tensor_scalar(mean[:], ps[0][:, 0:D], 1.0 / N, None, ALU.mult)
            v.drain()
            nc.vector.tensor_tensor(agg3, agg3, bc(mean), ALU.subtract).then_inc(centred, 1)
            v.wait_ge(sq_summed, 1)
            nc.vector.tensor_scalar(root[:], ps[1][:, 0:D], 1.0 / N, LNEPS, ALU.mult, ALU.add).then_inc(var_in, 1)
            v.wait_ge(rooted, 1)
            nc.vector.reciprocal(root[:], root[:])
            v.drain()
            v.wait_ge(loaded, 32)
            nc.vector.tensor_tensor(root[:], root[:], gamma[:], ALU.mult)
            v.drain()
            nc.vector.tensor_tensor(agg3, agg3, bc(root), ALU.mult)
            v.drain()
            nc.vector.tensor_tensor(agg3, agg3, bc(beta), ALU.add)
            v.drain()
            nc.vector.scalar_tensor_tensor(S.x[:], S.agg[:], 0.0, S.x[:], ALU.max, ALU.add)
            v.drain()


def emit_sort_edges(nc, S, tag, n_chunks, take, give, weight, slots, rec_dram, rec_sb, ranges):
    sem = lambda n: S.sem(tag + n)
    R = 3 if weight is not None else 2
    GC, GS = n_chunks, slots
    loaded, filled, hots, ranked, tile_read, packed, copied, back = (sem("_" + n) for n in (
        "in", "fill", "hot", "rank", "read", "pack", "copy", "back"))
    put = [sem(f"_put{i}") for i in range(8)]
    with ExitStack() as ctx:
        sb = lambda n, s, d: ctx.enter_context(nc.sbuf_tensor(tag + "_" + n, s, d))
        srci, dsti, tilei = (sb(n, [P, GC], I32) for n in ("src", "dst", "tile"))
        tilef, pos, incl, part, zero = (sb(n, [P, GC], F32) for n in ("tilef", "pos", "incl", "part", "zero"))
        hot = sb("hot", [P, NT, GC], BF16)
        trib, onesb = sb("trib", [P, P], BF16), sb("onesb", [P, P], BF16)
        blocks = sb("blocks", [P, 1], F32)
        base = sb("base", [P, 1], F32)
        cnt = sb("cnt", [P, 1], F32)
        cnti = sb("cnti", [P, 1], I32)
        row = sb("row", [P, NT + 1], F32)
        rec = sb("rec", [P, GC + 1, R + 1], I32)
        slot = sb("slot", [P, 8, R + 1], I32)
        empty = sb("empty", [P, GS, R], I32)
        psr = ctx.enter_context(nc.psum_tensor(tag + "_psr", [P, 512], F32))
        pst = ctx.enter_context(nc.psum_tensor(tag + "_pst", [P, 512], F32))
        block = ctx.enter_context(nc.Block())

        @block.sync
        def _(sp):
            sp.dma_start(srci[:], take).then_inc(loaded, 16)
            sp.dma_start(dsti[:], give).then_inc(loaded, 16)
            sp.wait_ge(filled, 1)
            sp.dma_start(rec_dram.rearrange("(p c) r -> p c r", p=P), empty[:]).then_inc(back, 16)
            sp.wait_ge(back, 16)
            for i in range(8):
                sp.wait_ge(put[i], 16 * (GC // 8))
            sp.dma_start(rec_sb[:], rec_dram.rearrange("(p c) r -> p c r", p=P)).then_inc(back, 16)
            sp.wait_ge(back, 32)

        @block.gpsimd
        def _(pool):
            nc.gpsimd.memset(empty[:, :, 0:1], 0)
            if R == 3:
                nc.gpsimd.memset(empty[:, :, 2:3], 0)
            nc.gpsimd.memset(empty[:, :, 1:2], 2 * P).then_inc(filled, 1)
            pool.wait_ge(packed, 1)
            pool.wait_ge(back, 16)
            with pool.Fori(0, GC // 8) as o:
                for i in range(8):
                    pool.wait_ge(put[i], 16 * o)
                    count = pool.snap(o * 8 + (i + 1), min_val=1, max_val=GC)
                    nc.gpsimd.tensor_copy(slot[:, i:i + 1, :], rec[:, bass.ds(count, 1), :]).then_inc(copied, 1)
                    count = pool.snap(o * 8 + i + 1)
                    pool.wait_ge(copied, 1)
                    pool.wait_ge(copied, count)
                    pool.indirect_dma_start(rec_dram, bass.IndirectOffsetOnAxis(ap=slot[:, i, 0:1], axis=0),
                                            slot[:, i, 1:R + 1], None).then_inc(put[i], 16)

        @block.tensor
        def _(pe):
            pe.wait_ge(hots, 1)
            with pe.Fori(0, NT) as t:
                pe.wait_ge(tile_read, t)
                nc.tensor.matmul(psr[:, 0:GC], trib[:], hot[:, bass.ds(t, 1), :].rearrange("p a c -> p (a c)"), start=True, stop=True)
                nc.tensor.matmul(pst[:, 0:GC], onesb[:], hot[:, bass.ds(t, 1), :].rearrange("p a c -> p (a c)"),
                                 start=True, stop=True).then_inc(ranked, 1)

        @block.vector
        def _(v):
            nc.vector.tensor_copy(trib[:], S.tri[:])
            nc.vector.tensor_copy(onesb[:], S.ones[:, 0:P])
            nc.vector.memset(zero[:], 0.0)
            nc.vector.memset(pos[:], 0.0)
            nc.vector.memset(blocks[:], 0.0)
            nc.vector.memset(row[:], 0.0)
            v.wait_ge(loaded, 32)
            nc.vector.tensor_scalar(tilei[:], dsti[:], 7, None, ALU.logical_shift_right)
            nc.vector.tensor_scalar(dsti[:], dsti[:], P - 1, None, ALU.bitwise_and)
            nc.vector.tensor_copy(rec[:, 1:GC + 1, 1], srci[:])
            if weight is not None:
                nc.vector.tensor_copy(rec[:, 1:GC + 1, 3].bitcast(F32), weight)
            v.drain()
            nc.vector.tensor_copy(tilef[:], tilei[:])
            nc.vector.tensor_copy(rec[:, 1:GC + 1, 2], dsti[:])
            v.drain()
            nc.vector.tensor_tensor(hot[:], tilef[:].unsqueeze(1).to_broadcast([P, NT, GC]),
                                    S.iota[:, 0:NT].unsqueeze(2).to_broadcast([P, NT, GC]), ALU.is_equal)
            v.drain().then_inc(hots, 1)
            with v.Fori(0, NT) as t:
                nc.vector.tensor_scalar(base[:], blocks[:], float(GB), None, ALU.mult)
                v.wait_ge(ranked, t + 1)
                nc.vector.tensor_tensor_scan(incl[:], pst[:, 0:GC], zero[:], 0.0, ALU.add, ALU.add)
                v.drain()
                nc.vector.tensor_tensor(part[:], incl[:], pst[:, 0:GC], ALU.subtract)
                nc.vector.tensor_scalar(cnt[:], incl[:, GC - 1:GC], float(GB - 1), None, ALU.add)
                v.drain()
                nc.vector.tensor_tensor(part[:], part[:], psr[:, 0:GC], ALU.add)
                nc.vector.tensor_copy(cnti[:], cnt[:])
                v.drain().then_inc(tile_read, 1)
                nc.vector.scalar_tensor_tensor(part[:], part[:], base[:, 0:1], hot[:, bass.ds(t, 1), :].rearrange("p a c -> p (a c)"),
                                               ALU.add, ALU.mult)
                nc.vector.tensor_scalar(cnti[:], cnti[:], 9, None, ALU.logical_shift_right)
                v.drain()
                nc.vector.tensor_tensor(pos[:], pos[:], part[:], ALU.add)
                nc.vector.tensor_copy(cnt[:], cnti[:])
                v.drain()
                nc.vector.tensor_scalar(cnt[:], cnt[:], 1.0, None, ALU.max)
                v.drain()
                nc.vector.tensor_tensor(blocks[:], blocks[:], cnt[:], ALU.add)
                v.drain()
                nc.vector.tensor_copy(row[:, bass.ds(t + 1, 1)], blocks[:])
            v.drain()
            nc.vector.tensor_copy(ranges[:], row[:])
            nc.vector.tensor_copy(tilei[:], pos[:])
            v.drain()
            nc.vector.tensor_scalar(dsti[:], tilei[:], P - 1, None, ALU.bitwise_and)
            nc.vector.tensor_scalar(srci[:], tilei[:], 7, None, ALU.logical_shift_right)
            v.drain()
            nc.vector.tensor_copy(part[:], dsti[:])
            nc.vector.tensor_copy(pos[:], srci[:])
            v.drain()
            nc.vector.scalar_tensor_tensor(part[:], part[:], float(GS), pos[:], ALU.mult, ALU.add)
            v.drain()
            nc.vector.tensor_copy(rec[:, 1:GC + 1, 0], part[:])
            v.drain().then_inc(packed, 1)


def emit_routing(nc, S, A):
    sem = S.sem
    gathered = [sem(f"gt_g{i}") for i in range(BL)]
    indexed, kept, lanes, best, best_t, evac, vals = (sem("gt_" + n) for n in ("idx", "kept", "lanes", "best", "bestT", "evac", "vals"))
    hot, hot_t, hot_tc, ends, logit, expd, weighed, added, closed, closed_read, selfz, selfe = (sem("gt_" + n) for n in (
        "hot", "hotT", "hotTc", "ends", "logit", "exp", "w", "agg", "closed", "clr", "selfz", "selfe"))
    loaded, var_in, rooted, dz, de = (sem("gt_" + n) for n in ("in", "var", "root", "dz", "de"))
    with ExitStack() as ctx:
        sb = lambda n, s, d: ctx.enter_context(nc.sbuf_tensor("gt_" + n, s, d))
        idx = sb("idx", [P, BL], I32)
        land = sb("land", [P, BL, GW], F32)
        rows = sb("rows", [P, GS, GW], F32)
        lane = sb("lane", [P, GS], F32)
        nb = sb("nb", [P, BL, P], F32)
        top = sb("top", [P, HEADS, P], F32)
        ms = sb("ms", [P, NT, HEADS], F32)
        val = sb("val", [P, NT, 2 * HEADS], F32)
        onehot = sb("hot", [P, BL, P], F32)
        onehot_t = sb("hotT", [P, BL, P], F32)
        z = sb("z", [P, BL, HEADS], F32)
        z2 = sb("z2", [P, BL, HEADS], F32)
        w = sb("w", [P, BL, GW], F32)
        sums = sb("sums", [P, NT, GW], F32)
        zs = sb("zs", [P, NT, HEADS], F32)
        tmp = sb("tmp", [P, NT, HW], F32)
        mean, var = sb("mean", [P, NT], F32), sb("var", [P, NT], F32)
        b_gat, gamma, beta = (sb(n, [P, HW], F32) for n in ("bgat", "gamma", "beta"))
        first, second = sb("first", [P, NT, NE1], F32), sb("second", [P, NT, NE1], F32)
        topv = sb("topv", [P, NT, 2], F32)
        psT = ctx.enter_context(nc.psum_tensor("gt_psT", [P, BL, P], F32))
        psE = ctx.enter_context(nc.psum_tensor("gt_psE", [P, 512], F32))
        psO = ctx.enter_context(nc.psum_tensor("gt_psO", [P, 512], F32))
        block = ctx.enter_context(nc.Block())
        own = S.gat_sb

        @block.sync
        def _(sp):
            for dst, name in ((b_gat, "b_gat"), (gamma, "ln_gamma"), (beta, "ln_beta")):
                sp.dma_start(dst[:], A[name].unsqueeze(0).to_broadcast([P, HW])).then_inc(loaded, 16)

        @block.gpsimd
        def _(pool):
            total = pool.value_load(S.granges[0:1, NT:NT + 1], min_val=0, max_val=GBLOCKS)
            with pool.Fori(0, total) as g:
                c = slot_of(nc, pool, g, GBLOCKS)
                for i in range(BL):
                    pool.wait_ge(kept, g * BL + i + 1)
                    nc.gpsimd.tensor_copy(idx[:, i:i + 1], S.rec_sb[:, bass.ds(c + i, 1), 0:1].rearrange("p a b -> p (a b)")
                                          ).then_inc(indexed, 1)
                    count = pool.snap(g * BL + i + 1)
                    pool.wait_ge(indexed, 1)
                    pool.wait_ge(indexed, count)
                    pool.indirect_dma_start(land[:, i, :], None, S.table_gat,
                                            bass.IndirectOffsetOnAxis(ap=idx[:, i:i + 1], axis=0)).then_inc(gathered[i], 16)

        @block.vector
        def _(v):
            v.sem_inc(kept, BL)
            nc.vector.tensor_copy(lane[:], S.rec_sb[:, :, 1])
            v.drain()
            with v.Fori(0, NT) as t:
                g0, g1 = sorted_range(v, S.granges, t, GBLOCKS)
                nc.vector.memset(top[:], -BIG)
                v.drain()
                with v.Fori(g0, g1) as g:
                    c = slot_of(nc, v, g, GBLOCKS)
                    for i in range(BL):
                        nc.vector.tensor_scalar(nb[:, i, :], S.iota[:, 0:P], lane[:, bass.ds(c + i, 1)], -BIG, ALU.not_equal, ALU.mult)
                        v.wait_ge(gathered[i], g * 16 + 16)
                        nc.vector.tensor_copy(rows[:, bass.ds(c + i, 1), :], land[:, i:i + 1, :]).then_inc(kept, 1)
                        v.drain()
                        for h in range(HEADS):
                            nc.vector.scalar_tensor_tensor(top[:, h, :], nb[:, i, :], rows[:, bass.ds(c + i, 1), HW + h:HW + h + 1].rearrange("p a b -> p (a b)"),
                                                           top[:, h, :], ALU.add, ALU.max)
                v.drain().then_inc(best, 1)
                v.wait_ge(best_t, t + 1)
                nc.vector.tensor_reduce(ms[:, bass.ds(t, 1), :], psT[:].unsqueeze(1), AX.X, ALU.max).then_inc(evac, 1)
            v.drain()
            src_own, dst_own = own[:, :, HW:HW + HEADS], own[:, :, GW:GW + HEADS]
            nc.vector.tensor_tensor(ms[:], ms[:], src_own, ALU.max)
            v.drain()
            nc.vector.tensor_tensor(ms[:], ms[:], dst_own, ALU.add)
            nc.vector.tensor_tensor(zs[:], src_own, dst_own, ALU.add)
            v.drain()
            nc.vector.tensor_copy(val[:, :, 0:HEADS], dst_own)
            nc.vector.scalar_tensor_tensor(val[:, :, HEADS:2 * HEADS], ms[:], 0.2, ms[:], ALU.mult, ALU.max)
            nc.vector.scalar_tensor_tensor(zs[:], zs[:], 0.2, zs[:], ALU.mult, ALU.max)
            v.drain().then_inc(vals, 1)
            nc.vector.tensor_tensor(zs[:], zs[:], val[:, :, HEADS:2 * HEADS], ALU.subtract).then_inc(selfz, 1)
            with v.Fori(0, NT) as t:
                g0, g1 = sorted_range(v, S.granges, t, GBLOCKS)
                with v.Fori(g0, g1) as g:
                    c = slot_of(nc, v, g, GBLOCKS)
                    v.wait_ge(added, g)
                    for i in range(BL):
                        ins = nc.vector.tensor_scalar(onehot[:, i, :], S.iota[:, 0:P], lane[:, bass.ds(c + i, 1)], None, ALU.is_equal)
                    ins.then_inc(hot, 1)
                    v.wait_ge(ends, g + 1)
                    pe3 = psE[:, 0:BL * 2 * HEADS].rearrange("p (i k) -> p i k", i=BL)
                    nc.vector.tensor_tensor(z[:], rows[:, bass.ds(c, BL), HW:GW], pe3[:, :, 0:HEADS], ALU.add)
                    v.drain()
                    nc.vector.scalar_tensor_tensor(z2[:], z[:], 0.2, z[:], ALU.mult, ALU.max)
                    v.drain()
                    nc.vector.tensor_tensor(z[:], z2[:], pe3[:, :, HEADS:2 * HEADS], ALU.subtract).then_inc(logit, 1)
                    v.wait_ge(expd, g + 1)
                    nc.vector.tensor_tensor(w[:, :, 0:HW].rearrange("p i (h k) -> p i h k", h=HEADS),
                                            rows[:, bass.ds(c, BL), 0:HW].rearrange("p i (h k) -> p i h k", h=HEADS),
                                            w[:, :, HW:GW].unsqueeze(3).to_broadcast([P, BL, HEADS, HC]), ALU.mult).then_inc(weighed, 1)
                v.wait_ge(closed, t + 1)
                nc.vector.tensor_copy(sums[:, bass.ds(t, 1), :], psO[:, 0:GW].unsqueeze(1)).then_inc(closed_read, 1)
            v.drain()
            v.wait_ge(selfe, 1)
            heads = lambda a: a.rearrange("p t (h k) -> p t h k", h=HEADS)
            spread = lambda a: a.unsqueeze(3).to_broadcast([P, NT, HEADS, HC])
            row = lambda r: r[:].unsqueeze(1).to_broadcast([P, NT, HW])
            nc.vector.tensor_tensor(heads(tmp[:]), heads(own[:, :, 0:HW]), spread(zs[:]), ALU.mult)
            v.drain()
            nc.vector.tensor_tensor(zs[:], zs[:], sums[:, :, HW:GW], ALU.add)
            v.drain()
            nc.vector.tensor_tensor(tmp[:], tmp[:], sums[:, :, 0:HW], ALU.add)
            nc.vector.tensor_scalar(zs[:], zs[:], 1e-16, None, ALU.add)
            v.drain()
            nc.vector.reciprocal(zs[:], zs[:])
            v.drain()
            nc.vector.tensor_tensor(heads(tmp[:]), heads(tmp[:]), spread(zs[:]), ALU.mult)
            v.drain()
            v.wait_ge(loaded, 48)
            nc.vector.tensor_tensor(tmp[:], tmp[:], row(b_gat), ALU.add)
            v.drain()
            nc.vector.tensor_reduce(mean[:], tmp[:], AX.X, ALU.add)
            v.drain()
            nc.vector.tensor_scalar(mean[:], mean[:], 1.0 / HW, None, ALU.mult)
            v.drain()
            nc.vector.tensor_tensor(tmp[:], tmp[:], mean[:].unsqueeze(2).to_broadcast([P, NT, HW]), ALU.subtract)
            v.drain()
            nc.vector.tensor_tensor(sums[:, :, 0:HW], tmp[:], tmp[:], ALU.mult)
            v.drain()
            nc.vector.tensor_reduce(var[:], sums[:, :, 0:HW], AX.X, ALU.add)
            v.drain()
            nc.vector.tensor_scalar(var[:], var[:], 1.0 / HW, LNEPS, ALU.mult, ALU.add).then_inc(var_in, 1)
            v.wait_ge(rooted, 1)
            nc.vector.reciprocal(var[:], var[:])
            v.drain()
            nc.vector.tensor_tensor(tmp[:], tmp[:], var[:].unsqueeze(2).to_broadcast([P, NT, HW]), ALU.mult)
            v.drain()
            nc.vector.tensor_tensor(tmp[:], tmp[:], row(gamma), ALU.mult)
            v.drain()
            nc.vector.tensor_tensor(tmp[:], tmp[:], row(beta), ALU.add)
            v.drain()
            nc.vector.tensor_reduce(S.gate1[:], tmp[:].rearrange("p t (h k) -> p t k h", h=HEADS), AX.X, ALU.add)
            v.drain()
            nc.vector.tensor_scalar(S.gate1[:], S.gate1[:], 1.0 / HEADS, None, ALU.mult)
            v.drain()
            choose_two(nc, v, S, S.gate1, NE1, first, second, mean, topv)
            nc.vector.tensor_tensor(topv[:, :, 1], topv[:, :, 1], topv[:, :, 0], ALU.subtract).then_inc(dz, 1)
            v.wait_ge(de, 1)
            nc.vector.tensor_scalar(topv[:, :, 0], topv[:, :, 1], 1.0, None, ALU.add)
            v.drain()
            nc.vector.reciprocal(topv[:, :, 0], topv[:, :, 0])
            v.drain()
            nc.vector.tensor_tensor(topv[:, :, 1], topv[:, :, 1], topv[:, :, 0], ALU.mult)
            v.drain()
            nc.vector.tensor_tensor(first[:], first[:], topv[:, :, 0:1].to_broadcast([P, NT, NE1]), ALU.mult)
            nc.vector.tensor_tensor(second[:], second[:], topv[:, :, 1:2].to_broadcast([P, NT, NE1]), ALU.mult)
            v.drain()
            nc.vector.tensor_tensor(S.gate1[:], first[:], second[:], ALU.add)
            v.drain()

        @block.scalar
        def _(act):
            nc.scalar.preload_act_table(ACT.Exp)
            act.wait_ge(selfz, 1)
            nc.scalar.activation(zs[:], zs[:], ACT.Exp).then_inc(selfe, 1)
            total = act.value_load(S.granges[0:1, NT:NT + 1], min_val=0, max_val=GBLOCKS)
            with act.Fori(0, total) as g:
                act.wait_ge(hot_t, g + 1)
                nc.scalar.copy(onehot_t[:], psT[:]).then_inc(hot_tc, 1)
                act.wait_ge(logit, g + 1)
                act.wait_ge(added, g)
                nc.scalar.activation(w[:, :, HW:GW], z[:], ACT.Exp).then_inc(expd, 1)
            act.wait_ge(var_in, 1)
            nc.scalar.activation(var[:], var[:], ACT.Sqrt).then_inc(rooted, 1)
            act.wait_ge(dz, 1)
            nc.scalar.activation(topv[:, :, 1], topv[:, :, 1], ACT.Exp).then_inc(de, 1)

        @block.tensor
        def _(pe):
            with pe.Fori(0, NT) as t:
                pe.wait_ge(best, t + 1)
                for h in range(HEADS):
                    ins = nc.tensor.transpose(psT[:, h, :], top[:, h, :], S.ident[:])
                ins.then_inc(best_t, 1)
            pe.wait_ge(vals, 1)
            pe.wait_ge(evac, NT)
            with pe.Fori(0, NT) as t:
                g0, g1 = sorted_range(pe, S.granges, t, GBLOCKS)
                pe.wait_ge(closed_read, t)
                nc.tensor.matmul(psO[:, 0:GW], S.zeros[0:1, 0:P], S.iota[0:1, 0:GW], start=True, stop=False)
                with pe.Fori(g0, g1) as g:
                    pe.wait_ge(hot, g + 1)
                    pe.wait_ge(hot_tc, g)
                    for i in range(BL):
                        ins = nc.tensor.transpose(psT[:, i, :], onehot[:, i, :], S.ident[:])
                    ins.then_inc(hot_t, 1)
                    pe.wait_ge(hot_tc, g + 1)
                    for i in range(BL):
                        ins = nc.tensor.matmul(psE[:, i * 2 * HEADS:(i + 1) * 2 * HEADS], onehot_t[:, i, :],
                                               val[:, bass.ds(t, 1), :].rearrange("p a k -> p (a k)"), start=True, stop=True)
                    ins.then_inc(ends, 1)
                    pe.wait_ge(weighed, g + 1)
                    for i in range(BL):
                        ins = nc.tensor.matmul(psO[:, 0:GW], onehot[:, i, :], w[:, i, :], start=False, stop=False)
                    ins.then_inc(added, 1)
                nc.tensor.matmul(psO[:, 0:GW], S.zeros[0:1, 0:P], S.iota[0:1, 0:GW], start=False, stop=True).then_inc(closed, 1)


class _Shared:
    pass


def build_kernel(nc, A, out):
    with ExitStack() as ctx:
        S = _Shared()
        taken = []

        def sem(name):
            taken.append(nc.alloc_semaphore(name=name))
            return taken[-1]

        def end_stage():
            nc.clear_and_free_semaphores(taken)
            nc.all_engine_barrier()
            taken.clear()

        S.sem = sem

        def sb(n, s, d, c=ctx):
            return c.enter_context(nc.sbuf_tensor("k_" + n, s, d))

        def dram(n, s, d):
            return nc.dram_tensor(n, s, d, kind="Internal").ap()

        S.x = sb("x", [P, NT * D], F32)
        S.iota = sb("iota", [P, NP], F32)
        S.lane = sb("lane", [P, 1], F32)
        S.ident, S.tri, S.zeros, S.ones = (sb(n, [P, P], F32) for n in ("ident", "tri", "zeros", "ones"))
        S.identb = sb("identb", [P, P], BF16)
        S.countdown = sb("countdown", [P, NE0], F32)
        S.src = sb("src", [P, NCP], I32)
        S.dstf, S.ew, S.score, S.srct = (sb(n, [P, NCP], F32) for n in ("dstf", "ew", "score", "srct"))
        S.ranges = sb("ranges", [P, 64], I32)
        S.granges = sb("granges", [P, NT + 1], I32)
        S.rec_sb = sb("rec", [P, GS, 2], I32)
        S.erec_sb = sb("erec", [P, ES, 3], I32)
        S.esource, S.elane, S.eweight = sb("esource", [P, ES], I32), sb("elane", [P, ES], F32), sb("eweight", [P, ES], F32)
        S.eranges = sb("eranges", [P, NT + 1], I32)
        S.gate0, S.gate1 = sb("gate0", [P, NT, NE0], F32), sb("gate1", [P, NT, NE1], F32)
        S.lane_row = dram("lane_row", [NC * P], BF16)
        rec_dram = dram("records", [P * GS, 2], I32)
        erec_dram = dram("erecords", [P * ES, 3], I32)
        table = dram("table", [NP, TW], F32)
        S.table_gat = dram("table_gat", [NP, GW], F32)

        with ExitStack() as stage:
            S.table_sb = sb("tbl0", [P, NT, TW], F32, stage)
            S.w_aug = sb("w_aug", [P, KD, D + 4], F32, stage)
            S.bn_row = sb("bn_row", [P, D], F32, stage)
            S.we_attn, S.bias_attn = sb("we_attn", [P, 1], F32, stage), sb("bias_attn", [P, 1], F32, stage)
            S.hs = sb("hs", [P, NT], F32, stage)
            S.src_tile = sb("src_tile", [P, NC, NT], BF16, stage)
            emit_setup(nc, S, A)

            def rows_and_score(v, o, i, ps):
                nc.vector.tensor_tensor(S.table_sb[:, bass.ds(o * U + i, 1), 0:D], ps[:, 0:D].unsqueeze(1),
                                        S.bn_row[:].unsqueeze(1), ALU.add)
                nc.vector.tensor_copy(S.hs[:, bass.ds(o * U + i, 1)], ps[:, D:D + 1])

            emit_layernorm_project(nc, S, "l0", S.w_aug, D + 1, False, rows_and_score, table, S.table_sb)
            emit_edge_scores(nc, S, A)
        emit_aggregate(nc, S, "a0", table, True)
        end_stage()

        emit_sort_edges(nc, S, "so", GC, A["gsrc"], A["gdst"], None, GS, rec_dram, S.rec_sb, S.granges)
        emit_sort_edges(nc, S, "se", NC, A["dst_pc"][:, 0:NC], A["src_pc"][:, 0:NC], S.ew[:, 0:NC], ES, erec_dram, S.erec_sb,
                        S.eranges)
        with ExitStack() as stage:
            S.xnT = sb("xnT0", [P, KD, NP], F32, stage)
            wg = sb("wg", [P, KD, NE0], F32, stage)
            bg = sb("bg", [P, NE0], F32, stage)
            wg_in = S.sem("wg_in")

            def load_gate(v):
                v.wait_ge(wg_in, 32)

            with nc.Block() as block:
                @block.sync
                def _(sp):
                    sp.dma_start(wg[:], A["Wg"].rearrange("(k p) e -> p k e", p=P)).then_inc(wg_in, 16)
                    sp.dma_start(bg[:], A["bg"].unsqueeze(0).to_broadcast([P, NE0])).then_inc(wg_in, 16)
                    sp.wait_ge(wg_in, 32)

            def gate_scores(v, o, i, ps):
                nc.vector.tensor_tensor(S.gate0[:, bass.ds(o * U + i, 1), :], ps.unsqueeze(1), bg[:].unsqueeze(1), ALU.add)

            emit_layernorm_project(nc, S, "l1", wg, NE0, True, gate_scores)
            emit_top2_mask(nc, S)
            emit_experts(nc, S, "f0", A, NE0, S.gate0)
        end_stage()

        with ExitStack() as stage:
            w_in = S.sem("w1_in")
            with ExitStack() as inner:
                S.table_sb = sb("tbl1", [P, NT, TW], F32, inner)
                w = sb("w_gcn", [P, KD, D], F32, inner)
                with nc.Block() as block:
                    @block.sync
                    def _(sp):
                        sp.dma_start(w[:], A["gcn_W"].rearrange("(k p) o -> p k o", p=P)).then_inc(w_in, 16)
                        sp.wait_ge(w_in, 16)

                    @block.vector
                    def _(v):
                        nc.vector.memset(S.table_sb[:, :, D:TW], 0.0)
                        nc.vector.tensor_copy(S.esource[:], S.erec_sb[:, :, 0])
                        nc.vector.tensor_copy(S.elane[:], S.erec_sb[:, :, 1])
                        nc.vector.tensor_copy(S.eweight[:], S.erec_sb[:, :, 2].bitcast(F32))
                        v.drain()

                def rows(v, o, i, ps):
                    nc.vector.tensor_copy(S.table_sb[:, bass.ds(o * U + i, 1), 0:D], ps.unsqueeze(1))

                emit_layernorm_project(nc, S, "l2", w, D, False, rows, table, S.table_sb)
            S.agg = sb("agg", [P, NT * D], F32, stage)
            S.bias_row = sb("bias_row", [P, D], F32, stage)
            bias_in = S.sem("bias_in")
            with nc.Block() as block:
                @block.sync
                def _(sp):
                    sp.dma_start(S.bias_row[:], A["gcn_bias"].unsqueeze(0).to_broadcast([P, D])).then_inc(bias_in, 16)
                    sp.wait_ge(bias_in, 16)
            emit_aggregate(nc, S, "a1", table, False)
            emit_batchnorm(nc, S, A)
        end_stage()

        with ExitStack() as stage:
            S.xnT = sb("xnT1", [P, KD, NP], F32, stage)
            with ExitStack() as inner:
                S.gat_sb = sb("gat", [P, NT, GW + HEADS], F32, inner)
                wgat = sb("wgat", [P, KD, HW], F32, inner)
                att = sb("att", [P, 2, HW], F32, inner)
                wgat_in = S.sem("wgat_in")
                with nc.Block() as block:
                    @block.sync
                    def _(sp):
                        sp.dma_start(wgat[:], A["W_gat"].rearrange("(k p) o -> p k o", p=P)).then_inc(wgat_in, 16)
                        sp.dma_start(att[:, 0, :], A["att_src"].unsqueeze(0).to_broadcast([P, HW])).then_inc(wgat_in, 16)
                        sp.dma_start(att[:, 1, :], A["att_dst"].unsqueeze(0).to_broadcast([P, HW])).then_inc(wgat_in, 16)
                        sp.wait_ge(wgat_in, 48)

                def rows(v, o, i, ps):
                    nc.vector.tensor_copy(S.gat_sb[:, bass.ds(o * U + i, 1), 0:HW], ps.unsqueeze(1))

                emit_layernorm_project(nc, S, "l3", wgat, HW, True, rows)
                prod = sb("prod", [P, NT, HW], F32, inner)
                tabled = S.sem("gat_tabled")
                stored = S.sem("gat_stored")
                with nc.Block() as block:
                    @block.vector
                    def _(v):
                        for k in range(2):
                            nc.vector.tensor_tensor(prod[:], S.gat_sb[:, :, 0:HW], att[:, k, :].unsqueeze(1).to_broadcast([P, NT, HW]), ALU.mult)
                            v.drain()
                            nc.vector.tensor_reduce(S.gat_sb[:, :, HW + k * HEADS:HW + (k + 1) * HEADS],
                                                    prod[:].rearrange("p t (h k) -> p t h k", h=HEADS), AX.X, ALU.add)
                            v.drain()
                        v.drain().then_inc(tabled, 1)

                    @block.sync
                    def _(sp):
                        sp.wait_ge(tabled, 1)
                        sp.dma_start(S.table_gat.rearrange("(t p) d -> p t d", p=P), S.gat_sb[:, :, 0:GW]).then_inc(stored, 16)
                        sp.wait_ge(stored, 16)
                emit_routing(nc, S, A)
            emit_experts(nc, S, "f1", A, NE1, S.gate1)

        done = S.sem("out_done")
        with nc.Block() as block:
            @block.sync
            def _(sp):
                rows = (NT - 1) * P
                x3 = S.x[:].rearrange("p (t d) -> p t d", d=D)
                sp.dma_start(out[0:rows, :].rearrange("(t p) d -> p t d", p=P), x3[:, 0:NT - 1, :]).then_inc(done, 16)
                sp.dma_start(out[rows:N, :], x3[0:N - rows, NT - 1, :]).then_inc(done, 16)
                sp.wait_ge(done, 32)
        end_stage()


def kernel(x, src, dst, edge_attr_128, edge_weight, L0_gnn_Wn, L0_gnn_bn, L0_gnn_We, L0_gnn_be, L0_gnn_attn, L0_ffn_Wg,
           L0_ffn_bg, L0_ffn_W1, L0_ffn_b1, L0_ffn_W2, L0_ffn_b2, L1_gnn_W, L1_gnn_bias, L1_gnn_gamma, L1_gnn_beta,
           L1_ffn_W_gat, L1_ffn_att_src, L1_ffn_att_dst, L1_ffn_b_gat, L1_ffn_ln_gamma, L1_ffn_ln_beta, L1_ffn_W1,
           L1_ffn_b1, L1_ffn_W2, L1_ffn_b2, L1_ffn_edge_index):
    import concourse.bacc as bacc
    from concourse.bass_utils import run_bass_kernel_spmd

    def padded(a, rows, value):
        a = np.asarray(a)
        return np.concatenate([a, np.full((rows - a.shape[0],) + a.shape[1:], value, a.dtype)])

    def chunks(a, n_chunks, value=0):
        return np.ascontiguousarray(padded(a, n_chunks * P, value).reshape(n_chunks, P).T)

    ge = np.asarray(L1_ffn_edge_index)
    arrays = {
        "x": padded(x, NP, 0), "src_pc": chunks(src, NCP), "dst_pc": chunks(dst, NCP, NP - 1),
        "src_pj": padded(src, NC * P, 0).reshape(P, NC), "ew_pc": chunks(edge_weight, NCP),
        "eaT": np.ascontiguousarray(padded(edge_attr_128, NC * P, 0).T),
        "Wn": L0_gnn_Wn, "WnT": np.ascontiguousarray(np.asarray(L0_gnn_Wn).T), "We": L0_gnn_We, "bn": L0_gnn_bn,
        "be": L0_gnn_be, "attn": np.asarray(L0_gnn_attn).reshape(-1),
        "Wg": L0_ffn_Wg, "bg": L0_ffn_bg, "f0_W1": L0_ffn_W1, "f0_b1": L0_ffn_b1, "f0_W2": L0_ffn_W2, "f0_b2": L0_ffn_b2,
        "gcn_W": L1_gnn_W, "gcn_bias": L1_gnn_bias, "bn_gamma": L1_gnn_gamma, "bn_beta": L1_gnn_beta,
        "W_gat": L1_ffn_W_gat, "att_src": np.asarray(L1_ffn_att_src).reshape(-1),
        "att_dst": np.asarray(L1_ffn_att_dst).reshape(-1), "b_gat": L1_ffn_b_gat, "ln_gamma": L1_ffn_ln_gamma,
        "ln_beta": L1_ffn_ln_beta, "f1_W1": L1_ffn_W1, "f1_b1": L1_ffn_b1, "f1_W2": L1_ffn_W2, "f1_b2": L1_ffn_b2,
        "gsrc": chunks(ge[0], GC), "gdst": chunks(ge[1], GC),
    }
    arrays = {"in_" + k: np.ascontiguousarray(v) for k, v in arrays.items()}
    nc = bacc.Bacc("TRN2", target_bir_lowering=False, num_devices=1)
    aps = {k[3:]: nc.dram_tensor(k, v.shape, mybir.dt.from_np(v.dtype), kind="ExternalInput").ap()
           for k, v in arrays.items()}
    out = nc.dram_tensor("out_x", (N, D), F32, kind="ExternalOutput").ap()
    build_kernel(nc, aps, out)
    r = run_bass_kernel_spmd(nc, [arrays], core_ids=[0])
    return r.results[0]["out_x"]
```

```python
from contextlib import ExitStack

import concourse.bass as bass
import concourse.mybir as mybir
import numpy as np

F32, BF16, I32, U32 = mybir.dt.float32, mybir.dt.bfloat16, mybir.dt.int32, mybir.dt.uint32
ALU = mybir.AluOpType
ACT = mybir.ActivationFunctionType
AX = mybir.AxisListType

P = 128
N = 3125
NT = -(-N // P)
NP = NT * P
D = 256
KD = D // P
U = 5
SLOTS = 4
OUT = NT // U
E = 53125
NC = -(-E // P)
BL = 4
BG = 6
NCP = NC + BG
KB = -(-NC // BG) + 1
ED = 128
PIECE = 26
NPIECE = NC // PIECE
BIG = 1.0e30
LNEPS = 1e-5
TW = 260
H0 = 512
KH = H0 // P
NE0, NE1 = 8, 4
GE = 32768
GC = GE // P
GBLOCKS = GE // (BL * P) + NT
GS = GBLOCKS * BL
EBLOCKS = NC // BG + 1 + NT
ES = EBLOCKS * BG
PACK = 512
EARLY = 176
HEADS, HC = 4, NE1
HW = HEADS * HC
SPREAD = (2, 3)
GW = HW + HEADS


def emit_layernorm_project(nc, S, tag, w, n_out, keep_xT, sink, table=None, table_sb=None, before=None):
    sem, x = S.sem, S.x
    stats_ready, rstd_root = sem(tag + "_stats"), sem(tag + "_root")
    xn_ready, transposed = sem(tag + "_xn"), sem(tag + "_tp")
    xt_ready, projected, sunk, stored = sem(tag + "_xt"), sem(tag + "_pj"), sem(tag + "_sunk"), sem(tag + "_st")
    with ExitStack() as ctx:
        sb = lambda n, s, d: ctx.enter_context(nc.sbuf_tensor(tag + n, s, d))
        st = sb("st", [P, U, 6], F32)
        mv = sb("mv", [P, U, 2], F32)
        root = sb("root", [P, U], F32)
        xn = sb("xn", [P, U, D], F32)
        xT = sb("xT", [P, U, D], F32)
        tp = ctx.enter_context(nc.psum_tensor(tag + "tp", [P, SLOTS, 512], F32))
        pj = ctx.enter_context(nc.psum_tensor(tag + "pj", [P, SLOTS, 512], F32))
        block = ctx.enter_context(nc.Block())

        @block.vector
        def _(v):
            if before is not None:
                before(v)
            v.sem_inc(sunk, U)
            with v.Fori(0, OUT) as o:
                for i in range(U):
                    nc.vector.bn_stats(st[:, i, :], x[:, bass.ds(o * (U * D) + i * D, D)])
                v.drain()
                for i in range(U):
                    nc.vector.bn_aggr(mv[:, i, :], st[:, i, :])
                v.drain()
                nc.vector.tensor_scalar(root[:], mv[:, :, 1], LNEPS, None, ALU.add).then_inc(stats_ready, 1)
                v.wait_ge(rstd_root, o + 1)
                nc.vector.reciprocal(root[:], root[:])
                v.drain()
                v.wait_ge(transposed, (o + 1) * U)
                for i in range(U):
                    nc.vector.tensor_scalar(xn[:, i, :], x[:, bass.ds(o * (U * D) + i * D, D)], mv[:, i, 0:1],
                                            root[:, i:i + 1], ALU.subtract, ALU.mult).then_inc(xn_ready, 1)
                for i in range(U):
                    v.wait_ge(projected, (o + 1) * U + i + 1)
                    sink(v, o, i, pj[:, i % SLOTS, 0:n_out])
                    v.drain().then_inc(sunk, 1)

        @block.scalar
        def _(act):
            nc.scalar.preload_act_table(ACT.Sqrt)
            act.sem_inc(xt_ready, U)
            with act.Fori(0, OUT) as o:
                act.wait_ge(stats_ready, o + 1)
                nc.scalar.activation(root[:], root[:], ACT.Sqrt).then_inc(rstd_root, 1)
                act.wait_ge(projected, (o + 1) * U)
                for i in range(U):
                    act.wait_ge(transposed, (o + 1) * U + i + 1)
                    ins = nc.scalar.copy(xT[:, i, :], tp[:, i % SLOTS, 0:D])
                    if keep_xT:
                        ins = nc.scalar.copy(S.xnT[:, :, bass.ds(o * (U * P) + i * P, P)],
                                             tp[:, i % SLOTS, 0:D].rearrange("p (k n) -> p k n", k=KD))
                    ins.then_inc(xt_ready, 1)

        @block.tensor
        def _(pe):
            for each in (transposed, projected):
                pe.sem_inc(each, U)
            with pe.Fori(0, OUT) as o:
                pe.wait_ge(xt_ready, (o + 1) * U)
                for i in range(U):
                    if i >= SLOTS:
                        pe.wait_ge(xt_ready, (o + 1) * U + i - SLOTS + 1)
                    pe.wait_ge(xn_ready, o * U + i + 1)
                    for k in range(KD):
                        ins = nc.tensor.transpose(tp[:, i % SLOTS, k * P:(k + 1) * P], xn[:, i, k * P:(k + 1) * P], S.ident[:])
                    ins.then_inc(transposed, 1)
                pe.wait_ge(sunk, (o + 1) * U)
                for i in range(U):
                    if i >= SLOTS:
                        pe.wait_ge(sunk, (o + 1) * U + i - SLOTS + 1)
                    pe.wait_ge(xt_ready, (o + 1) * U + i + 1)
                    for k in range(KD):
                        ins = nc.tensor.matmul(pj[:, i % SLOTS, 0:n_out], xT[:, i, k * P:(k + 1) * P], w[:, k, 0:n_out],
                                               start=(k == 0), stop=(k == KD - 1))
                    ins.then_inc(projected, 1)

        if table is not None:
            @block.sync
            def _(sp):
                rows = table.rearrange("(t p) d -> p t d", p=P)
                width = table.shape[1]
                with sp.Fori(0, OUT) as o:
                    sp.wait_ge(sunk, (o + 2) * U)
                    sp.dma_start(rows[:, bass.ds(o * U, U), :],
                                 table_sb[:, bass.ds(o * U, U), :]).then_inc(stored, 16)
                sp.wait_ge(stored, 16 * OUT)


def emit_setup(nc, S, A):
    sem = S.sem
    made, loaded, tables, wide, prods, dve1, cols, small = (sem("su_" + n) for n in (
        "made", "loaded", "tables", "wide", "prods", "dve1", "cols", "small"))
    laned = sem("su_laned")
    with ExitStack() as ctx:
        sb = lambda n, s, d: ctx.enter_context(nc.sbuf_tensor("su_" + n, s, d))
        wn = sb("wn", [P, KD, D], F32)
        we = sb("we", [P, KD, ED], F32)
        attn = sb("attn", [P, KD], F32)
        attn_wide = sb("attnw", [P, KD, P], F32)
        bsum = sb("bsum", [P, KD], F32)
        be = sb("be", [P, KD], F32)
        dsti = sb("dsti", [P, NCP], I32)
        tilei = sb("tilei", [P, NCP], I32)
        span = sb("span", [P, 2, NC], F32)
        spanmax = sb("spanmax", [P, 2, NC], F32)
        has = sb("has", [P, 2, NC], F32)
        key = sb("key", [P, 2, NC], F32)
        ends = sb("ends", [P, 2], F32)
        cnt = sb("cnt", [P, 2], F32)
        starts = sb("starts", [P, KB], F32)
        word = sb("word", [P, NT], F32)
        spj = sb("spj", [P, NC], I32)
        lane = sb("lane", [P, NC], BF16)
        ps = ctx.enter_context(nc.psum_tensor("su_ps", [P, 512], F32))
        block = ctx.enter_context(nc.Block())

        @block.gpsimd
        def _(pool):
            nc.gpsimd.iota(S.iota[:], [[1, NP]], base=0, channel_multiplier=0,
                           allow_small_or_imprecise_dtypes=True).then_inc(made, 1)
            nc.gpsimd.iota(S.lane[:], [[1, 1]], base=0, channel_multiplier=1,
                           allow_small_or_imprecise_dtypes=True).then_inc(made, 1)
            pool.wait_ge(tables, 2)
            nc.gpsimd.partition_all_reduce(spanmax[:].rearrange("p a c -> p (a c)"),
                                           span[:].rearrange("p a c -> p (a c)"), P, bass.bass_isa.ReduceOp.max).then_inc(wide, 1)

        @block.sync
        def _(sp):
            for dst, src in ((dsti[:], A["dst_pc"]), (S.src[:], A["src_pc"]), (spj[:], A["src_pj"]),
                             (attn[:], A["attn"].rearrange("(k p) -> p k", p=P)), (bsum[:], A["bn"].rearrange("(k p) -> p k", p=P)),
                             (be[:], A["be"].rearrange("(k p) -> p k", p=P)),
                             (wn[:], A["Wn"].rearrange("(k p) i -> p k i", p=P)), (we[:], A["We"].rearrange("(k p) i -> p k i", p=P)),
                             (S.w_aug[:, :, 0:D], A["WnT"].rearrange("(k p) o -> p k o", p=P)),
                             (S.bn_row[:], A["bn"].rearrange("(a d) -> a d", a=1).to_broadcast([P, D])),
                             (S.x[:].rearrange("p (t d) -> p t d", d=D), A["x"].rearrange("(t p) d -> p t d", p=P)),
                             (S.ew[:], A["ew_pc"])):
                with nc.allow_non_contiguous_dma(reason="a few vectors, one element to a partition"):
                    sp.dma_start(dst, src).then_inc(loaded, 16)
            sp.wait_ge(laned, 1)
            sp.dma_start(S.lane_row.rearrange("(p j) -> p j", p=P), lane[:]).then_inc(loaded, 16)
            sp.wait_ge(loaded, 16 * 13)

        @block.vector
        def _(v):
            v.wait_ge(made, 2)
            nc.vector.tensor_scalar(S.ident[:], S.iota[:, 0:P], S.lane[:, 0:1], None, ALU.is_equal)
            nc.vector.tensor_scalar(S.identb[:], S.iota[:, 0:P], S.lane[:, 0:1], None, ALU.is_equal)
            nc.vector.tensor_scalar(S.tri[:], S.iota[:, 0:P], S.lane[:, 0:1], None, ALU.is_gt)
            nc.vector.tensor_copy(S.iotab[:], S.iota[:, 0:P])
            nc.vector.memset(S.zeros[:], 0.0)
            nc.vector.memset(S.ones[:], 1.0)
            nc.vector.memset(S.table_sb[:], 1.0)
            nc.vector.tensor_scalar(S.countdown[:], S.iota[:, 0:NE0], -1.0, float(NE0), ALU.mult, ALU.add)
            v.drain()
            v.wait_ge(loaded, 16 * 12)
            nc.vector.tensor_scalar(tilei[:], dsti[:], 7, None, ALU.logical_shift_right)
            nc.vector.tensor_copy(S.dstf[:], dsti[:])
            v.drain()
            nc.vector.tensor_copy(span[:, 0, :], tilei[:, 0:NC])
            v.drain()
            nc.vector.tensor_scalar(span[:, 1, :], span[:, 0, :], -1.0, None, ALU.mult)
            v.drain().then_inc(tables, 2)
            nc.vector.tensor_scalar(spj[:], spj[:], P - 1, None, ALU.bitwise_and)
            nc.vector.tensor_scalar(tilei[:], S.src[:], 7, None, ALU.logical_shift_right)
            v.drain()
            nc.vector.tensor_copy(lane[:], spj[:])
            nc.vector.tensor_copy(S.srct[:], tilei[:])
            v.drain().then_inc(laned, 1)
            nc.vector.tensor_tensor(S.src_tile[:], S.srct[:, 0:NC].unsqueeze(2).to_broadcast([P, NC, NT]),
                                    S.iota[:, 0:NT].unsqueeze(1).to_broadcast([P, NC, NT]), ALU.is_equal)
            nc.vector.tensor_tensor(bsum[:], bsum[:], be[:], ALU.add)
            for k in range(KD):
                nc.vector.tensor_scalar(attn_wide[:, k, :], S.ones[:, 0:P], attn[:, k:k + 1], None, ALU.mult)
            v.drain().then_inc(dve1, 1)
            v.wait_ge(prods, 1)
            nc.vector.tensor_copy(S.w_aug[:, :, D:D + 1], ps[:, 0:KD].unsqueeze(2))
            nc.vector.tensor_copy(S.we_attn[:], ps[:, 2:3])
            nc.vector.tensor_copy(S.bias_attn[:], ps[:, 3:4])
            v.wait_ge(wide, 1)
            nc.vector.tensor_scalar(has[:, 0, :], spanmax[:, 0, :], S.lane[:, 0:1], None, ALU.is_ge)
            nc.vector.tensor_scalar(has[:, 1, :], spanmax[:, 1, :], -1.0, S.lane[:, 0:1], ALU.mult, ALU.is_le)
            nc.vector.tensor_scalar(key[:, 0, :], S.iota[:, 0:NC], 1.0, None, ALU.add)
            nc.vector.tensor_scalar(key[:, 1, :], S.iota[:, 0:NC], -1.0, float(NC), ALU.mult, ALU.add)
            v.drain()
            nc.vector.tensor_tensor(has[:, 0, :], has[:, 0, :], has[:, 1, :], ALU.mult)
            v.drain()
            nc.vector.tensor_tensor(key[:], key[:], has[:, 0, :].unsqueeze(1).to_broadcast([P, 2, NC]), ALU.mult)
            v.drain()
            nc.vector.tensor_reduce(ends[:], key[:], AX.X, ALU.max)
            v.drain()
            nc.vector.tensor_scalar(starts[:], S.iota[:, 0:KB], float(BG), None, ALU.mult)
            nc.vector.tensor_scalar(cnt[:, 1:2], ends[:, 1:2], -1.0, float(NC), ALU.mult, ALU.add)
            v.drain()
            nc.vector.tensor_scalar(cnt[:, 1:2], cnt[:, 1:2], float(NC - BG), None, ALU.min)
            v.drain()
            nc.vector.tensor_tensor(cnt[:, 0:1], ends[:, 0:1], cnt[:, 1:2], ALU.subtract)
            v.drain()
            nc.vector.tensor_scalar(starts[:], starts[:], cnt[:, 0:1], None, ALU.is_lt)
            v.drain()
            nc.vector.tensor_reduce(cnt[:, 0:1], starts[:], AX.X, ALU.add)
            v.drain()
            nc.vector.tensor_scalar(cnt[:, 0:1], cnt[:, 0:1], 1.0, None, ALU.max)
            v.drain().then_inc(cols, 1)
            v.wait_ge(small, 1)
            nc.vector.tensor_scalar(word[0:1, :], ps[0:1, 8 + 1:8 + 1 + NT], float(PACK), None, ALU.mult)
            v.drain()
            nc.vector.tensor_tensor(word[0:1, :], word[0:1, :], ps[0:1, 8 + 32:8 + 32 + NT], ALU.add)
            v.drain()
            nc.vector.tensor_copy(S.ranges[0:1, :], word[0:1, :])
            v.drain()

        @block.tensor
        def _(pe):
            pe.wait_ge(dve1, 1)
            for i in range(KD):
                for k in range(KD):
                    nc.tensor.matmul(ps[:, i:i + 1], wn[:, k, i * P:(i + 1) * P], attn[:, k:k + 1],
                                     start=(k == 0), stop=(k == KD - 1))
            for k in range(KD):
                nc.tensor.matmul(ps[:, 2:3], we[:, k, :], attn[:, k:k + 1], start=(k == 0), stop=(k == KD - 1))
            for k in range(KD):
                ins = nc.tensor.matmul(ps[:, 3:4], attn_wide[:, k, :], bsum[:, k:k + 1],
                                       start=(k == 0), stop=(k == KD - 1))
            ins.then_inc(prods, 1)
            pe.wait_ge(cols, 1)
            nc.tensor.matmul(ps[0:1, 8:8 + 32], cnt[0:NT, 0:1], S.tri[0:NT, 0:32], start=True, stop=True)
            nc.tensor.matmul(ps[0:1, 8 + 32:8 + 64], cnt[0:NT, 1:2], S.ident[0:NT, 0:32],
                             start=True, stop=True).then_inc(small, 1)


def emit_edge_scores(nc, S, A, scatter):
    sem = S.sem
    arrived = [sem(f"es_in{i}") for i in range(2)]
    split, hot, mm, used, read = sem("es_split"), sem("es_hot"), sem("es_mm"), sem("es_used"), sem("es_read")
    HALF = PIECE // 2
    with ExitStack() as ctx:
        sb = lambda n, s, d: ctx.enter_context(nc.sbuf_tensor("es_" + n, s, d))
        ea = sb("ea", [P, 2, PIECE * P], F32)
        lane = sb("lane", [P, 2, PIECE * P], BF16)
        onehot = sb("hot", [P, 2, PIECE * P], BF16)
        parts = sb("parts", [P, 3, NT], BF16)
        rest = sb("rest", [P, 2, NT], F32)
        picked = sb("picked", [P, PIECE, NT], F32)
        ps = [ctx.enter_context(nc.psum_tensor(f"es_ps{i}", [P, 3, 512], F32)) for i in range(2)]
        block = ctx.enter_context(nc.Block())
        lane_row = S.lane_row.rearrange("(a n) -> a n", a=1)

        @block.sync
        def _(sp):
            with sp.Fori(0, NPIECE // 2) as o:
                for i in range(2):
                    sp.wait_ge(read, 2 * o + i + 1)
                    col = o * (2 * PIECE * P) + i * PIECE * P
                    sp.dma_start(ea[:, i, :], A["eaT"][:, bass.ds(col, PIECE * P)]).then_inc(arrived[i], 16)
                    sp.dma_start(lane[:, i, :], lane_row[:, bass.ds(col, PIECE * P)].to_broadcast([P, PIECE * P])
                                 ).then_inc(arrived[i], 16)

            scatter.finish(sp)

        @block.gpsimd
        def _(pool):
            scatter.run(pool)

        @block.vector
        def _(v):
            nc.vector.tensor_copy(parts[:, 0, :], S.hs[:])
            v.drain()
            nc.vector.tensor_tensor(rest[:, 0, :], S.hs[:], parts[:, 0, :], ALU.subtract)
            v.drain()
            nc.vector.tensor_copy(parts[:, 1, :], rest[:, 0, :])
            v.drain()
            nc.vector.tensor_tensor(rest[:, 1, :], rest[:, 0, :], parts[:, 1, :], ALU.subtract)
            v.drain()
            nc.vector.tensor_copy(parts[:, 2, :], rest[:, 1, :])
            v.drain().then_inc(split, 1)
            v.sem_inc(read, 2)
            with v.Fori(0, NPIECE // 2) as o:
                for i in range(2):
                    v.wait_ge(arrived[i], 32 * o + 32)
                    nc.vector.tensor_scalar(onehot[:, i, :], lane[:, i, :], S.lane[:, 0:1], None, ALU.is_equal
                                            ).then_inc(hot, 1)
                    v.wait_ge(mm, 2 * o + i + 1)
                    c = o * (2 * PIECE) + i * PIECE
                    nc.vector.tensor_tensor(
                        picked[:].rearrange("p (a c) t -> p a (c t)", a=2), ps[i][:, 0:2, 0:HALF * NT],
                        S.src_tile[:, bass.ds(c, PIECE), :].rearrange("p (a c) t -> p a (c t)", a=2), ALU.mult)
                    v.drain()
                    nc.vector.tensor_reduce(S.score[:, bass.ds(c, PIECE)], picked[:], AX.X, ALU.add)
                    v.drain()
                    nc.vector.tensor_tensor(S.score[:, bass.ds(c, PIECE)], S.score[:, bass.ds(c, PIECE)],
                                            ps[i][:, 2, 0:PIECE], ALU.add)
                    v.drain().then_inc(read, 1)
            nc.vector.memset(S.score[:, NC:NCP], 0.0)
            nc.vector.tensor_scalar(S.score[:, 0:NC], S.score[:, 0:NC], S.bias_attn[:, 0:1], None, ALU.add)
            v.drain()
            nc.vector.tensor_scalar(picked[:, 0:17, :].rearrange("p c t -> p (c t)")[:, 0:NC], S.score[:, 0:NC], 0.01, None, ALU.mult)
            v.drain()
            nc.vector.tensor_tensor(S.score[:, 0:NC], S.score[:, 0:NC],
                                    picked[:, 0:17, :].rearrange("p c t -> p (c t)")[:, 0:NC], ALU.max)
            v.drain()

        @block.tensor
        def _(pe):
            pe.wait_ge(split, 1)
            with pe.Fori(0, NPIECE // 2) as o:
                for i in range(2):
                    pe.wait_ge(read, 2 * o + i + 1)
                    pe.wait_ge(arrived[i], 32 * o + 32)
                    for c in range(PIECE):
                        nc.tensor.matmul(ps[i][:, 2, c:c + 1], ea[:, i, c * P:(c + 1) * P], S.we_attn[:, 0:1],
                                         start=True, stop=True)
                    pe.wait_ge(hot, 2 * o + i + 1)
                    for c in range(PIECE):
                        for k in range(3):
                            ins = nc.tensor.matmul(ps[i][:, c // HALF, (c % HALF) * NT:(c % HALF + 1) * NT],
                                                   onehot[:, i, c * P:(c + 1) * P], parts[:, k, :],
                                                   start=(k == 0), stop=(k == 2))
                    ins.then_inc(mm, 1)


def tile_range(nc, eng, S, t):
    word = eng.value_load(S.ranges[0:1, bass.ds(t, 1)], min_val=PACK, max_val=NT * KB * PACK)
    return eng.snap(word // PACK), eng.snap(word % PACK)


def chunk_of(nc, eng, g, g0, c0):
    return eng.snap(nc.s_assert_within(c0 + (g - g0) * BG, 0, NC, skip_runtime_bounds_check_because=
                                       "a tile's blocks end within a block of its last chunk"))


def slot_of(nc, eng, g, blocks, size=BL):
    return eng.snap(nc.s_assert_within(g * size, 0, (blocks - 1) * size, skip_runtime_bounds_check_because=
                                       "whole blocks of all tiles are at most so many"))


def emit_aggregate(nc, S, tag, table, softmax):
    sem = S.sem
    gathered = [sem(f"{tag}_g{i}") for i in range(BG)]
    indexed, agg_done, masked, weighed = sem(tag + "_idx"), sem(tag + "_agg"), sem(tag + "_msk"), sem(tag + "_w")
    best, best_t, negs, negs_w, closed, evac = (sem(f"{tag}_{n}") for n in ("best", "bestT", "negs", "negsW", "closed", "evac"))
    width = D + 1 if softmax else D
    with ExitStack() as ctx:
        sb = lambda n, s, d: ctx.enter_context(nc.sbuf_tensor(tag + n, s, d))
        idx = sb("idx", [P, BG], I32)
        rows = sb("rows", [P, BG, TW], F32)
        w = sb("w", [P, BG, P], F32)
        nb = sb("nb", [P, BG, P], F32)
        mb = sb("mb", [P, BG, P], F32)
        top = sb("top", [P, BG, P], F32)
        top1 = sb("top1", [P, P], F32)
        m = sb("m", [P, 1], F32)
        diag = sb("diag", [P, P], F32)
        negm = sb("negm", [P, P], F32)
        rden = sb("rden", [P, 1], F32)
        relu = sb("relu", [P, D], F32)
        ps = ctx.enter_context(nc.psum_tensor(tag + "ps", [P, 512], F32))
        psT = ctx.enter_context(nc.psum_tensor(tag + "psT", [P, 512], F32))
        psM = ctx.enter_context(nc.psum_tensor(tag + "psM", [P, 512], F32))
        block = ctx.enter_context(nc.Block())

        source = S.src if softmax else S.esource

        class Tiles:

            def __init__(self, eng, who):
                self.eng = eng
                self.start, self.stop, self.first = (eng.alloc_register(f"{tag}_{who}_{n}") for n in ("start", "stop", "first"))
                eng.reg_mov(self.stop, 0)

            def load(self, t):
                if softmax:
                    self.next, self.next_first = tile_range(nc, self.eng, S, t)
                else:
                    self.next = self.eng.value_load(S.eranges[0:1, bass.ds(t + 1, 1)], min_val=0, max_val=EBLOCKS)

            def step(self):
                self.eng.reg_mov(self.start, self.stop)
                self.eng.reg_mov(self.stop, self.next)
                if softmax:
                    self.eng.reg_mov(self.first, self.next_first)
                    self.block, self.at = self.eng.snap(self.start), self.eng.snap(self.first)

            def blocks(self):
                return self.eng.Fori(self.start, self.stop)

            def chunk(self, g):
                if softmax:
                    return chunk_of(nc, self.eng, g, self.block, self.at)
                return slot_of(nc, self.eng, g, EBLOCKS, BG)

        def gather(pool, g, c):
            for i in range(BG):
                pool.wait_ge(agg_done, g * BG + i + 1)
                nc.gpsimd.tensor_copy(idx[:, i:i + 1], source[:, bass.ds(c + i, 1)]).then_inc(indexed, 1)
                count = pool.snap(g * BG + i + 1)
                pool.wait_ge(indexed, 1)
                pool.wait_ge(indexed, count)
                pool.indirect_dma_start(rows[:, i, 0:TW], None, table,
                                        bass.IndirectOffsetOnAxis(ap=idx[:, i:i + 1], axis=0)).then_inc(gathered[i], 16)

        @block.gpsimd
        def _(pool):
            if softmax:
                tiles = Tiles(pool, "pool")
                with pool.Fori(0, NT) as t:
                    tiles.load(t)
                    tiles.step()
                    with tiles.blocks() as g:
                        gather(pool, g, tiles.chunk(g))
            else:
                total = pool.value_load(S.eranges[0:1, NT:NT + 1], min_val=0, max_val=EBLOCKS)
                with pool.Fori(0, total) as g:
                    gather(pool, g, slot_of(nc, pool, g, EBLOCKS, BG))

        @block.tensor
        def _(pe):
            pe.sem_inc(agg_done, BG)
            tiles = Tiles(pe, "pe")

            def find_max(t):
                pe.wait_ge(best, t + 1)
                nc.tensor.transpose(psT[:, 0:P], top1[:], S.ident[:]).then_inc(best_t, 1)

            def sum_tile(t):
                tiles.load(t)
                tiles.step()
                if softmax:
                    pe.wait_ge(negs, t + 1)
                    nc.tensor.matmul(psM[:, 0:P], S.ones[:, 0:P], diag[:], start=True, stop=True).then_inc(negs_w, 1)
                pe.wait_ge(evac, t + 1)
                nc.tensor.matmul(ps[:, 0:width], S.zeros[0:1, 0:P], S.iota[0:1, 0:width], start=True, stop=False)

            def add_blocks():
                with tiles.blocks() as g:
                    for i in range(BG):
                        pe.wait_ge(gathered[i], g * 16 + 16)
                        pe.wait_ge(weighed, g * BG + i + 2)
                        nc.tensor.matmul(ps[:, 0:width], w[:, i, :], rows[:, i, 0:width],
                                         start=False, stop=False).then_inc(agg_done, 1)
                nc.tensor.matmul(ps[:, 0:width], S.zeros[0:1, 0:P], S.iota[0:1, 0:width],
                                 start=False, stop=True).then_inc(closed, 1)

            if softmax:
                find_max(0)
                with pe.Fori(0, NT - 1) as t:
                    sum_tile(t)
                    find_max(t + 1)
                    add_blocks()
                sum_tile(NT - 1)
                add_blocks()
            else:
                with pe.Fori(0, NT) as t:
                    sum_tile(t)
                    add_blocks()

        if not softmax:
            @block.vector
            def _(v):
                v.sem_inc(weighed, 1)
                v.sem_inc(evac, 1)
                tiles = Tiles(v, "v")
                with v.Fori(0, NT) as t:
                    tiles.load(t)
                    tiles.step()
                    with tiles.blocks() as g:
                        c = tiles.chunk(g)
                        for i in range(BG):
                            v.wait_ge(agg_done, g * BG + i + 1)
                            nc.vector.tensor_scalar(w[:, i, :], S.iota[:, 0:P], S.elane[:, bass.ds(c + i, 1)],
                                                    S.eweight[:, bass.ds(c + i, 1)], ALU.is_equal, ALU.mult).then_inc(weighed, 1)
                    v.wait_ge(closed, t + 1)
                    nc.vector.tensor_tensor(S.agg[:, bass.ds(t * D, D)], ps[:, 0:D], S.bias_row[:], ALU.add).then_inc(evac, 1)
            return

        @block.vector
        def _(v):
            v.sem_inc(evac, 1)
            ahead, tiles = Tiles(v, "scan"), Tiles(v, "v")

            def mask(to, t, c, i):
                nc.vector.tensor_scalar(to[:, i, :], S.iota[:, bass.ds(t * P, P)], S.dstf[:, bass.ds(c + i, 1)], -BIG,
                                        ALU.not_equal, ALU.mult)

            def scan(t):
                ahead.load(t)
                ahead.step()
                nc.vector.memset(top[:], -BIG)
                v.drain()
                with ahead.blocks() as g:
                    c = ahead.chunk(g)
                    for i in range(BG):
                        mask(mb, t, c, i)
                    v.drain()
                    for i in range(BG):
                        nc.vector.scalar_tensor_tensor(top[:, i, :], mb[:, i, :], S.score[:, bass.ds(c + i, 1)], top[:, i, :],
                                                       ALU.add, ALU.max)
                    v.drain()
                nc.vector.tensor_reduce(top1[:], top[:].rearrange("p i n -> p n i"), AX.X, ALU.max).then_inc(best, 1)

            def negate_max(t):
                v.wait_ge(best_t, t + 1)
                nc.vector.tensor_reduce(m[:], psT[:, 0:P], AX.X, ALU.max)
                v.drain()
                nc.vector.tensor_scalar(m[:], m[:], -0.1 * BIG, -1.0, ALU.max, ALU.mult)
                v.drain()
                nc.vector.tensor_scalar(diag[:], S.ident[:], m[:, 0:1], None, ALU.mult).then_inc(negs, 1)

            def mask_tile(t):
                v.wait_ge(negs_w, t + 1)
                nc.vector.tensor_copy(negm[:], psM[:, 0:P])
                v.drain()
                with tiles.blocks() as g:
                    c = tiles.chunk(g)
                    v.wait_ge(weighed, g * BG + 1)
                    for i in range(BG):
                        mask(nb, t, c, i)
                    v.drain()
                    nc.vector.tensor_tensor(nb[:], nb[:], negm[:].unsqueeze(1).to_broadcast([P, BG, P]), ALU.add
                                            ).then_inc(masked, 1)

            def finish_tile(t, n):
                v.wait_ge(closed, n)
                nc.vector.tensor_scalar(rden[:], ps[:, D:D + 1], 1e-16, None, ALU.add)
                v.drain()
                nc.vector.reciprocal(rden[:], rden[:])
                v.drain()
                nc.vector.tensor_scalar(relu[:], ps[:, 0:D], rden[:, 0:1], 0.0, ALU.mult, ALU.max).then_inc(evac, 1)
                v.drain()
                nc.vector.tensor_tensor(S.x[:, bass.ds(t * D, D)], S.x[:, bass.ds(t * D, D)], relu[:], ALU.add)

            scan(0)
            negate_max(0)
            tiles.next, tiles.next_first = ahead.stop, ahead.first
            tiles.step()
            scan(1)
            mask_tile(0)
            negate_max(1)
            with v.Fori(1, NT - 1) as t:
                tiles.step()
                scan(t + 1)
                finish_tile(t - 1, t)
                mask_tile(t)
                negate_max(t + 1)
            tiles.step()
            finish_tile(NT - 2, NT - 1)
            mask_tile(NT - 1)
            finish_tile(NT - 1, NT)
            v.drain()

        @block.scalar
        def _(act):
            nc.scalar.preload_act_table(ACT.Exp)
            act.sem_inc(weighed, 1)
            tiles = Tiles(act, "act")
            with act.Fori(0, NT) as t:
                tiles.load(t)
                tiles.step()
                with tiles.blocks() as g:
                    c = tiles.chunk(g)
                    act.wait_ge(masked, g + 1)
                    for i in range(BG):
                        act.wait_ge(agg_done, g * BG + i + 1)
                        nc.scalar.activation(w[:, i, :], nb[:, i, :], ACT.Exp, bias=S.score[:, bass.ds(c + i, 1)]).then_inc(weighed, 1)


def emit_experts(nc, S, tag, A, n_experts, gate, beside=()):
    sem = S.sem
    STEPS, HALF = 2 * OUT, U * P // 2
    arrived = [sem(f"{tag}_w{i}") for i in range(2)]
    up_done, hid_ready, down_done, added, b2_in = (sem(f"{tag}_{n}") for n in ("up", "hid", "down", "add", "b2"))
    W1, b1, W2, b2 = A[tag + "_W1"], A[tag + "_b1"], A[tag + "_W2"], A[tag + "_b2"]
    with ExitStack() as ctx:
        sb = lambda n, s, d: ctx.enter_context(nc.sbuf_tensor(tag + n, s, d))
        w1 = [sb(f"w1_{i}", [P, KD, H0], F32) for i in range(2)]
        w2 = [sb(f"w2_{i}", [P, KH, D], F32) for i in range(2)]
        bias1 = [sb(f"b1_{i}", [P, KH], F32) for i in range(2)]
        hid = [sb(f"hid{i}", [P, KH, 2, HALF], F32) for i in range(2)]
        b2_rows = sb("b2", [P, n_experts, D], F32)
        up = [ctx.enter_context(nc.psum_tensor(f"{tag}up{i}", [P, 2, 512], F32)) for i in range(2)]
        down = [ctx.enter_context(nc.psum_tensor(f"{tag}dn{i}", [P, 512], F32)) for i in range(4)]
        block = ctx.enter_context(nc.Block())

        @block.sync
        def _(sp):
            def load(e, i):
                sp.dma_start(w1[i][:], W1[bass.ds(e, 1), :, :].rearrange("a (k p) h -> p (a k) h", p=P)).then_inc(arrived[i], 16)
                sp.dma_start(w2[i][:], W2[bass.ds(e, 1), :, :].rearrange("a (k p) d -> p (a k) d", p=P)).then_inc(arrived[i], 16)
                with nc.allow_non_contiguous_dma(reason="biases, one element to a partition"):
                    sp.dma_start(bias1[i][:], b1[bass.ds(e, 1), :].rearrange("a (k p) -> p (a k)", p=P)).then_inc(arrived[i], 16)

            load(0, 0)
            sp.dma_start(b2_rows[:], b2.unsqueeze(0).to_broadcast([P, n_experts, D])).then_inc(b2_in, 16)
            load(1, 1)
            with sp.Fori(0, n_experts // 2 - 1) as o:
                for i in range(2):
                    sp.wait_ge(down_done, 1 + o * (STEPS * U) + (i + 1) * (OUT * U))
                    load(o * 2 + 2 + i, i)
            for scatter in beside:
                scatter.finish(sp)

        if beside:
            @block.gpsimd
            def _(pool):
                for scatter in beside:
                    scatter.run(pool)

        @block.tensor
        def _(pe):
            pe.sem_inc(down_done, 1)
            with pe.Fori(0, n_experts // 2) as o:
                def down_step(s):
                    pe.wait_ge(hid_ready, 1 + o * (STEPS * KH) + (s + 1) * KH)
                    for j in range(U):
                        r = s * U + j
                        pe.wait_ge(added, 1 + o * (STEPS * U) + max(r - 3, 0))
                        for k in range(KH):
                            ins = nc.tensor.matmul(down[r % 4][:, 0:D],
                                                   hid[s % 2][:, k, :, :].rearrange("p a n -> p (a n)")[:, j * P:(j + 1) * P],
                                                   w2[s // OUT][:, k, :], start=(k == 0), stop=(k == KH - 1))
                        ins.then_inc(down_done, 1)

                for s in range(STEPS):
                    e, grp = s // OUT, s % OUT
                    if grp == 0:
                        pe.wait_ge(arrived[e], o * 48 + 48)
                    for m in range(KH):
                        q = s * KH + m
                        pe.wait_ge(hid_ready, 1 + o * (STEPS * KH) + max(q - 1, 0))
                        for k in range(KD):
                            for a in range(2):
                                col = grp * U * P + a * HALF
                                ins = nc.tensor.matmul(up[q % 2][:, a, 0:HALF], w1[e][:, k, m * P:(m + 1) * P],
                                                       S.xnT[:, k, col:col + HALF], start=(k == 0), stop=(k == KD - 1))
                        ins.then_inc(up_done, 1)
                    if s >= 1:
                        down_step(s - 1)
                down_step(STEPS - 1)

        @block.scalar
        def _(act):
            nc.scalar.preload_act_table(ACT.Gelu)
            act.sem_inc(hid_ready, 1)
            with act.Fori(0, n_experts // 2) as o:
                for s in range(STEPS):
                    act.wait_ge(down_done, 1 + o * (STEPS * U) + max(s - 1, 0) * U)
                    for m in range(KH):
                        act.wait_ge(up_done, o * (STEPS * KH) + s * KH + m + 1)
                        nc.scalar.activation(hid[s % 2][:, m, :, :], up[m % 2][:, :, 0:HALF], ACT.Gelu,
                                             bias=bias1[s // OUT][:, m:m + 1]).then_inc(hid_ready, 1)

        @block.vector
        def _(v):
            v.sem_inc(added, 1)
            v.wait_ge(b2_in, 16)
            with v.Fori(0, n_experts) as e:
                for t in range(NT):
                    nc.vector.scalar_tensor_tensor(S.x[:, t * D:(t + 1) * D], b2_rows[:, bass.ds(e, 1), :].rearrange("p a d -> p (a d)"),
                                                   gate[:, t, bass.ds(e, 1)], S.x[:, t * D:(t + 1) * D], ALU.mult, ALU.add)
                v.drain()
            with v.Fori(0, n_experts // 2) as o:
                for s in range(STEPS):
                    for j in range(U):
                        r, t = s * U + j, (s % OUT) * U + j
                        v.wait_ge(down_done, 1 + o * (STEPS * U) + r + 1)
                        nc.vector.scalar_tensor_tensor(S.x[:, t * D:(t + 1) * D], down[r % 4][:, 0:D],
                                                       gate[:, t, bass.ds(o * 2 + s // OUT, 1)], S.x[:, t * D:(t + 1) * D],
                                                       ALU.mult, ALU.add).then_inc(added, 1)
                    if s % OUT == OUT - 1:
                        v.drain()


def choose_two(nc, v, S, score, n, first, second, tmp, top):
    for r, pick in enumerate((first, second)):
        nc.vector.tensor_reduce(top[:, :, r], score[:], AX.X, ALU.max)
        v.drain()
        nc.vector.tensor_tensor(pick[:], score[:], top[:, :, r:r + 1].to_broadcast([P, NT, n]), ALU.is_equal)
        v.drain()
        nc.vector.tensor_tensor(pick[:], pick[:], S.countdown[:, 0:n].unsqueeze(1).to_broadcast([P, NT, n]), ALU.mult)
        v.drain()
        nc.vector.tensor_reduce(tmp[:], pick[:], AX.X, ALU.max)
        v.drain()
        nc.vector.tensor_tensor(pick[:], pick[:], tmp[:].unsqueeze(2).to_broadcast([P, NT, n]), ALU.is_equal)
        v.drain()
        if r == 0:
            nc.vector.scalar_tensor_tensor(score[:], pick[:], -BIG, score[:], ALU.mult, ALU.add)
            v.drain()


def emit_top2_mask(nc, S):
    with ExitStack() as ctx:
        sb = lambda n, s, d: ctx.enter_context(nc.sbuf_tensor("t2" + n, s, d))
        first, second = sb("a", [P, NT, NE0], F32), sb("b", [P, NT, NE0], F32)
        tmp, top = sb("c", [P, NT], F32), sb("d", [P, NT, 2], F32)
        block = ctx.enter_context(nc.Block())

        @block.vector
        def _(v):
            choose_two(nc, v, S, S.gate0, NE0, first, second, tmp, top)
            nc.vector.tensor_tensor(S.gate0[:], first[:], second[:], ALU.add)
            v.drain()


def emit_batchnorm(nc, S, A):
    sem = S.sem
    loaded, summed, centred, squared, sq_summed, var_in, rooted = (sem("bn_" + n) for n in (
        "in", "sum", "cen", "sq", "sqsum", "var", "root"))
    LAST = N - (NT - 1) * P
    with ExitStack() as ctx:
        sb = lambda n, s, d: ctx.enter_context(nc.sbuf_tensor("bn" + n, s, d))
        gamma, beta, mean, root = (sb(n, [P, D], F32) for n in ("gamma", "beta", "mean", "root"))
        sq = sb("sq", [P, NT * D], F32)
        ps = [ctx.enter_context(nc.psum_tensor(f"bnps{i}", [P, 512], F32)) for i in range(2)]
        block = ctx.enter_context(nc.Block())

        @block.sync
        def _(sp):
            sp.dma_start(gamma[:], A["bn_gamma"].unsqueeze(0).to_broadcast([P, D])).then_inc(loaded, 16)
            sp.dma_start(beta[:], A["bn_beta"].unsqueeze(0).to_broadcast([P, D])).then_inc(loaded, 16)

        @block.tensor
        def _(pe):
            def sum_over_nodes(ps, a):
                for t in range(NT):
                    k = P if t < NT - 1 else LAST
                    ins = nc.tensor.matmul(ps[:, 0:D], S.ones[0:k, 0:P], a[0:k, t * D:(t + 1) * D],
                                           start=(t == 0), stop=(t == NT - 1))
                return ins

            sum_over_nodes(ps[0], S.agg).then_inc(summed, 1)
            pe.wait_ge(squared, 1)
            sum_over_nodes(ps[1], sq).then_inc(sq_summed, 1)

        @block.scalar
        def _(act):
            nc.scalar.preload_act_table(ACT.Sqrt)
            act.wait_ge(centred, 1)
            nc.scalar.activation(sq[:], S.agg[:], ACT.Square).then_inc(squared, 1)
            act.wait_ge(var_in, 1)
            nc.scalar.activation(root[:], root[:], ACT.Sqrt).then_inc(rooted, 1)

        @block.vector
        def _(v):
            agg3 = S.agg[:].rearrange("p (t d) -> p t d", d=D)
            x3 = S.x[:].rearrange("p (t d) -> p t d", d=D)
            bc = lambda row: row[:].unsqueeze(1).to_broadcast([P, NT, D])
            v.wait_ge(summed, 1)
            nc.vector.tensor_scalar(mean[:], ps[0][:, 0:D], 1.0 / N, None, ALU.mult)
            v.drain()
            nc.vector.tensor_tensor(agg3, agg3, bc(mean), ALU.subtract).then_inc(centred, 1)
            v.wait_ge(sq_summed, 1)
            nc.vector.tensor_scalar(root[:], ps[1][:, 0:D], 1.0 / N, LNEPS, ALU.mult, ALU.add).then_inc(var_in, 1)
            v.wait_ge(rooted, 1)
            nc.vector.reciprocal(root[:], root[:])
            v.drain()
            v.wait_ge(loaded, 32)
            nc.vector.tensor_tensor(root[:], root[:], gamma[:], ALU.mult)
            v.drain()
            nc.vector.tensor_tensor(agg3, agg3, bc(root), ALU.mult)
            v.drain()
            nc.vector.tensor_tensor(agg3, agg3, bc(beta), ALU.add)
            v.drain()
            nc.vector.scalar_tensor_tensor(S.x[:], S.agg[:], 0.0, S.x[:], ALU.max, ALU.add)
            v.drain()


class Scatter:

    def __init__(self, nc, S, tag, rec, rec_dram, first, last, rec_sb=None, stage=None):
        self.nc, self.rec, self.rec_dram, self.rec_sb = nc, rec, rec_dram, rec_sb
        self.first, self.last = first // 8, last // 8
        self.copied, self.back = S.sem(tag + "_copy"), S.sem(tag + "_back")
        self.put = [S.sem(f"{tag}_put{i}") for i in range(8)]
        self.slot = stage.enter_context(nc.sbuf_tensor(tag + "_slot", [P, 8, rec.shape[2]], I32))

    def run(self, pool):
        nc, slot, R = self.nc, self.slot, self.rec.shape[2] - 1

        def trip(o, is_first):
            for i in range(8):
                if not is_first:
                    pool.wait_ge(self.put[i], 16 * (o - self.first))
                count = pool.snap(o * 8 + (i + 1), min_val=1, max_val=self.last * 8)
                nc.gpsimd.tensor_copy(slot[:, i:i + 1, :], self.rec[:, bass.ds(count, 1), :]).then_inc(self.copied, 1)
                count = pool.snap(o * 8 + i + 1)
                pool.wait_ge(self.copied, 1)
                pool.wait_ge(self.copied, count)
                pool.indirect_dma_start(self.rec_dram, bass.IndirectOffsetOnAxis(ap=slot[:, i, 0:1], axis=0),
                                        slot[:, i, 1:R + 1], None).then_inc(self.put[i], 16)

        if self.first:
            pool.sem_inc(self.copied, self.first * 8)
        with pool.Fori(self.first, self.first + 1) as o:
            trip(o, True)
        with pool.Fori(self.first + 1, self.last) as o:
            trip(o, False)

    def finish(self, sp):
        for i in range(8):
            sp.wait_ge(self.put[i], 16 * (self.last - self.first))
        if self.rec_sb is not None:
            sp.dma_start(self.rec_sb[:], self.rec_dram.rearrange("(p c) r -> p c r", p=P)).then_inc(self.back, 16)
            sp.wait_ge(self.back, 16)


def emit_rank_edges(nc, S, tag, n_chunks, block, take, give, weight, slots, rec, rec_dram, ranges):
    sem = lambda n: S.sem(tag + n)
    R = 3 if weight is not None else 2
    GC, GS, GB = n_chunks, slots, block * P
    KB = -(-n_chunks // block) + 1
    loaded, filled, hots, ranked, tile_read, emptied = (sem("_" + n) for n in (
        "in", "fill", "hot", "rank", "read", "empty"))
    with ExitStack() as ctx:
        sb = lambda n, s, d: ctx.enter_context(nc.sbuf_tensor(tag + "_" + n, s, d))
        srci, dsti, tilei = (sb(n, [P, GC], I32) for n in ("src", "dst", "tile"))
        tilef, pos, incl, part, zero = (sb(n, [P, GC], F32) for n in ("tilef", "pos", "incl", "part", "zero"))
        hot = sb("hot", [P, NT, GC], BF16)
        trib, onesb = sb("trib", [P, P], BF16), sb("onesb", [P, P], BF16)
        blocks = sb("blocks", [P, 1], F32)
        base = sb("base", [P, 1], F32)
        cnt = sb("cnt", [P, 1], F32)
        starts, under = sb("starts", [P, KB], F32), sb("under", [P, KB], F32)
        row = sb("row", [P, NT + 1], F32)
        empty = sb("empty", [P, GS, R], I32)
        psr = ctx.enter_context(nc.psum_tensor(tag + "_psr", [P, 512], F32))
        pst = ctx.enter_context(nc.psum_tensor(tag + "_pst", [P, 512], F32))
        program = ctx.enter_context(nc.Block())

        @program.sync
        def _(sp):
            sp.dma_start(srci[:], take).then_inc(loaded, 16)
            sp.dma_start(dsti[:], give).then_inc(loaded, 16)
            sp.wait_ge(filled, 1)
            sp.dma_start(rec_dram.rearrange("(p c) r -> p c r", p=P), empty[:]).then_inc(emptied, 16)
            sp.wait_ge(emptied, 16)

        @program.gpsimd
        def _(pool):
            nc.gpsimd.memset(empty[:, :, 0:1], 0)
            if R == 3:
                nc.gpsimd.memset(empty[:, :, 2:3], 0)
            nc.gpsimd.memset(empty[:, :, 1:2], 2 * P).then_inc(filled, 1)

        @program.tensor
        def _(pe):
            pe.wait_ge(hots, 1)
            with pe.Fori(0, NT) as t:
                pe.wait_ge(tile_read, t + 1)
                nc.tensor.matmul(psr[:, 0:GC], trib[:], hot[:, bass.ds(t, 1), :].rearrange("p a c -> p (a c)"), start=True, stop=True)
                nc.tensor.matmul(pst[:, 0:GC], onesb[:], hot[:, bass.ds(t, 1), :].rearrange("p a c -> p (a c)"),
                                 start=True, stop=True).then_inc(ranked, 1)

        @program.vector
        def _(v):
            v.sem_inc(tile_read, 1)
            nc.vector.tensor_copy(trib[:], S.tri[:])
            nc.vector.tensor_copy(onesb[:], S.ones[:, 0:P])
            nc.vector.memset(zero[:], 0.0)
            nc.vector.memset(pos[:], 0.0)
            nc.vector.memset(blocks[:], 0.0)
            nc.vector.memset(row[:], 0.0)
            nc.vector.tensor_scalar(starts[:], S.iota[:, 0:KB], float(GB), None, ALU.mult)
            v.wait_ge(loaded, 32)
            nc.vector.tensor_scalar(tilei[:], dsti[:], 7, None, ALU.logical_shift_right)
            nc.vector.tensor_scalar(dsti[:], dsti[:], P - 1, None, ALU.bitwise_and)
            nc.vector.tensor_copy(rec[:, 1:GC + 1, 1], srci[:])
            if weight is not None:
                nc.vector.tensor_copy(rec[:, 1:GC + 1, 3].bitcast(F32), weight)
            v.drain()
            nc.vector.tensor_copy(tilef[:], tilei[:])
            nc.vector.tensor_copy(rec[:, 1:GC + 1, 2], dsti[:])
            v.drain()
            nc.vector.tensor_tensor(hot[:], tilef[:].unsqueeze(1).to_broadcast([P, NT, GC]),
                                    S.iota[:, 0:NT].unsqueeze(2).to_broadcast([P, NT, GC]), ALU.is_equal)
            v.drain().then_inc(hots, 1)
            with v.Fori(0, NT) as t:
                nc.vector.tensor_scalar(base[:], blocks[:], float(GB), None, ALU.mult)
                v.wait_ge(ranked, t + 1)
                nc.vector.tensor_tensor_scan(incl[:], pst[:, 0:GC], zero[:], 0.0, ALU.add, ALU.add)
                v.drain()
                nc.vector.tensor_tensor(part[:], incl[:], pst[:, 0:GC], ALU.subtract)
                nc.vector.tensor_scalar(under[:], starts[:], incl[:, GC - 1:GC], None, ALU.is_lt)
                v.drain()
                nc.vector.tensor_tensor(part[:], part[:], psr[:, 0:GC], ALU.add)
                nc.vector.tensor_reduce(cnt[:], under[:], AX.X, ALU.add)
                v.drain().then_inc(tile_read, 1)
                nc.vector.scalar_tensor_tensor(part[:], part[:], base[:, 0:1], hot[:, bass.ds(t, 1), :].rearrange("p a c -> p (a c)"),
                                               ALU.add, ALU.mult)
                nc.vector.tensor_scalar(cnt[:], cnt[:], 1.0, None, ALU.max)
                v.drain()
                nc.vector.tensor_tensor(pos[:], pos[:], part[:], ALU.add)
                nc.vector.tensor_tensor(blocks[:], blocks[:], cnt[:], ALU.add)
                v.drain()
                nc.vector.tensor_copy(row[:, bass.ds(t + 1, 1)], blocks[:])
            v.drain()
            nc.vector.tensor_copy(ranges[:], row[:])
            nc.vector.tensor_copy(tilei[:], pos[:])
            v.drain()
            nc.vector.tensor_scalar(dsti[:], tilei[:], P - 1, None, ALU.bitwise_and)
            nc.vector.tensor_scalar(srci[:], tilei[:], 7, None, ALU.logical_shift_right)
            v.drain()
            nc.vector.tensor_copy(part[:], dsti[:])
            nc.vector.tensor_copy(pos[:], srci[:])
            v.drain()
            nc.vector.scalar_tensor_tensor(part[:], part[:], float(GS), pos[:], ALU.mult, ALU.add)
            v.drain()
            nc.vector.tensor_copy(rec[:, 1:GC + 1, 0], part[:])
            v.drain()


def emit_routing(nc, S, A):
    sem = S.sem
    gathered = [sem(f"gt_g{i}") for i in range(BL)]
    indexed, kept, lanes, best, best_t, evac, vals = (sem("gt_" + n) for n in ("idx", "kept", "lanes", "best", "bestT", "evac", "vals"))
    masked, spread_done, maxed, end_read = (sem("gt_" + n) for n in ("msk", "spr", "mx", "endr"))
    cleared, hot, hot_t, hot_tc, ends, logit, expd, weighed, hot2, added, closed, closed_read = (sem("gt_" + n) for n in (
        "clear", "hot", "hotT", "hotTc", "ends", "logit", "exp", "w", "hot2", "agg", "closed", "clr"))
    loaded, var_in, rooted, dz, de = (sem("gt_" + n) for n in ("in", "var", "root", "dz", "de"))
    with ExitStack() as ctx:
        sb = lambda n, s, d: ctx.enter_context(nc.sbuf_tensor("gt_" + n, s, d))
        idx = sb("idx", [P, BL], I32)
        land = sb("land", [P, BL, GW], F32)
        rows = sb("rows", [P, GS, GW], F32)
        lane = sb("lane", [P, GS], F32)
        nb = sb("nb", [P, BL, P], BF16)
        spread_score = sb("spread", [P, BL, HEADS, P], F32)
        top = sb("top", [P, HEADS, P], F32)
        ms = sb("ms", [P, NT, HEADS], F32)
        val = sb("val", [P, NT, 2 * HEADS], F32)
        onehotb = sb("hotb", [P, BL, P], BF16)
        onehot = sb("hot", [P, BL, P], F32)
        onehot_t = sb("hotT", [P, BL, P], F32)
        z = sb("z", [P, GS + NT, HEADS], F32)
        z2 = sb("z2", [P, GS + NT, HEADS], F32)
        end = sb("end", [P, GS, 2 * HEADS], F32)
        sums = sb("sums", [P, NT, GW], F32)
        tmp = sb("tmp", [P, NT, HW], F32)
        mean, var = sb("mean", [P, NT], F32), sb("var", [P, NT], F32)
        b_gat, gamma, beta = (sb(n, [P, HW], F32) for n in ("bgat", "gamma", "beta"))
        first, second = sb("first", [P, NT, NE1], F32), sb("second", [P, NT, NE1], F32)
        topv = sb("topv", [P, NT, 2], F32)
        psB = ctx.enter_context(nc.psum_tensor("gt_psB", [P, 2, 1024], BF16))
        psT = ctx.enter_context(nc.psum_tensor("gt_psT", [P, BL, P], F32))
        psE = ctx.enter_context(nc.psum_tensor("gt_psE", [P, 2, 512], F32))
        psO = ctx.enter_context(nc.psum_tensor("gt_psO", [P, 512], F32))
        block = ctx.enter_context(nc.Block())
        zs = z[:, GS:GS + NT, :]
        own = S.gat_sb

        @block.sync
        def _(sp):
            for dst, name in ((b_gat, "b_gat"), (gamma, "ln_gamma"), (beta, "ln_beta")):
                sp.dma_start(dst[:], A[name].unsqueeze(0).to_broadcast([P, HW])).then_inc(loaded, 16)

        @block.gpsimd
        def _(pool):
            total = pool.value_load(S.granges[0:1, NT:NT + 1], min_val=0, max_val=GBLOCKS)
            with pool.Fori(0, total) as g:
                c = slot_of(nc, pool, g, GBLOCKS)
                for i in range(BL):
                    pool.wait_ge(kept, g * BL + i + 1)
                    nc.gpsimd.tensor_copy(idx[:, i:i + 1], S.rec_sb[:, bass.ds(c + i, 1), 0:1].rearrange("p a b -> p (a b)")
                                          ).then_inc(indexed, 1)
                    count = pool.snap(g * BL + i + 1)
                    pool.wait_ge(indexed, 1)
                    pool.wait_ge(indexed, count)
                    pool.indirect_dma_start(land[:, i, :], None, S.table_gat,
                                            bass.IndirectOffsetOnAxis(ap=idx[:, i:i + 1], axis=0)).then_inc(gathered[i], 16)

        @block.vector
        def _(v):
            nc.vector.memset(rows[:], 0.0)
            nc.vector.memset(end[:], 0.0)
            v.drain().then_inc(cleared, 1)
            v.sem_inc(hot_t, 2)
            v.sem_inc(added, BL)
            v.sem_inc(maxed, BL)
            v.sem_inc(end_read, 1)
            nc.vector.tensor_copy(lane[:], S.rec_sb[:, :, 1])
            v.drain()
            start = v.alloc_register("gt_start_v")
            v.reg_mov(start, 0)
            with v.Fori(0, NT) as t:
                g1 = v.value_load(S.granges[0:1, bass.ds(t + 1, 1)], min_val=0, max_val=GBLOCKS)
                nc.vector.memset(top[:], -BIG)
                v.drain()
                with v.Fori(start, g1) as g:
                    c = slot_of(nc, v, g, GBLOCKS)
                    v.drain()
                    v.wait_ge(spread_done, g * BL + BL + 1)
                    for i in range(BL):
                        nc.vector.tensor_scalar(nb[:, i, :], S.iotab[:], lane[:, bass.ds(c + i, 1)], -BIG, ALU.not_equal, ALU.mult
                                                ).then_inc(masked, 1)
                    for i in range(BL):
                        v.drain()
                        v.wait_ge(spread_done, g * BL + BL + i + 2)
                        k = SPREAD[i % 2]
                        for h in range(k, HEADS):
                            nc.vector.scalar_tensor_tensor(top[:, h, :], nb[:, i, :], rows[:, bass.ds(c + i, 1), HW + h:HW + h + 1].rearrange("p a b -> p (a b)"),
                                                           top[:, h, :], ALU.add, ALU.max)
                        nc.vector.tensor_tensor(top[:, 0:k, :], top[:, 0:k, :], spread_score[:, i, 0:k, :], ALU.max).then_inc(maxed, 1)
                v.reg_mov(start, g1)
                v.drain().then_inc(best, 1)
                v.wait_ge(best_t, t + 1)
                nc.vector.tensor_reduce(ms[:, bass.ds(t, 1), :], psT[:].unsqueeze(1), AX.X, ALU.max).then_inc(evac, 1)
            v.drain()
            src_own, dst_own = own[:, :, HW:HW + HEADS], own[:, :, GW:GW + HEADS]
            nc.vector.tensor_tensor(ms[:], ms[:], src_own, ALU.max)
            v.drain()
            nc.vector.tensor_tensor(ms[:], ms[:], dst_own, ALU.add)
            nc.vector.tensor_tensor(zs, src_own, dst_own, ALU.add)
            v.drain()
            nc.vector.tensor_copy(val[:, :, 0:HEADS], dst_own)
            nc.vector.scalar_tensor_tensor(val[:, :, HEADS:2 * HEADS], ms[:], 0.2, ms[:], ALU.mult, ALU.max)
            v.drain().then_inc(vals, 1)
            total = v.value_load(S.granges[0:1, NT:NT + 1], min_val=0, max_val=GBLOCKS)
            def one_hots(g):
                c = slot_of(nc, v, g, GBLOCKS)
                v.wait_ge(hot_t, 2 * g + 2)
                for i in range(BL):
                    nc.vector.tensor_scalar(onehotb[:, i, :], S.iotab[:], lane[:, bass.ds(c + i, 1)], None, ALU.is_equal
                                            ).then_inc(hot, 1)

            def keep_ends(g):
                c = slot_of(nc, v, g, GBLOCKS)
                v.wait_ge(ends, g + 1)
                nc.vector.tensor_copy(end[:, bass.ds(c, BL), :].rearrange("p (a i) k -> p a (i k)", a=2),
                                      psE[:, :, 0:BL * HEADS]).then_inc(end_read, 1)

            one_hots(0)
            with v.Fori(1, total) as g:
                one_hots(g)
                keep_ends(g - 1)
            with v.Fori(total - 1, total) as g:
                keep_ends(g)
            v.drain()
            nc.vector.tensor_tensor(z[:, 0:GS, :], rows[:, :, HW:GW], end[:, :, 0:HEADS], ALU.add)
            v.drain()
            nc.vector.scalar_tensor_tensor(z2[:], z[:], 0.2, z[:], ALU.mult, ALU.max)
            v.drain()
            nc.vector.tensor_tensor(z2[:, 0:GS, :], z2[:, 0:GS, :], end[:, :, HEADS:2 * HEADS], ALU.subtract)
            nc.vector.tensor_tensor(z2[:, GS:GS + NT, :], z2[:, GS:GS + NT, :], val[:, :, HEADS:2 * HEADS], ALU.subtract)
            v.drain()
            nc.vector.tensor_scalar(z2[:], z2[:], 0.0, None, ALU.min).then_inc(logit, 1)
            v.wait_ge(expd, 1)
            spread4 = z[:, 0:GS, :].unsqueeze(3).to_broadcast([P, GS, HEADS, HC])
            by_head = rows[:, :, 0:HW].rearrange("p i (h k) -> p i h k", h=HEADS)
            nc.vector.tensor_tensor(by_head, by_head, spread4, ALU.mult)
            nc.vector.tensor_copy(rows[:, :, HW:GW], z[:, 0:GS, :])
            v.drain().then_inc(weighed, 1)
            with v.Fori(0, total) as g:
                c = slot_of(nc, v, g, GBLOCKS)
                for i in range(BL):
                    v.wait_ge(added, g * BL + i + 1)
                    nc.vector.tensor_scalar(onehot[:, i, :], S.iota[:, 0:P], lane[:, bass.ds(c + i, 1)], None, ALU.is_equal
                                            ).then_inc(hot2, 1)
            v.wait_ge(closed_read, NT + 1)
            heads = lambda a: a.rearrange("p t (h k) -> p t h k", h=HEADS)
            spread = lambda a: a.unsqueeze(3).to_broadcast([P, NT, HEADS, HC])
            row = lambda r: r[:].unsqueeze(1).to_broadcast([P, NT, HW])
            nc.vector.tensor_tensor(heads(tmp[:]), heads(own[:, :, 0:HW]), spread(zs), ALU.mult)
            v.drain()
            nc.vector.tensor_tensor(zs, zs, sums[:, :, HW:GW], ALU.add)
            v.drain()
            nc.vector.tensor_tensor(tmp[:], tmp[:], sums[:, :, 0:HW], ALU.add)
            nc.vector.tensor_scalar(zs, zs, 1e-16, None, ALU.add)
            v.drain()
            nc.vector.reciprocal(zs, zs)
            v.drain()
            nc.vector.tensor_tensor(heads(tmp[:]), heads(tmp[:]), spread(zs), ALU.mult)
            v.drain()
            v.wait_ge(loaded, 48)
            nc.vector.tensor_tensor(tmp[:], tmp[:], row(b_gat), ALU.add)
            v.drain()
            nc.vector.tensor_reduce(mean[:], tmp[:], AX.X, ALU.add)
            v.drain()
            nc.vector.tensor_scalar(mean[:], mean[:], 1.0 / HW, None, ALU.mult)
            v.drain()
            nc.vector.tensor_tensor(tmp[:], tmp[:], mean[:].unsqueeze(2).to_broadcast([P, NT, HW]), ALU.subtract)
            v.drain()
            nc.vector.tensor_tensor(sums[:, :, 0:HW], tmp[:], tmp[:], ALU.mult)
            v.drain()
            nc.vector.tensor_reduce(var[:], sums[:, :, 0:HW], AX.X, ALU.add)
            v.drain()
            nc.vector.tensor_scalar(var[:], var[:], 1.0 / HW, LNEPS, ALU.mult, ALU.add).then_inc(var_in, 1)
            v.wait_ge(rooted, 1)
            nc.vector.reciprocal(var[:], var[:])
            v.drain()
            nc.vector.tensor_tensor(tmp[:], tmp[:], var[:].unsqueeze(2).to_broadcast([P, NT, HW]), ALU.mult)
            v.drain()
            nc.vector.tensor_tensor(tmp[:], tmp[:], row(gamma), ALU.mult)
            v.drain()
            nc.vector.tensor_tensor(tmp[:], tmp[:], row(beta), ALU.add)
            v.drain()
            nc.vector.tensor_reduce(S.gate1[:], tmp[:].rearrange("p t (h k) -> p t k h", h=HEADS), AX.X, ALU.add)
            v.drain()
            nc.vector.tensor_scalar(S.gate1[:], S.gate1[:], 1.0 / HEADS, None, ALU.mult)
            v.drain()
            choose_two(nc, v, S, S.gate1, NE1, first, second, mean, topv)
            nc.vector.tensor_tensor(topv[:, :, 1], topv[:, :, 1], topv[:, :, 0], ALU.subtract).then_inc(dz, 1)
            v.wait_ge(de, 1)
            nc.vector.tensor_scalar(topv[:, :, 0], topv[:, :, 1], 1.0, None, ALU.add)
            v.drain()
            nc.vector.reciprocal(topv[:, :, 0], topv[:, :, 0])
            v.drain()
            nc.vector.tensor_tensor(topv[:, :, 1], topv[:, :, 1], topv[:, :, 0], ALU.mult)
            v.drain()
            nc.vector.tensor_tensor(first[:], first[:], topv[:, :, 0:1].to_broadcast([P, NT, NE1]), ALU.mult)
            nc.vector.tensor_tensor(second[:], second[:], topv[:, :, 1:2].to_broadcast([P, NT, NE1]), ALU.mult)
            v.drain()
            nc.vector.tensor_tensor(S.gate1[:], first[:], second[:], ALU.add)
            v.drain()

        @block.scalar
        def _(act):
            nc.scalar.preload_act_table(ACT.Exp)
            total = act.value_load(S.granges[0:1, NT:NT + 1], min_val=0, max_val=GBLOCKS)
            act.sem_inc(kept, BL)
            act.sem_inc(spread_done, BL + 1)
            act.sem_inc(hot_tc, 2)
            act.sem_inc(closed_read, 1)
            act.wait_ge(cleared, 1)
            with act.Fori(0, total) as g:
                c = slot_of(nc, act, g, GBLOCKS)
                for i in range(BL):
                    act.wait_ge(gathered[i], g * 16 + 16)
                    nc.scalar.copy(rows[:, bass.ds(c + i, 1), :], land[:, i:i + 1, :]).then_inc(kept, 1)
                    act.drain()
                    act.wait_ge(masked, g * BL + i + 1)
                    act.wait_ge(maxed, g * BL + i + 1)
                    for h in range(SPREAD[i % 2]):
                        ins = nc.scalar.activation(spread_score[:, i, h:h + 1, :], nb[:, i:i + 1, :], ACT.Identity,
                                                   bias=rows[:, bass.ds(c + i, 1), HW + h:HW + h + 1].rearrange("p a b -> p (a b)"))
                    ins.then_inc(spread_done, 1)
            with act.Fori(0, total) as g:
                for a in range(2):
                    act.wait_ge(hot_t, 2 * g + a + 3)
                    nc.scalar.copy(onehot_t[:, 2 * a:2 * a + 2, :].rearrange("p i n -> p (i n)"), psB[:, a, 0:2 * P]).then_inc(hot_tc, 1)
            act.wait_ge(logit, 1)
            nc.scalar.activation(z[:], z2[:], ACT.Exp).then_inc(expd, 1)
            with act.Fori(0, NT) as t:
                act.wait_ge(closed, t + 1)
                nc.scalar.copy(sums[:, bass.ds(t, 1), :], psO[:, 0:GW].unsqueeze(1)).then_inc(closed_read, 1)
            act.wait_ge(var_in, 1)
            nc.scalar.activation(var[:], var[:], ACT.Sqrt).then_inc(rooted, 1)
            act.wait_ge(dz, 1)
            nc.scalar.activation(topv[:, :, 1], topv[:, :, 1], ACT.Exp).then_inc(de, 1)

        @block.tensor
        def _(pe):
            with pe.Fori(0, NT) as t:
                pe.wait_ge(best, t + 1)
                for h in range(HEADS):
                    ins = nc.tensor.transpose(psT[:, h, :], top[:, h, :], S.ident[:])
                ins.then_inc(best_t, 1)
            pe.wait_ge(vals, 1)
            start = pe.alloc_register("gt_start_pe")
            pe.reg_mov(start, 0)
            with pe.Fori(0, NT) as t:
                g1 = pe.value_load(S.granges[0:1, bass.ds(t + 1, 1)], min_val=0, max_val=GBLOCKS)
                with pe.Fori(start, g1) as g:
                    for a in range(2):
                        pe.wait_ge(hot, g * BL + 2 * a + 2)
                        pe.wait_ge(hot_tc, 2 * g + a + 1)
                        for i in range(2):
                            ins = nc.tensor.transpose(psB[:, a, i * P:(i + 1) * P], onehotb[:, 2 * a + i, :], S.identb[:])
                        ins.then_inc(hot_t, 1)
                    pe.wait_ge(end_read, g + 1)
                    for a in range(2):
                        pe.wait_ge(hot_tc, 2 * g + a + 3)
                        for i in range(2):
                            ins = nc.tensor.matmul(psE[:, a, i * 2 * HEADS:(i + 1) * 2 * HEADS], onehot_t[:, 2 * a + i, :],
                                                   val[:, bass.ds(t, 1), :].rearrange("p a k -> p (a k)"), start=True, stop=True)
                    ins.then_inc(ends, 1)
                pe.reg_mov(start, g1)
            pe.wait_ge(weighed, 1)
            pe.reg_mov(start, 0)
            with pe.Fori(0, NT) as t:
                g1 = pe.value_load(S.granges[0:1, bass.ds(t + 1, 1)], min_val=0, max_val=GBLOCKS)
                pe.wait_ge(closed_read, t + 1)
                nc.tensor.matmul(psO[:, 0:GW], S.zeros[0:1, 0:P], S.iota[0:1, 0:GW], start=True, stop=False)
                with pe.Fori(start, g1) as g:
                    c = slot_of(nc, pe, g, GBLOCKS)
                    for i in range(BL):
                        pe.wait_ge(hot2, g * BL + i + 1)
                        nc.tensor.matmul(psO[:, 0:GW], onehot[:, i, :], rows[:, bass.ds(c + i, 1), :].rearrange("p a k -> p (a k)"),
                                         start=False, stop=False).then_inc(added, 1)
                pe.reg_mov(start, g1)
                nc.tensor.matmul(psO[:, 0:GW], S.zeros[0:1, 0:P], S.iota[0:1, 0:GW], start=False, stop=True).then_inc(closed, 1)


class _Shared:
    pass


def build_kernel(nc, A, out):
    with ExitStack() as ctx:
        S = _Shared()
        taken = []

        def sem(name):
            taken.append(nc.alloc_semaphore(name=name))
            return taken[-1]

        def end_stage():
            nc.clear_and_free_semaphores(taken)
            nc.all_engine_barrier()
            taken.clear()

        S.sem = sem

        def sb(n, s, d, c=ctx):
            return c.enter_context(nc.sbuf_tensor("k_" + n, s, d))

        def dram(n, s, d):
            return nc.dram_tensor(n, s, d, kind="Internal").ap()

        S.x = sb("x", [P, NT * D], F32)
        S.iota = sb("iota", [P, NP], F32)
        S.lane = sb("lane", [P, 1], F32)
        S.ident, S.tri, S.zeros, S.ones = (sb(n, [P, P], F32) for n in ("ident", "tri", "zeros", "ones"))
        S.identb, S.iotab = sb("identb", [P, P], BF16), sb("iotab", [P, P], BF16)
        S.countdown = sb("countdown", [P, NE0], F32)
        S.src = sb("src", [P, NCP], I32)
        S.dstf, S.ew, S.score, S.srct = (sb(n, [P, NCP], F32) for n in ("dstf", "ew", "score", "srct"))
        S.ranges = sb("ranges", [P, NT], I32)
        S.granges = sb("granges", [P, NT + 1], I32)
        S.rec_sb = sb("rec", [P, GS, 2], I32)
        S.erec_sb = sb("erec", [P, ES, 3], I32)
        S.esource, S.elane, S.eweight = sb("esource", [P, ES], I32), sb("elane", [P, ES], F32), sb("eweight", [P, ES], F32)
        S.eranges = sb("eranges", [P, NT + 1], I32)
        S.gate0, S.gate1 = sb("gate0", [P, NT, NE0], F32), sb("gate1", [P, NT, NE1], F32)
        S.lane_row = dram("lane_row", [NC * P], BF16)
        recg = sb("recg", [P, GC + 1, 3], I32)
        rec_dram = dram("records", [P * GS, 2], I32)
        erec_dram = dram("erecords", [P * ES, 3], I32)
        table = dram("table", [NP, TW], F32)
        S.table_gat = dram("table_gat", [NP, GW], F32)

        with ExitStack() as stage:
            S.table_sb = sb("tbl0", [P, NT, TW], F32, stage)
            S.w_aug = sb("w_aug", [P, KD, D + 4], F32, stage)
            S.bn_row = sb("bn_row", [P, D], F32, stage)
            S.we_attn, S.bias_attn = sb("we_attn", [P, 1], F32, stage), sb("bias_attn", [P, 1], F32, stage)
            S.hs = sb("hs", [P, NT], F32, stage)
            S.src_tile = sb("src_tile", [P, NC, NT], BF16, stage)
            emit_setup(nc, S, A)

            def rows_and_score(v, o, i, ps):
                nc.vector.tensor_tensor(S.table_sb[:, bass.ds(o * U + i, 1), 0:D], ps[:, 0:D].unsqueeze(1),
                                        S.bn_row[:].unsqueeze(1), ALU.add)
                nc.vector.tensor_copy(S.hs[:, bass.ds(o * U + i, 1)], ps[:, D:D + 1])

            emit_layernorm_project(nc, S, "l0", S.w_aug, D + 1, False, rows_and_score, table, S.table_sb)
            emit_rank_edges(nc, S, "so", GC, BL, A["gsrc"], A["gdst"], None, GS, recg, rec_dram, S.granges)
            emit_edge_scores(nc, S, A, Scatter(nc, S, "sa", recg, rec_dram, 0, EARLY, stage=stage))
        emit_aggregate(nc, S, "a0", table, True)
        end_stage()

        with ExitStack() as stage:
            rece = sb("rece", [P, NC + 1, 4], I32, stage)
            emit_rank_edges(nc, S, "se", NC, BG, A["dst_pc"][:, 0:NC], A["src_pc"][:, 0:NC], S.ew[:, 0:NC], ES, rece, erec_dram,
                            S.eranges)
            S.xnT = sb("xnT0", [P, KD, NP], F32, stage)
            wg = sb("wg", [P, KD, NE0], F32, stage)
            bg = sb("bg", [P, NE0], F32, stage)
            wg_in = S.sem("wg_in")

            def load_gate(v):
                v.wait_ge(wg_in, 32)

            with nc.Block() as block:
                @block.sync
                def _(sp):
                    sp.dma_start(wg[:], A["Wg"].rearrange("(k p) e -> p k e", p=P)).then_inc(wg_in, 16)
                    sp.dma_start(bg[:], A["bg"].unsqueeze(0).to_broadcast([P, NE0])).then_inc(wg_in, 16)
                    sp.wait_ge(wg_in, 32)

            def gate_scores(v, o, i, ps):
                nc.vector.tensor_tensor(S.gate0[:, bass.ds(o * U + i, 1), :], ps.unsqueeze(1), bg[:].unsqueeze(1), ALU.add)

            emit_layernorm_project(nc, S, "l1", wg, NE0, True, gate_scores)
            emit_top2_mask(nc, S)
            beside = (Scatter(nc, S, "sb", recg, rec_dram, EARLY, GC, S.rec_sb, stage),
                      Scatter(nc, S, "sc", rece, erec_dram, 0, NC, S.erec_sb, stage))
            emit_experts(nc, S, "f0", A, NE0, S.gate0, beside)
        end_stage()

        with ExitStack() as stage:
            w_in = S.sem("w1_in")
            with ExitStack() as inner:
                S.table_sb = sb("tbl1", [P, NT, TW], F32, inner)
                w = sb("w_gcn", [P, KD, D], F32, inner)
                with nc.Block() as block:
                    @block.sync
                    def _(sp):
                        sp.dma_start(w[:], A["gcn_W"].rearrange("(k p) o -> p k o", p=P)).then_inc(w_in, 16)
                        sp.wait_ge(w_in, 16)

                    @block.vector
                    def _(v):
                        nc.vector.memset(S.table_sb[:, :, D:TW], 0.0)
                        nc.vector.tensor_copy(S.esource[:], S.erec_sb[:, :, 0])
                        nc.vector.tensor_copy(S.elane[:], S.erec_sb[:, :, 1])
                        nc.vector.tensor_copy(S.eweight[:], S.erec_sb[:, :, 2].bitcast(F32))
                        v.drain()

                def rows(v, o, i, ps):
                    nc.vector.tensor_copy(S.table_sb[:, bass.ds(o * U + i, 1), 0:D], ps.unsqueeze(1))

                emit_layernorm_project(nc, S, "l2", w, D, False, rows, table, S.table_sb)
            S.agg = sb("agg", [P, NT * D], F32, stage)
            S.bias_row = sb("bias_row", [P, D], F32, stage)
            bias_in = S.sem("bias_in")
            with nc.Block() as block:
                @block.sync
                def _(sp):
                    sp.dma_start(S.bias_row[:], A["gcn_bias"].unsqueeze(0).to_broadcast([P, D])).then_inc(bias_in, 16)
                    sp.wait_ge(bias_in, 16)
            emit_aggregate(nc, S, "a1", table, False)
            emit_batchnorm(nc, S, A)
        end_stage()

        with ExitStack() as stage:
            S.xnT = sb("xnT1", [P, KD, NP], F32, stage)
            with ExitStack() as inner:
                S.gat_sb = sb("gat", [P, NT, GW + HEADS], F32, inner)
                wgat = sb("wgat", [P, KD, HW], F32, inner)
                att = sb("att", [P, 2, HW], F32, inner)
                wgat_in = S.sem("wgat_in")
                with nc.Block() as block:
                    @block.sync
                    def _(sp):
                        sp.dma_start(wgat[:], A["W_gat"].rearrange("(k p) o -> p k o", p=P)).then_inc(wgat_in, 16)
                        sp.dma_start(att[:, 0, :], A["att_src"].unsqueeze(0).to_broadcast([P, HW])).then_inc(wgat_in, 16)
                        sp.dma_start(att[:, 1, :], A["att_dst"].unsqueeze(0).to_broadcast([P, HW])).then_inc(wgat_in, 16)
                        sp.wait_ge(wgat_in, 48)

                def rows(v, o, i, ps):
                    nc.vector.tensor_copy(S.gat_sb[:, bass.ds(o * U + i, 1), 0:HW], ps.unsqueeze(1))

                emit_layernorm_project(nc, S, "l3", wgat, HW, True, rows)
                prod = sb("prod", [P, NT, HW], F32, inner)
                tabled = S.sem("gat_tabled")
                stored = S.sem("gat_stored")
                with nc.Block() as block:
                    @block.vector
                    def _(v):
                        for k in range(2):
                            nc.vector.tensor_tensor(prod[:], S.gat_sb[:, :, 0:HW], att[:, k, :].unsqueeze(1).to_broadcast([P, NT, HW]), ALU.mult)
                            v.drain()
                            nc.vector.tensor_reduce(S.gat_sb[:, :, HW + k * HEADS:HW + (k + 1) * HEADS],
                                                    prod[:].rearrange("p t (h k) -> p t h k", h=HEADS), AX.X, ALU.add)
                            v.drain()
                        v.drain().then_inc(tabled, 1)

                    @block.sync
                    def _(sp):
                        sp.wait_ge(tabled, 1)
                        sp.dma_start(S.table_gat.rearrange("(t p) d -> p t d", p=P), S.gat_sb[:, :, 0:GW]).then_inc(stored, 16)
                        sp.wait_ge(stored, 16)
                emit_routing(nc, S, A)
            emit_experts(nc, S, "f1", A, NE1, S.gate1)

        done = S.sem("out_done")
        with nc.Block() as block:
            @block.sync
            def _(sp):
                rows = (NT - 1) * P
                x3 = S.x[:].rearrange("p (t d) -> p t d", d=D)
                sp.dma_start(out[0:rows, :].rearrange("(t p) d -> p t d", p=P), x3[:, 0:NT - 1, :]).then_inc(done, 16)
                sp.dma_start(out[rows:N, :], x3[0:N - rows, NT - 1, :]).then_inc(done, 16)
                sp.wait_ge(done, 32)
        end_stage()


def kernel(x, src, dst, edge_attr_128, edge_weight, L0_gnn_Wn, L0_gnn_bn, L0_gnn_We, L0_gnn_be, L0_gnn_attn, L0_ffn_Wg,
           L0_ffn_bg, L0_ffn_W1, L0_ffn_b1, L0_ffn_W2, L0_ffn_b2, L1_gnn_W, L1_gnn_bias, L1_gnn_gamma, L1_gnn_beta,
           L1_ffn_W_gat, L1_ffn_att_src, L1_ffn_att_dst, L1_ffn_b_gat, L1_ffn_ln_gamma, L1_ffn_ln_beta, L1_ffn_W1,
           L1_ffn_b1, L1_ffn_W2, L1_ffn_b2, L1_ffn_edge_index):
    import concourse.bacc as bacc
    from concourse.bass_utils import run_bass_kernel_spmd

    def padded(a, rows, value):
        a = np.asarray(a)
        return np.concatenate([a, np.full((rows - a.shape[0],) + a.shape[1:], value, a.dtype)])

    def chunks(a, n_chunks, value=0):
        return np.ascontiguousarray(padded(a, n_chunks * P, value).reshape(n_chunks, P).T)

    ge = np.asarray(L1_ffn_edge_index)
    arrays = {
        "x": padded(x, NP, 0), "src_pc": chunks(src, NCP), "dst_pc": chunks(dst, NCP, NP - 1),
        "src_pj": padded(src, NC * P, 0).reshape(P, NC), "ew_pc": chunks(edge_weight, NCP),
        "eaT": np.ascontiguousarray(padded(edge_attr_128, NC * P, 0).T),
        "Wn": L0_gnn_Wn, "WnT": np.ascontiguousarray(np.asarray(L0_gnn_Wn).T), "We": L0_gnn_We, "bn": L0_gnn_bn,
        "be": L0_gnn_be, "attn": np.asarray(L0_gnn_attn).reshape(-1),
        "Wg": L0_ffn_Wg, "bg": L0_ffn_bg, "f0_W1": L0_ffn_W1, "f0_b1": L0_ffn_b1, "f0_W2": L0_ffn_W2, "f0_b2": L0_ffn_b2,
        "gcn_W": L1_gnn_W, "gcn_bias": L1_gnn_bias, "bn_gamma": L1_gnn_gamma, "bn_beta": L1_gnn_beta,
        "W_gat": L1_ffn_W_gat, "att_src": np.asarray(L1_ffn_att_src).reshape(-1),
        "att_dst": np.asarray(L1_ffn_att_dst).reshape(-1), "b_gat": L1_ffn_b_gat, "ln_gamma": L1_ffn_ln_gamma,
        "ln_beta": L1_ffn_ln_beta, "f1_W1": L1_ffn_W1, "f1_b1": L1_ffn_b1, "f1_W2": L1_ffn_W2, "f1_b2": L1_ffn_b2,
        "gsrc": chunks(ge[0], GC), "gdst": chunks(ge[1], GC),
    }
    arrays = {"in_" + k: np.ascontiguousarray(v) for k, v in arrays.items()}
    nc = bacc.Bacc("TRN2", target_bir_lowering=False, num_devices=1)
    aps = {k[3:]: nc.dram_tensor(k, v.shape, mybir.dt.from_np(v.dtype), kind="ExternalInput").ap()
           for k, v in arrays.items()}
    out = nc.dram_tensor("out_x", (N, D), F32, kind="ExternalOutput").ap()
    build_kernel(nc, aps, out)
    r = run_bass_kernel_spmd(nc, [arrays], core_ids=[0])
    return r.results[0]["out_x"]
```

```python
from contextlib import ExitStack

import concourse.bass as bass
import concourse.mybir as mybir
import numpy as np

F32, BF16, I32, U32 = mybir.dt.float32, mybir.dt.bfloat16, mybir.dt.int32, mybir.dt.uint32
ALU = mybir.AluOpType
ACT = mybir.ActivationFunctionType
AX = mybir.AxisListType

P = 128
N = 3125
NT = -(-N // P)
NP = NT * P
D = 256
KD = D // P
U = 5
SLOTS = 4
OUT = NT // U
E = 53125
NC = -(-E // P)
BL = 4
BG = 6
NCP = NC + BG
RING = 4
KB = -(-NC // BG) + 1
ED = 128
PIECE = 26
NPIECE = NC // PIECE
BIG = 1.0e30
LNEPS = 1e-5
TW = 260
H0 = 512
KH = H0 // P
NE0, NE1 = 8, 4
GE = 32768
GC = GE // P
GBLOCKS = GE // (BL * P) + NT
GS = GBLOCKS * BL
EBLOCKS = NC // BG + 1 + NT
ES = EBLOCKS * BG
PACK = 512
EARLY = 176
HEADS, HC = 4, NE1
HW = HEADS * HC
GW = HW + HEADS


def emit_layernorm_project(nc, S, tag, w, n_out, keep_xT, sink, table=None, table_sb=None, before=None):
    sem, x = S.sem, S.x
    stats_ready, rstd_root = sem(tag + "_stats"), sem(tag + "_root")
    xn_ready, transposed = sem(tag + "_xn"), sem(tag + "_tp")
    xt_ready, projected, sunk, stored = sem(tag + "_xt"), sem(tag + "_pj"), sem(tag + "_sunk"), sem(tag + "_st")
    with ExitStack() as ctx:
        sb = lambda n, s, d: ctx.enter_context(nc.sbuf_tensor(tag + n, s, d))
        st = sb("st", [P, U, 6], F32)
        mv = sb("mv", [P, U, 2], F32)
        root = sb("root", [P, U], F32)
        xn = sb("xn", [P, U, D], F32)
        xT = sb("xT", [P, U, D], F32)
        tp = ctx.enter_context(nc.psum_tensor(tag + "tp", [P, SLOTS, 512], F32))
        pj = ctx.enter_context(nc.psum_tensor(tag + "pj", [P, SLOTS, 512], F32))
        block = ctx.enter_context(nc.Block())

        @block.vector
        def _(v):
            if before is not None:
                before(v)
            v.sem_inc(sunk, U)
            with v.Fori(0, OUT) as o:
                for i in range(U):
                    nc.vector.bn_stats(st[:, i, :], x[:, bass.ds(o * (U * D) + i * D, D)])
                v.drain()
                for i in range(U):
                    nc.vector.bn_aggr(mv[:, i, :], st[:, i, :])
                v.drain()
                nc.vector.tensor_scalar(root[:], mv[:, :, 1], LNEPS, None, ALU.add).then_inc(stats_ready, 1)
                v.wait_ge(rstd_root, o + 1)
                nc.vector.reciprocal(root[:], root[:])
                v.drain()
                v.wait_ge(transposed, (o + 1) * U)
                for i in range(U):
                    nc.vector.tensor_scalar(xn[:, i, :], x[:, bass.ds(o * (U * D) + i * D, D)], mv[:, i, 0:1],
                                            root[:, i:i + 1], ALU.subtract, ALU.mult).then_inc(xn_ready, 1)
                for i in range(U):
                    v.wait_ge(projected, (o + 1) * U + i + 1)
                    sink(v, o, i, pj[:, i % SLOTS, 0:n_out])
                    v.drain().then_inc(sunk, 1)

        @block.scalar
        def _(act):
            nc.scalar.preload_act_table(ACT.Sqrt)
            act.sem_inc(xt_ready, U)
            with act.Fori(0, OUT) as o:
                act.wait_ge(stats_ready, o + 1)
                nc.scalar.activation(root[:], root[:], ACT.Sqrt).then_inc(rstd_root, 1)
                act.wait_ge(projected, (o + 1) * U)
                for i in range(U):
                    act.wait_ge(transposed, (o + 1) * U + i + 1)
                    ins = nc.scalar.copy(xT[:, i, :], tp[:, i % SLOTS, 0:D])
                    if keep_xT:
                        ins = nc.scalar.copy(S.xnT[:, :, bass.ds(o * (U * P) + i * P, P)],
                                             tp[:, i % SLOTS, 0:D].rearrange("p (k n) -> p k n", k=KD))
                    ins.then_inc(xt_ready, 1)

        @block.tensor
        def _(pe):
            for each in (transposed, projected):
                pe.sem_inc(each, U)
            with pe.Fori(0, OUT) as o:
                pe.wait_ge(xt_ready, (o + 1) * U)
                for i in range(U):
                    if i >= SLOTS:
                        pe.wait_ge(xt_ready, (o + 1) * U + i - SLOTS + 1)
                    pe.wait_ge(xn_ready, o * U + i + 1)
                    for k in range(KD):
                        ins = nc.tensor.transpose(tp[:, i % SLOTS, k * P:(k + 1) * P], xn[:, i, k * P:(k + 1) * P], S.ident[:])
                    ins.then_inc(transposed, 1)
                pe.wait_ge(sunk, (o + 1) * U)
                for i in range(U):
                    if i >= SLOTS:
                        pe.wait_ge(sunk, (o + 1) * U + i - SLOTS + 1)
                    pe.wait_ge(xt_ready, (o + 1) * U + i + 1)
                    for k in range(KD):
                        ins = nc.tensor.matmul(pj[:, i % SLOTS, 0:n_out], xT[:, i, k * P:(k + 1) * P], w[:, k, 0:n_out],
                                               start=(k == 0), stop=(k == KD - 1))
                    ins.then_inc(projected, 1)

        if table is not None:
            @block.sync
            def _(sp):
                rows = table.rearrange("(t p) d -> p t d", p=P)
                width = table.shape[1]
                with sp.Fori(0, OUT) as o:
                    sp.wait_ge(sunk, (o + 2) * U)
                    sp.dma_start(rows[:, bass.ds(o * U, U), :],
                                 table_sb[:, bass.ds(o * U, U), :]).then_inc(stored, 16)
                sp.wait_ge(stored, 16 * OUT)


def emit_setup(nc, S, A):
    sem = S.sem
    made, loaded, tables, wide, prods, dve1, cols, small = (sem("su_" + n) for n in (
        "made", "loaded", "tables", "wide", "prods", "dve1", "cols", "small"))
    laned = sem("su_laned")
    with ExitStack() as ctx:
        sb = lambda n, s, d: ctx.enter_context(nc.sbuf_tensor("su_" + n, s, d))
        wn = sb("wn", [P, KD, D], F32)
        we = sb("we", [P, KD, ED], F32)
        attn = sb("attn", [P, KD], F32)
        attn_wide = sb("attnw", [P, KD, P], F32)
        bsum = sb("bsum", [P, KD], F32)
        be = sb("be", [P, KD], F32)
        dsti = sb("dsti", [P, NCP], I32)
        tilei = sb("tilei", [P, NCP], I32)
        span = sb("span", [P, 2, NC], F32)
        spanmax = sb("spanmax", [P, 2, NC], F32)
        has = sb("has", [P, 2, NC], F32)
        key = sb("key", [P, 2, NC], F32)
        ends = sb("ends", [P, 2], F32)
        cnt = sb("cnt", [P, 2], F32)
        starts = sb("starts", [P, KB], F32)
        word = sb("word", [P, NT], F32)
        spj = sb("spj", [P, NC], I32)
        lane = sb("lane", [P, NC], BF16)
        ps = ctx.enter_context(nc.psum_tensor("su_ps", [P, 512], F32))
        block = ctx.enter_context(nc.Block())

        @block.gpsimd
        def _(pool):
            nc.gpsimd.iota(S.iota[:], [[1, NP]], base=0, channel_multiplier=0,
                           allow_small_or_imprecise_dtypes=True).then_inc(made, 1)
            nc.gpsimd.iota(S.lane[:], [[1, 1]], base=0, channel_multiplier=1,
                           allow_small_or_imprecise_dtypes=True).then_inc(made, 1)
            pool.wait_ge(tables, 2)
            nc.gpsimd.partition_all_reduce(spanmax[:].rearrange("p a c -> p (a c)"),
                                           span[:].rearrange("p a c -> p (a c)"), P, bass.bass_isa.ReduceOp.max).then_inc(wide, 1)

        @block.sync
        def _(sp):
            for dst, src in ((dsti[:], A["dst_pc"]), (S.src[:], A["src_pc"]), (spj[:], A["src_pj"]),
                             (attn[:], A["attn"].rearrange("(k p) -> p k", p=P)), (bsum[:], A["bn"].rearrange("(k p) -> p k", p=P)),
                             (be[:], A["be"].rearrange("(k p) -> p k", p=P)),
                             (wn[:], A["Wn"].rearrange("(k p) i -> p k i", p=P)), (we[:], A["We"].rearrange("(k p) i -> p k i", p=P)),
                             (S.w_aug[:, :, 0:D], A["WnT"].rearrange("(k p) o -> p k o", p=P)),
                             (S.bn_row[:], A["bn"].rearrange("(a d) -> a d", a=1).to_broadcast([P, D])),
                             (S.x[:].rearrange("p (t d) -> p t d", d=D), A["x"].rearrange("(t p) d -> p t d", p=P)),
                             (S.ew[:], A["ew_pc"])):
                with nc.allow_non_contiguous_dma(reason="a few vectors, one element to a partition"):
                    sp.dma_start(dst, src).then_inc(loaded, 16)
            sp.wait_ge(laned, 1)
            sp.dma_start(S.lane_row.rearrange("(p j) -> p j", p=P), lane[:]).then_inc(loaded, 16)
            sp.wait_ge(loaded, 16 * 13)

        @block.vector
        def _(v):
            v.wait_ge(made, 2)
            nc.vector.tensor_scalar(S.ident[:], S.iota[:, 0:P], S.lane[:, 0:1], None, ALU.is_equal)
            nc.vector.tensor_scalar(S.identb[:], S.iota[:, 0:P], S.lane[:, 0:1], None, ALU.is_equal)
            nc.vector.tensor_scalar(S.tri[:], S.iota[:, 0:P], S.lane[:, 0:1], None, ALU.is_gt)
            nc.vector.tensor_copy(S.iotab[:], S.iota[:, 0:P])
            nc.vector.memset(S.zeros[:], 0.0)
            nc.vector.memset(S.ones[:], 1.0)
            nc.vector.memset(S.table_sb[:], 1.0)
            nc.vector.tensor_scalar(S.countdown[:], S.iota[:, 0:NE0], -1.0, float(NE0), ALU.mult, ALU.add)
            v.drain()
            v.wait_ge(loaded, 16 * 12)
            nc.vector.tensor_scalar(tilei[:], dsti[:], 7, None, ALU.logical_shift_right)
            nc.vector.tensor_copy(S.dstf[:], dsti[:])
            v.drain()
            nc.vector.tensor_copy(span[:, 0, :], tilei[:, 0:NC])
            v.drain()
            nc.vector.tensor_scalar(span[:, 1, :], span[:, 0, :], -1.0, None, ALU.mult)
            v.drain().then_inc(tables, 2)
            nc.vector.tensor_scalar(spj[:], spj[:], P - 1, None, ALU.bitwise_and)
            nc.vector.tensor_scalar(tilei[:], S.src[:], 7, None, ALU.logical_shift_right)
            v.drain()
            nc.vector.tensor_copy(lane[:], spj[:])
            nc.vector.tensor_copy(S.srct[:], tilei[:])
            v.drain().then_inc(laned, 1)
            nc.vector.tensor_tensor(S.src_tile[:], S.srct[:, 0:NC].unsqueeze(2).to_broadcast([P, NC, NT]),
                                    S.iota[:, 0:NT].unsqueeze(1).to_broadcast([P, NC, NT]), ALU.is_equal)
            nc.vector.tensor_tensor(bsum[:], bsum[:], be[:], ALU.add)
            for k in range(KD):
                nc.vector.tensor_scalar(attn_wide[:, k, :], S.ones[:, 0:P], attn[:, k:k + 1], None, ALU.mult)
            v.drain().then_inc(dve1, 1)
            v.wait_ge(prods, 1)
            nc.vector.tensor_copy(S.w_aug[:, :, D:D + 1], ps[:, 0:KD].unsqueeze(2))
            nc.vector.tensor_copy(S.we_attn[:], ps[:, 2:3])
            nc.vector.tensor_copy(S.bias_attn[:], ps[:, 3:4])
            v.wait_ge(wide, 1)
            nc.vector.tensor_scalar(has[:, 0, :], spanmax[:, 0, :], S.lane[:, 0:1], None, ALU.is_ge)
            nc.vector.tensor_scalar(has[:, 1, :], spanmax[:, 1, :], -1.0, S.lane[:, 0:1], ALU.mult, ALU.is_le)
            nc.vector.tensor_scalar(key[:, 0, :], S.iota[:, 0:NC], 1.0, None, ALU.add)
            nc.vector.tensor_scalar(key[:, 1, :], S.iota[:, 0:NC], -1.0, float(NC), ALU.mult, ALU.add)
            v.drain()
            nc.vector.tensor_tensor(has[:, 0, :], has[:, 0, :], has[:, 1, :], ALU.mult)
            v.drain()
            nc.vector.tensor_tensor(key[:], key[:], has[:, 0, :].unsqueeze(1).to_broadcast([P, 2, NC]), ALU.mult)
            v.drain()
            nc.vector.tensor_reduce(ends[:], key[:], AX.X, ALU.max)
            v.drain()
            nc.vector.tensor_scalar(starts[:], S.iota[:, 0:KB], float(BG), None, ALU.mult)
            nc.vector.tensor_scalar(cnt[:, 1:2], ends[:, 1:2], -1.0, float(NC), ALU.mult, ALU.add)
            v.drain()
            nc.vector.tensor_scalar(cnt[:, 1:2], cnt[:, 1:2], float(NC - BG), None, ALU.min)
            v.drain()
            nc.vector.tensor_tensor(cnt[:, 0:1], ends[:, 0:1], cnt[:, 1:2], ALU.subtract)
            v.drain()
            nc.vector.tensor_scalar(starts[:], starts[:], cnt[:, 0:1], None, ALU.is_lt)
            v.drain()
            nc.vector.tensor_reduce(cnt[:, 0:1], starts[:], AX.X, ALU.add)
            v.drain()
            nc.vector.tensor_scalar(cnt[:, 0:1], cnt[:, 0:1], 2.0, None, ALU.max)
            v.drain().then_inc(cols, 1)
            v.wait_ge(small, 1)
            nc.vector.tensor_scalar(word[0:1, :], ps[0:1, 8 + 1:8 + 1 + NT], float(PACK), None, ALU.mult)
            v.drain()
            nc.vector.tensor_tensor(word[0:1, :], word[0:1, :], ps[0:1, 8 + 32:8 + 32 + NT], ALU.add)
            v.drain()
            nc.vector.tensor_copy(S.ranges[0:1, :], word[0:1, :])
            v.drain()

        @block.tensor
        def _(pe):
            pe.wait_ge(dve1, 1)
            for i in range(KD):
                for k in range(KD):
                    nc.tensor.matmul(ps[:, i:i + 1], wn[:, k, i * P:(i + 1) * P], attn[:, k:k + 1],
                                     start=(k == 0), stop=(k == KD - 1))
            for k in range(KD):
                nc.tensor.matmul(ps[:, 2:3], we[:, k, :], attn[:, k:k + 1], start=(k == 0), stop=(k == KD - 1))
            for k in range(KD):
                ins = nc.tensor.matmul(ps[:, 3:4], attn_wide[:, k, :], bsum[:, k:k + 1],
                                       start=(k == 0), stop=(k == KD - 1))
            ins.then_inc(prods, 1)
            pe.wait_ge(cols, 1)
            nc.tensor.matmul(ps[0:1, 8:8 + 32], cnt[0:NT, 0:1], S.tri[0:NT, 0:32], start=True, stop=True)
            nc.tensor.matmul(ps[0:1, 8 + 32:8 + 64], cnt[0:NT, 1:2], S.ident[0:NT, 0:32],
                             start=True, stop=True).then_inc(small, 1)


def emit_edge_scores(nc, S, A, scatter):
    sem = S.sem
    arrived = [sem(f"es_in{i}") for i in range(2)]
    split, hot, mm, used, read = sem("es_split"), sem("es_hot"), sem("es_mm"), sem("es_used"), sem("es_read")
    HALF = PIECE // 2
    with ExitStack() as ctx:
        sb = lambda n, s, d: ctx.enter_context(nc.sbuf_tensor("es_" + n, s, d))
        ea = sb("ea", [P, 2, PIECE * P], F32)
        lane = sb("lane", [P, 2, PIECE * P], BF16)
        onehot = sb("hot", [P, 2, PIECE * P], BF16)
        parts = sb("parts", [P, 3, NT], BF16)
        rest = sb("rest", [P, 2, NT], F32)
        picked = sb("picked", [P, PIECE, NT], F32)
        ps = [ctx.enter_context(nc.psum_tensor(f"es_ps{i}", [P, 3, 512], F32)) for i in range(2)]
        block = ctx.enter_context(nc.Block())
        lane_row = S.lane_row.rearrange("(a n) -> a n", a=1)

        @block.sync
        def _(sp):
            with sp.Fori(0, NPIECE // 2) as o:
                for i in range(2):
                    sp.wait_ge(read, 2 * o + i + 1)
                    col = o * (2 * PIECE * P) + i * PIECE * P
                    sp.dma_start(ea[:, i, :], A["eaT"][:, bass.ds(col, PIECE * P)]).then_inc(arrived[i], 16)
                    sp.dma_start(lane[:, i, :], lane_row[:, bass.ds(col, PIECE * P)].to_broadcast([P, PIECE * P])
                                 ).then_inc(arrived[i], 16)

            scatter.finish(sp)

        @block.gpsimd
        def _(pool):
            scatter.run_copied(pool)

        @block.scalar
        def _(act):
            scatter.copy_records(act)

        @block.vector
        def _(v):
            nc.vector.tensor_copy(parts[:, 0, :], S.hs[:])
            v.drain()
            nc.vector.tensor_tensor(rest[:, 0, :], S.hs[:], parts[:, 0, :], ALU.subtract)
            v.drain()
            nc.vector.tensor_copy(parts[:, 1, :], rest[:, 0, :])
            v.drain()
            nc.vector.tensor_tensor(rest[:, 1, :], rest[:, 0, :], parts[:, 1, :], ALU.subtract)
            v.drain()
            nc.vector.tensor_copy(parts[:, 2, :], rest[:, 1, :])
            v.drain().then_inc(split, 1)
            v.sem_inc(read, 2)
            with v.Fori(0, NPIECE // 2) as o:
                for i in range(2):
                    v.wait_ge(arrived[i], 32 * o + 32)
                    nc.vector.tensor_scalar(onehot[:, i, :], lane[:, i, :], S.lane[:, 0:1], None, ALU.is_equal
                                            ).then_inc(hot, 1)
                    v.wait_ge(mm, 2 * o + i + 1)
                    c = o * (2 * PIECE) + i * PIECE
                    nc.vector.tensor_tensor(
                        picked[:].rearrange("p (a c) t -> p a (c t)", a=2), ps[i][:, 0:2, 0:HALF * NT],
                        S.src_tile[:, bass.ds(c, PIECE), :].rearrange("p (a c) t -> p a (c t)", a=2), ALU.mult)
                    v.drain()
                    nc.vector.tensor_reduce(S.score[:, bass.ds(c, PIECE)], picked[:], AX.X, ALU.add)
                    v.drain()
                    nc.vector.tensor_tensor(S.score[:, bass.ds(c, PIECE)], S.score[:, bass.ds(c, PIECE)],
                                            ps[i][:, 2, 0:PIECE], ALU.add)
                    v.drain().then_inc(read, 1)
            nc.vector.memset(S.score[:, NC:NCP], 0.0)
            nc.vector.tensor_scalar(S.score[:, 0:NC], S.score[:, 0:NC], S.bias_attn[:, 0:1], None, ALU.add)
            v.drain()
            nc.vector.tensor_scalar(picked[:, 0:17, :].rearrange("p c t -> p (c t)")[:, 0:NC], S.score[:, 0:NC], 0.01, None, ALU.mult)
            v.drain()
            nc.vector.tensor_tensor(S.score[:, 0:NC], S.score[:, 0:NC],
                                    picked[:, 0:17, :].rearrange("p c t -> p (c t)")[:, 0:NC], ALU.max)
            v.drain()

        @block.tensor
        def _(pe):
            pe.wait_ge(split, 1)
            with pe.Fori(0, NPIECE // 2) as o:
                for i in range(2):
                    pe.wait_ge(read, 2 * o + i + 1)
                    pe.wait_ge(arrived[i], 32 * o + 32)
                    for c in range(PIECE):
                        nc.tensor.matmul(ps[i][:, 2, c:c + 1], ea[:, i, c * P:(c + 1) * P], S.we_attn[:, 0:1],
                                         start=True, stop=True)
                    pe.wait_ge(hot, 2 * o + i + 1)
                    for c in range(PIECE):
                        for k in range(3):
                            ins = nc.tensor.matmul(ps[i][:, c // HALF, (c % HALF) * NT:(c % HALF + 1) * NT],
                                                   onehot[:, i, c * P:(c + 1) * P], parts[:, k, :],
                                                   start=(k == 0), stop=(k == 2))
                    ins.then_inc(mm, 1)


def tile_range(nc, eng, S, t):
    word = eng.value_load(S.ranges[0:1, bass.ds(t, 1)], min_val=2 * PACK, max_val=NT * KB * PACK)
    return eng.snap(word // PACK), eng.snap(word % PACK)


def chunk_of(nc, eng, g, g0, c0):
    return eng.snap(nc.s_assert_within(c0 + (g - g0) * BG, 0, NC, skip_runtime_bounds_check_because=
                                       "a tile's blocks end within a block of its last chunk"))


def slot_of(nc, eng, g, blocks, size=BL):
    return eng.snap(nc.s_assert_within(g * size, 0, (blocks - 1) * size, skip_runtime_bounds_check_because=
                                       "whole blocks of all tiles are at most so many"))


def emit_aggregate(nc, S, tag, table, softmax):
    sem = S.sem
    gathered = [sem(f"{tag}_g{i}") for i in range(BG)]
    indexed, agg_done, masked, weighed = sem(tag + "_idx"), sem(tag + "_agg"), sem(tag + "_msk"), sem(tag + "_w")
    best, best_t, negs, negs_w, closed, evac = (sem(f"{tag}_{n}") for n in ("best", "bestT", "negs", "negsW", "closed", "evac"))
    width = D + 1 if softmax else D
    with ExitStack() as ctx:
        sb = lambda n, s, d: ctx.enter_context(nc.sbuf_tensor(tag + n, s, d))
        idx = sb("idx", [P, BG], I32)
        rows = sb("rows", [P, BG, TW], F32)
        w = sb("w", [P, BG, P], F32)
        nb = sb("nb", [P, RING, BG, P], F32)
        ne = sb("ne", [P, BG, P], F32)
        mb = sb("mb", [P, BG, P], F32)
        top = sb("top", [P, BG // 2, P], F32)
        top1 = sb("top1", [P, P], F32)
        m = sb("m", [P, 1], F32)
        diag = sb("diag", [P, P], F32)
        negm = sb("negm", [P, P], F32)
        rden = sb("rden", [P, 1], F32)
        relu = sb("relu", [P, D], F32)
        ps = ctx.enter_context(nc.psum_tensor(tag + "ps", [P, 2 * 512], F32))
        psT = ctx.enter_context(nc.psum_tensor(tag + "psT", [P, 512], F32))
        psM = ctx.enter_context(nc.psum_tensor(tag + "psM", [P, 512], F32))
        block = ctx.enter_context(nc.Block())

        source = S.src if softmax else S.esource

        class Tiles:

            def __init__(self, eng, who):
                self.eng = eng
                self.start, self.stop, self.first = (eng.alloc_register(f"{tag}_{who}_{n}") for n in ("start", "stop", "first"))
                eng.reg_mov(self.stop, 0)

            def load(self, t):
                if softmax:
                    self.next, self.next_first = tile_range(nc, self.eng, S, t)
                else:
                    self.next = self.eng.value_load(S.eranges[0:1, bass.ds(t + 1, 1)], min_val=0, max_val=EBLOCKS)

            def step(self):
                self.eng.reg_mov(self.start, self.stop)
                self.eng.reg_mov(self.stop, self.next)
                if softmax:
                    self.eng.reg_mov(self.first, self.next_first)
                    self.block, self.at = self.eng.snap(self.start), self.eng.snap(self.first)

            def blocks(self):
                return self.eng.Fori(self.start, self.stop)

            def first_block(self):
                return self.eng.Fori(self.block, self.block + 1)

            def other_blocks(self):
                return self.eng.Fori(self.block + 1, self.stop)

            def chunk(self, g):
                if softmax:
                    return chunk_of(nc, self.eng, g, self.block, self.at)
                return slot_of(nc, self.eng, g, EBLOCKS, BG)

        def put_indices(act, g, c):
            for i in range(BG):
                act.wait_ge(agg_done, g * BG + i + 1)
                nc.scalar.copy(idx[:, i:i + 1], source[:, bass.ds(c + i, 1)]).then_inc(indexed, 1)

        @block.gpsimd
        def _(pool):
            if softmax:
                total = tile_range(nc, pool, S, NT - 1)[0]
            else:
                total = pool.value_load(S.eranges[0:1, NT:NT + 1], min_val=1, max_val=EBLOCKS)
            count = pool.alloc_register(tag + "_count")
            pool.reg_mov(count, 0)
            with pool.Fori(0, total) as g:
                for i in range(BG):
                    pool.reg_add(count, count, 1)
                    pool.wait_ge(indexed, 1)
                    pool.wait_ge(indexed, count)
                    pool.indirect_dma_start(rows[:, i, 0:TW], None, table,
                                            bass.IndirectOffsetOnAxis(ap=idx[:, i:i + 1], axis=0)).then_inc(gathered[i], 16)

        @block.tensor
        def _(pe):
            pe.sem_inc(agg_done, BG)
            tiles = Tiles(pe, "pe")

            def sum_of(t):
                return ps[:, bass.ds(t % 2 * 512, width)]

            def find_max(t):
                pe.wait_ge(best, t + 1)
                nc.tensor.transpose(psT[:, 0:P], top1[:], S.ident[:]).then_inc(best_t, 1)

            def spread_max(t):
                pe.wait_ge(negs, t + 1)
                nc.tensor.matmul(psM[:, 0:P], S.ones[:, 0:P], diag[:], start=True, stop=True).then_inc(negs_w, 1)

            def open_tile(t):
                tiles.load(t)
                tiles.step()
                pe.wait_ge(evac, t + 1)
                nc.tensor.matmul(sum_of(t), S.zeros[0:1, 0:P], S.iota[0:1, 0:width], start=True, stop=False)

            def add_blocks(t, blocks):
                with blocks as g:
                    for i in range(BG):
                        pe.wait_ge(gathered[i], g * 16 + 16)
                        pe.wait_ge(weighed, (g + RING - 1) * BG + i + 2)
                        nc.tensor.matmul(sum_of(t), w[:, i, :], rows[:, i, 0:width],
                                         start=False, stop=False).then_inc(agg_done, 1)

            def close_tile(t):
                nc.tensor.matmul(sum_of(t), S.zeros[0:1, 0:P], S.iota[0:1, 0:width],
                                 start=False, stop=True).then_inc(closed, 1)

            if softmax:
                find_max(0)
                spread_max(0)
                with pe.Fori(0, NT - 1) as t:
                    find_max(t + 1)
                    open_tile(t)
                    add_blocks(t, tiles.first_block())
                    spread_max(t + 1)
                    add_blocks(t, tiles.other_blocks())
                    close_tile(t)
                open_tile(NT - 1)
                add_blocks(NT - 1, tiles.blocks())
                close_tile(NT - 1)
            else:
                with pe.Fori(0, NT) as t:
                    open_tile(t)
                    add_blocks(t, tiles.blocks())
                    close_tile(t)

        if not softmax:
            @block.vector
            def _(v):
                v.sem_inc(weighed, (RING - 1) * BG + 1)
                v.sem_inc(evac, 2)
                tiles = Tiles(v, "v")
                with v.Fori(0, NT) as t:
                    tiles.load(t)
                    tiles.step()
                    with tiles.blocks() as g:
                        c = tiles.chunk(g)
                        for i in range(BG):
                            v.wait_ge(agg_done, g * BG + i + 1)
                            nc.vector.tensor_scalar(w[:, i, :], S.iota[:, 0:P], S.elane[:, bass.ds(c + i, 1)],
                                                    S.eweight[:, bass.ds(c + i, 1)], ALU.is_equal, ALU.mult).then_inc(weighed, 1)
                    v.wait_ge(closed, t + 1)
                    nc.vector.tensor_tensor(S.agg[:, bass.ds(t * D, D)], ps[:, bass.ds(t % 2 * 512, D)], S.bias_row[:], ALU.add
                                            ).then_inc(evac, 1)

            @block.scalar
            def _(act):
                total = act.value_load(S.eranges[0:1, NT:NT + 1], min_val=1, max_val=EBLOCKS)
                with act.Fori(0, total) as g:
                    put_indices(act, g, slot_of(nc, act, g, EBLOCKS, BG))
            return

        @block.vector
        def _(v):
            v.sem_inc(evac, 2)
            ahead, middle, tiles = Tiles(v, "scan"), Tiles(v, "mid"), Tiles(v, "v")

            def pass_on():
                tiles.next, tiles.next_first = middle.stop, middle.first
                tiles.step()
                middle.next, middle.next_first = ahead.stop, ahead.first
                middle.step()

            def mask(to, t, c, i):
                nc.vector.tensor_scalar(to[:, i, :], S.iota[:, bass.ds(t * P, P)], S.dstf[:, bass.ds(c + i, 1)], -BIG,
                                        ALU.not_equal, ALU.mult)

            def scan(t):
                ahead.load(t)
                ahead.step()
                nc.vector.memset(top[:], -BIG)
                v.drain()
                with ahead.blocks() as g:
                    c = ahead.chunk(g)
                    for i in range(BG):
                        mask(mb, t, c, i)
                    v.drain()
                    for i in range(BG):
                        if i == BG // 2:
                            v.drain()
                        nc.vector.scalar_tensor_tensor(top[:, i % (BG // 2), :], mb[:, i, :], S.score[:, bass.ds(c + i, 1)],
                                                       top[:, i % (BG // 2), :], ALU.add, ALU.max)
                    v.drain()
                nc.vector.tensor_reduce(top1[:], top[:].rearrange("p i n -> p n i"), AX.X, ALU.max).then_inc(best, 1)

            def negate_max(t):
                v.wait_ge(best_t, t + 1)
                nc.vector.tensor_reduce(m[:], psT[:, 0:P], AX.X, ALU.max)
                v.drain()
                nc.vector.tensor_scalar(m[:], m[:], -0.1 * BIG, -1.0, ALU.max, ALU.mult)
                v.drain()
                nc.vector.tensor_scalar(diag[:], S.ident[:], m[:, 0:1], None, ALU.mult).then_inc(negs, 1)

            def keep_max(t):
                v.wait_ge(negs_w, t + 1)
                nc.vector.tensor_copy(negm[:], psM[:, 0:P])
                v.drain()

            def mask_blocks(t, blocks):
                with blocks as g:
                    c = tiles.chunk(g)
                    nc.vector.tensor_tensor(ne[:], S.iota[:, bass.ds(t * P, P)].unsqueeze(1).to_broadcast([P, BG, P]),
                                            S.dstf[:, bass.ds(c, BG)].unsqueeze(2).to_broadcast([P, BG, P]), ALU.not_equal)
                    v.drain()
                    v.wait_ge(weighed, g * BG + 1)
                    nc.vector.scalar_tensor_tensor(nb[:, bass.ds(g % RING, 1), :, :].rearrange("p a i n -> p (a i) n"), ne[:], -BIG,
                                                   negm[:].unsqueeze(1).to_broadcast([P, BG, P]), ALU.mult, ALU.add
                                                   ).then_inc(masked, 1)
                    v.drain()

            def finish_tile(t, n):
                at = t % 2 * 512
                v.wait_ge(closed, n)
                nc.vector.tensor_scalar(rden[:], ps[:, bass.ds(at + D, 1)], 1e-16, None, ALU.add)
                v.drain()
                nc.vector.reciprocal(rden[:], rden[:])
                v.drain()
                nc.vector.tensor_scalar(relu[:], ps[:, bass.ds(at, D)], rden[:, 0:1], 0.0, ALU.mult, ALU.max).then_inc(evac, 1)
                v.drain()
                nc.vector.tensor_tensor(S.x[:, bass.ds(t * D, D)], S.x[:, bass.ds(t * D, D)], relu[:], ALU.add)

            scan(0)
            negate_max(0)
            middle.next, middle.next_first = ahead.stop, ahead.first
            middle.step()
            scan(1)
            pass_on()
            keep_max(0)
            mask_blocks(0, tiles.first_block())
            negate_max(1)
            mask_blocks(0, tiles.other_blocks())
            scan(2)
            with v.Fori(1, NT - 2) as t:
                pass_on()
                keep_max(t)
                mask_blocks(t, tiles.first_block())
                negate_max(t + 1)
                mask_blocks(t, tiles.other_blocks())
                finish_tile(t - 1, t)
                scan(t + 2)
            pass_on()
            keep_max(NT - 2)
            mask_blocks(NT - 2, tiles.first_block())
            negate_max(NT - 1)
            mask_blocks(NT - 2, tiles.other_blocks())
            finish_tile(NT - 3, NT - 2)
            pass_on()
            keep_max(NT - 1)
            mask_blocks(NT - 1, tiles.blocks())
            finish_tile(NT - 2, NT - 1)
            finish_tile(NT - 1, NT)
            v.drain()

        @block.scalar
        def _(act):
            nc.scalar.preload_act_table(ACT.Exp)
            act.sem_inc(weighed, (RING - 1) * BG + 1)
            tiles = Tiles(act, "act")
            with act.Fori(0, NT) as t:
                tiles.load(t)
                tiles.step()
                with tiles.blocks() as g:
                    c = tiles.chunk(g)
                    put_indices(act, g, c)
                    act.wait_ge(masked, g + 1)
                    for i in range(BG):
                        act.wait_ge(agg_done, g * BG + i + 1)
                        nc.scalar.activation(w[:, i, :], nb[:, bass.ds(g % RING, 1), i, :].rearrange("p a n -> p (a n)"), ACT.Exp, bias=S.score[:, bass.ds(c + i, 1)]).then_inc(weighed, 1)


def emit_experts(nc, S, tag, A, n_experts, gate, beside=()):
    sem = S.sem
    STEPS, HALF = 2 * OUT, U * P // 2
    arrived = [sem(f"{tag}_w{i}") for i in range(2)]
    up_done, hid_ready, down_done, added, b2_in = (sem(f"{tag}_{n}") for n in ("up", "hid", "down", "add", "b2"))
    W1, b1, W2, b2 = A[tag + "_W1"], A[tag + "_b1"], A[tag + "_W2"], A[tag + "_b2"]
    with ExitStack() as ctx:
        sb = lambda n, s, d: ctx.enter_context(nc.sbuf_tensor(tag + n, s, d))
        w1 = [sb(f"w1_{i}", [P, KD, H0], F32) for i in range(2)]
        w2 = [sb(f"w2_{i}", [P, KH, D], F32) for i in range(2)]
        bias1 = [sb(f"b1_{i}", [P, KH], F32) for i in range(2)]
        hid = [sb(f"hid{i}", [P, KH, 2, HALF], F32) for i in range(2)]
        b2_rows = sb("b2", [P, n_experts, D], F32)
        up = [ctx.enter_context(nc.psum_tensor(f"{tag}up{i}", [P, 2, 512], F32)) for i in range(2)]
        down = [ctx.enter_context(nc.psum_tensor(f"{tag}dn{i}", [P, 512], F32)) for i in range(4)]
        block = ctx.enter_context(nc.Block())

        @block.sync
        def _(sp):
            def load(e, i):
                sp.dma_start(w1[i][:], W1[bass.ds(e, 1), :, :].rearrange("a (k p) h -> p (a k) h", p=P)).then_inc(arrived[i], 16)
                sp.dma_start(w2[i][:], W2[bass.ds(e, 1), :, :].rearrange("a (k p) d -> p (a k) d", p=P)).then_inc(arrived[i], 16)
                with nc.allow_non_contiguous_dma(reason="biases, one element to a partition"):
                    sp.dma_start(bias1[i][:], b1[bass.ds(e, 1), :].rearrange("a (k p) -> p (a k)", p=P)).then_inc(arrived[i], 16)

            load(0, 0)
            sp.dma_start(b2_rows[:], b2.unsqueeze(0).to_broadcast([P, n_experts, D])).then_inc(b2_in, 16)
            load(1, 1)
            with sp.Fori(0, n_experts // 2 - 1) as o:
                for i in range(2):
                    sp.wait_ge(down_done, 1 + o * (STEPS * U) + (i + 1) * (OUT * U))
                    load(o * 2 + 2 + i, i)
            for scatter in beside:
                scatter.finish(sp)

        if beside:
            @block.gpsimd
            def _(pool):
                for scatter in beside:
                    scatter.run(pool)

        @block.tensor
        def _(pe):
            pe.sem_inc(down_done, 1)
            with pe.Fori(0, n_experts // 2) as o:
                def down_step(s):
                    pe.wait_ge(hid_ready, 1 + o * (STEPS * KH) + (s + 1) * KH)
                    for j in range(U):
                        r = s * U + j
                        pe.wait_ge(added, 1 + o * (STEPS * U) + max(r - 3, 0))
                        for k in range(KH):
                            ins = nc.tensor.matmul(down[r % 4][:, 0:D],
                                                   hid[s % 2][:, k, :, :].rearrange("p a n -> p (a n)")[:, j * P:(j + 1) * P],
                                                   w2[s // OUT][:, k, :], start=(k == 0), stop=(k == KH - 1))
                        ins.then_inc(down_done, 1)

                for s in range(STEPS):
                    e, grp = s // OUT, s % OUT
                    if grp == 0:
                        pe.wait_ge(arrived[e], o * 48 + 48)
                    for m in range(KH):
                        q = s * KH + m
                        pe.wait_ge(hid_ready, 1 + o * (STEPS * KH) + max(q - 1, 0))
                        for k in range(KD):
                            for a in range(2):
                                col = grp * U * P + a * HALF
                                ins = nc.tensor.matmul(up[q % 2][:, a, 0:HALF], w1[e][:, k, m * P:(m + 1) * P],
                                                       S.xnT[:, k, col:col + HALF], start=(k == 0), stop=(k == KD - 1))
                        ins.then_inc(up_done, 1)
                    if s >= 1:
                        down_step(s - 1)
                down_step(STEPS - 1)

        @block.scalar
        def _(act):
            nc.scalar.preload_act_table(ACT.Gelu)
            act.sem_inc(hid_ready, 1)
            with act.Fori(0, n_experts // 2) as o:
                for s in range(STEPS):
                    act.wait_ge(down_done, 1 + o * (STEPS * U) + max(s - 1, 0) * U)
                    for m in range(KH):
                        act.wait_ge(up_done, o * (STEPS * KH) + s * KH + m + 1)
                        nc.scalar.activation(hid[s % 2][:, m, :, :], up[m % 2][:, :, 0:HALF], ACT.Gelu,
                                             bias=bias1[s // OUT][:, m:m + 1]).then_inc(hid_ready, 1)

        @block.vector
        def _(v):
            v.sem_inc(added, 1)
            v.wait_ge(b2_in, 16)
            with v.Fori(0, n_experts) as e:
                for t in range(NT):
                    nc.vector.scalar_tensor_tensor(S.x[:, t * D:(t + 1) * D], b2_rows[:, bass.ds(e, 1), :].rearrange("p a d -> p (a d)"),
                                                   gate[:, t, bass.ds(e, 1)], S.x[:, t * D:(t + 1) * D], ALU.mult, ALU.add)
                v.drain()
            with v.Fori(0, n_experts // 2) as o:
                for s in range(STEPS):
                    for j in range(U):
                        r, t = s * U + j, (s % OUT) * U + j
                        v.wait_ge(down_done, 1 + o * (STEPS * U) + r + 1)
                        nc.vector.scalar_tensor_tensor(S.x[:, t * D:(t + 1) * D], down[r % 4][:, 0:D],
                                                       gate[:, t, bass.ds(o * 2 + s // OUT, 1)], S.x[:, t * D:(t + 1) * D],
                                                       ALU.mult, ALU.add).then_inc(added, 1)
                    if s % OUT == OUT - 1:
                        v.drain()


def choose_two(nc, v, S, score, n, first, second, tmp, top):
    for r, pick in enumerate((first, second)):
        nc.vector.tensor_reduce(top[:, :, r], score[:], AX.X, ALU.max)
        v.drain()
        nc.vector.tensor_tensor(pick[:], score[:], top[:, :, r:r + 1].to_broadcast([P, NT, n]), ALU.is_equal)
        v.drain()
        nc.vector.tensor_tensor(pick[:], pick[:], S.countdown[:, 0:n].unsqueeze(1).to_broadcast([P, NT, n]), ALU.mult)
        v.drain()
        nc.vector.tensor_reduce(tmp[:], pick[:], AX.X, ALU.max)
        v.drain()
        nc.vector.tensor_tensor(pick[:], pick[:], tmp[:].unsqueeze(2).to_broadcast([P, NT, n]), ALU.is_equal)
        v.drain()
        if r == 0:
            nc.vector.scalar_tensor_tensor(score[:], pick[:], -BIG, score[:], ALU.mult, ALU.add)
            v.drain()


def emit_top2_mask(nc, S):
    with ExitStack() as ctx:
        sb = lambda n, s, d: ctx.enter_context(nc.sbuf_tensor("t2" + n, s, d))
        first, second = sb("a", [P, NT, NE0], F32), sb("b", [P, NT, NE0], F32)
        tmp, top = sb("c", [P, NT], F32), sb("d", [P, NT, 2], F32)
        block = ctx.enter_context(nc.Block())

        @block.vector
        def _(v):
            choose_two(nc, v, S, S.gate0, NE0, first, second, tmp, top)
            nc.vector.tensor_tensor(S.gate0[:], first[:], second[:], ALU.add)
            v.drain()


def emit_batchnorm(nc, S, A):
    sem = S.sem
    loaded, summed, centred, squared, sq_summed, var_in, rooted = (sem("bn_" + n) for n in (
        "in", "sum", "cen", "sq", "sqsum", "var", "root"))
    LAST = N - (NT - 1) * P
    with ExitStack() as ctx:
        sb = lambda n, s, d: ctx.enter_context(nc.sbuf_tensor("bn" + n, s, d))
        gamma, beta, mean, root = (sb(n, [P, D], F32) for n in ("gamma", "beta", "mean", "root"))
        sq = sb("sq", [P, NT * D], F32)
        ps = [ctx.enter_context(nc.psum_tensor(f"bnps{i}", [P, 512], F32)) for i in range(2)]
        block = ctx.enter_context(nc.Block())

        @block.sync
        def _(sp):
            sp.dma_start(gamma[:], A["bn_gamma"].unsqueeze(0).to_broadcast([P, D])).then_inc(loaded, 16)
            sp.dma_start(beta[:], A["bn_beta"].unsqueeze(0).to_broadcast([P, D])).then_inc(loaded, 16)

        @block.tensor
        def _(pe):
            def sum_over_nodes(ps, a):
                for t in range(NT):
                    k = P if t < NT - 1 else LAST
                    ins = nc.tensor.matmul(ps[:, 0:D], S.ones[0:k, 0:P], a[0:k, t * D:(t + 1) * D],
                                           start=(t == 0), stop=(t == NT - 1))
                return ins

            sum_over_nodes(ps[0], S.agg).then_inc(summed, 1)
            pe.wait_ge(squared, 1)
            sum_over_nodes(ps[1], sq).then_inc(sq_summed, 1)

        @block.scalar
        def _(act):
            nc.scalar.preload_act_table(ACT.Sqrt)
            act.wait_ge(centred, 1)
            nc.scalar.activation(sq[:], S.agg[:], ACT.Square).then_inc(squared, 1)
            act.wait_ge(var_in, 1)
            nc.scalar.activation(root[:], root[:], ACT.Sqrt).then_inc(rooted, 1)

        @block.vector
        def _(v):
            agg3 = S.agg[:].rearrange("p (t d) -> p t d", d=D)
            x3 = S.x[:].rearrange("p (t d) -> p t d", d=D)
            bc = lambda row: row[:].unsqueeze(1).to_broadcast([P, NT, D])
            v.wait_ge(summed, 1)
            nc.vector.tensor_scalar(mean[:], ps[0][:, 0:D], 1.0 / N, None, ALU.mult)
            v.drain()
            nc.vector.tensor_tensor(agg3, agg3, bc(mean), ALU.subtract).then_inc(centred, 1)
            v.wait_ge(sq_summed, 1)
            nc.vector.tensor_scalar(root[:], ps[1][:, 0:D], 1.0 / N, LNEPS, ALU.mult, ALU.add).then_inc(var_in, 1)
            v.wait_ge(rooted, 1)
            nc.vector.reciprocal(root[:], root[:])
            v.drain()
            v.wait_ge(loaded, 32)
            nc.vector.tensor_tensor(root[:], root[:], gamma[:], ALU.mult)
            v.drain()
            nc.vector.tensor_tensor(agg3, agg3, bc(root), ALU.mult)
            v.drain()
            nc.vector.tensor_tensor(agg3, agg3, bc(beta), ALU.add)
            v.drain()
            nc.vector.scalar_tensor_tensor(S.x[:], S.agg[:], 0.0, S.x[:], ALU.max, ALU.add)
            v.drain()


class Scatter:

    def __init__(self, nc, S, tag, rec, rec_dram, first, last, rec_sb=None, stage=None):
        self.nc, self.rec, self.rec_dram, self.rec_sb = nc, rec, rec_dram, rec_sb
        self.first, self.last = first // 8, last // 8
        self.copied, self.back = S.sem(tag + "_copy"), S.sem(tag + "_back")
        self.put = [S.sem(f"{tag}_put{i}") for i in range(8)]
        self.slot = stage.enter_context(nc.sbuf_tensor(tag + "_slot", [P, 8, rec.shape[2]], I32))

    def copy_records(self, act):
        def trip(o, is_first):
            for i in range(8):
                if not is_first:
                    act.wait_ge(self.put[i], 16 * (o - self.first))
                at = act.snap(o * 8 + (i + 1), min_val=1, max_val=self.last * 8)
                self.nc.scalar.copy(self.slot[:, i:i + 1, :], self.rec[:, bass.ds(at, 1), :]).then_inc(self.copied, 1)

        with act.Fori(self.first, self.first + 1) as o:
            trip(o, True)
        with act.Fori(self.first + 1, self.last) as o:
            trip(o, False)

    def run_copied(self, pool):
        count = pool.alloc_register("copied_count")
        pool.reg_mov(count, 0)
        with pool.Fori(self.first, self.last):
            for i in range(8):
                pool.reg_add(count, count, 1)
                pool.wait_ge(self.copied, 1)
                pool.wait_ge(self.copied, count)
                pool.indirect_dma_start(self.rec_dram, bass.IndirectOffsetOnAxis(ap=self.slot[:, i, 0:1], axis=0),
                                        self.slot[:, i, 1:self.rec.shape[2]], None).then_inc(self.put[i], 16)

    def run(self, pool):
        nc, slot, R = self.nc, self.slot, self.rec.shape[2] - 1

        def trip(o, is_first):
            for i in range(8):
                if not is_first:
                    pool.wait_ge(self.put[i], 16 * (o - self.first))
                count = pool.snap(o * 8 + (i + 1), min_val=1, max_val=self.last * 8)
                nc.gpsimd.tensor_copy(slot[:, i:i + 1, :], self.rec[:, bass.ds(count, 1), :]).then_inc(self.copied, 1)
                count = pool.snap(o * 8 + i + 1)
                pool.wait_ge(self.copied, 1)
                pool.wait_ge(self.copied, count)
                pool.indirect_dma_start(self.rec_dram, bass.IndirectOffsetOnAxis(ap=slot[:, i, 0:1], axis=0),
                                        slot[:, i, 1:R + 1], None).then_inc(self.put[i], 16)

        if self.first:
            pool.sem_inc(self.copied, self.first * 8)
        with pool.Fori(self.first, self.first + 1) as o:
            trip(o, True)
        with pool.Fori(self.first + 1, self.last) as o:
            trip(o, False)

    def finish(self, sp):
        for i in range(8):
            sp.wait_ge(self.put[i], 16 * (self.last - self.first))
        if self.rec_sb is not None:
            sp.dma_start(self.rec_sb[:], self.rec_dram.rearrange("(p c) r -> p c r", p=P)).then_inc(self.back, 16)
            sp.wait_ge(self.back, 16)


def emit_rank_edges(nc, S, tag, n_chunks, block, take, give, weight, slots, rec, rec_dram, ranges):
    sem = lambda n: S.sem(tag + n)
    R = 3 if weight is not None else 2
    GC, GS, GB = n_chunks, slots, block * P
    KB = -(-n_chunks // block) + 1
    loaded, filled, hots, ranked, tile_read, emptied = (sem("_" + n) for n in (
        "in", "fill", "hot", "rank", "read", "empty"))
    with ExitStack() as ctx:
        sb = lambda n, s, d: ctx.enter_context(nc.sbuf_tensor(tag + "_" + n, s, d))
        srci, dsti, tilei = (sb(n, [P, GC], I32) for n in ("src", "dst", "tile"))
        tilef, pos, incl, part, zero = (sb(n, [P, GC], F32) for n in ("tilef", "pos", "incl", "part", "zero"))
        hot = sb("hot", [P, NT, GC], BF16)
        trib, onesb = sb("trib", [P, P], BF16), sb("onesb", [P, P], BF16)
        blocks = sb("blocks", [P, 1], F32)
        base = sb("base", [P, 1], F32)
        cnt = sb("cnt", [P, 1], F32)
        starts, under = sb("starts", [P, KB], F32), sb("under", [P, KB], F32)
        row = sb("row", [P, NT + 1], F32)
        empty = sb("empty", [P, GS, R], I32)
        psr = ctx.enter_context(nc.psum_tensor(tag + "_psr", [P, 512], F32))
        pst = ctx.enter_context(nc.psum_tensor(tag + "_pst", [P, 512], F32))
        program = ctx.enter_context(nc.Block())

        @program.sync
        def _(sp):
            sp.dma_start(srci[:], take).then_inc(loaded, 16)
            sp.dma_start(dsti[:], give).then_inc(loaded, 16)
            sp.wait_ge(filled, 1)
            sp.dma_start(rec_dram.rearrange("(p c) r -> p c r", p=P), empty[:]).then_inc(emptied, 16)
            sp.wait_ge(emptied, 16)

        @program.gpsimd
        def _(pool):
            nc.gpsimd.memset(empty[:, :, 0:1], 0)
            if R == 3:
                nc.gpsimd.memset(empty[:, :, 2:3], 0)
            nc.gpsimd.memset(empty[:, :, 1:2], 2 * P).then_inc(filled, 1)

        @program.tensor
        def _(pe):
            pe.wait_ge(hots, 1)
            with pe.Fori(0, NT) as t:
                pe.wait_ge(tile_read, t + 1)
                nc.tensor.matmul(psr[:, 0:GC], trib[:], hot[:, bass.ds(t, 1), :].rearrange("p a c -> p (a c)"), start=True, stop=True)
                nc.tensor.matmul(pst[:, 0:GC], onesb[:], hot[:, bass.ds(t, 1), :].rearrange("p a c -> p (a c)"),
                                 start=True, stop=True).then_inc(ranked, 1)

        @program.vector
        def _(v):
            v.sem_inc(tile_read, 1)
            nc.vector.tensor_copy(trib[:], S.tri[:])
            nc.vector.tensor_copy(onesb[:], S.ones[:, 0:P])
            nc.vector.memset(zero[:], 0.0)
            nc.vector.memset(pos[:], 0.0)
            nc.vector.memset(blocks[:], 0.0)
            nc.vector.memset(row[:], 0.0)
            nc.vector.tensor_scalar(starts[:], S.iota[:, 0:KB], float(GB), None, ALU.mult)
            v.wait_ge(loaded, 32)
            nc.vector.tensor_scalar(tilei[:], dsti[:], 7, None, ALU.logical_shift_right)
            nc.vector.tensor_scalar(dsti[:], dsti[:], P - 1, None, ALU.bitwise_and)
            nc.vector.tensor_copy(rec[:, 1:GC + 1, 1], srci[:])
            if weight is not None:
                nc.vector.tensor_copy(rec[:, 1:GC + 1, 3].bitcast(F32), weight)
            v.drain()
            nc.vector.tensor_copy(tilef[:], tilei[:])
            nc.vector.tensor_copy(rec[:, 1:GC + 1, 2], dsti[:])
            v.drain()
            nc.vector.tensor_tensor(hot[:], tilef[:].unsqueeze(1).to_broadcast([P, NT, GC]),
                                    S.iota[:, 0:NT].unsqueeze(2).to_broadcast([P, NT, GC]), ALU.is_equal)
            v.drain().then_inc(hots, 1)
            with v.Fori(0, NT) as t:
                nc.vector.tensor_scalar(base[:], blocks[:], float(GB), None, ALU.mult)
                v.wait_ge(ranked, t + 1)
                nc.vector.tensor_tensor_scan(incl[:], pst[:, 0:GC], zero[:], 0.0, ALU.add, ALU.add)
                v.drain()
                nc.vector.tensor_tensor(part[:], incl[:], pst[:, 0:GC], ALU.subtract)
                nc.vector.tensor_scalar(under[:], starts[:], incl[:, GC - 1:GC], None, ALU.is_lt)
                v.drain()
                nc.vector.tensor_tensor(part[:], part[:], psr[:, 0:GC], ALU.add)
                nc.vector.tensor_reduce(cnt[:], under[:], AX.X, ALU.add)
                v.drain().then_inc(tile_read, 1)
                nc.vector.scalar_tensor_tensor(part[:], part[:], base[:, 0:1], hot[:, bass.ds(t, 1), :].rearrange("p a c -> p (a c)"),
                                               ALU.add, ALU.mult)
                nc.vector.tensor_scalar(cnt[:], cnt[:], 1.0, None, ALU.max)
                v.drain()
                nc.vector.tensor_tensor(pos[:], pos[:], part[:], ALU.add)
                nc.vector.tensor_tensor(blocks[:], blocks[:], cnt[:], ALU.add)
                v.drain()
                nc.vector.tensor_copy(row[:, bass.ds(t + 1, 1)], blocks[:])
            v.drain()
            nc.vector.tensor_copy(ranges[:], row[:])
            nc.vector.tensor_copy(tilei[:], pos[:])
            v.drain()
            nc.vector.tensor_scalar(dsti[:], tilei[:], P - 1, None, ALU.bitwise_and)
            nc.vector.tensor_scalar(srci[:], tilei[:], 7, None, ALU.logical_shift_right)
            v.drain()
            nc.vector.tensor_copy(part[:], dsti[:])
            nc.vector.tensor_copy(pos[:], srci[:])
            v.drain()
            nc.vector.scalar_tensor_tensor(part[:], part[:], float(GS), pos[:], ALU.mult, ALU.add)
            v.drain()
            nc.vector.tensor_copy(rec[:, 1:GC + 1, 0], part[:])
            v.drain()


def emit_routing(nc, S, A):
    sem = S.sem
    gathered = [sem(f"gt_g{i}") for i in range(BL)]
    indexed, kept, lanes, best, best_t, evac, vals = (sem("gt_" + n) for n in ("idx", "kept", "lanes", "best", "bestT", "evac", "vals"))
    masked, spread_done, maxed, end_read = (sem("gt_" + n) for n in ("msk", "spr", "mx", "endr"))
    cleared, hot, hot_t, hot_tc, ends, logit, expd, weighed, hot2, added, closed, closed_read = (sem("gt_" + n) for n in (
        "clear", "hot", "hotT", "hotTc", "ends", "logit", "exp", "w", "hot2", "agg", "closed", "clr"))
    loaded, var_in, rooted, dz, de = (sem("gt_" + n) for n in ("in", "var", "root", "dz", "de"))
    with ExitStack() as ctx:
        sb = lambda n, s, d: ctx.enter_context(nc.sbuf_tensor("gt_" + n, s, d))
        idx = sb("idx", [P, BL], I32)
        land = sb("land", [P, BL, GW], F32)
        rows = sb("rows", [P, GS, GW], F32)
        lane = sb("lane", [P, GS + BL], F32)
        nb = sb("nb", [P, 2 * BL, P], BF16)
        top = sb("top", [P, HEADS, P], F32)
        ms = sb("ms", [P, NT, HEADS], F32)
        val = sb("val", [P, NT, 2 * HEADS], F32)
        onehotb = sb("hotb", [P, BL, P], BF16)
        onehot = sb("hot", [P, BL, P], BF16)
        onehot_t = sb("hotT", [P, BL, P], BF16)
        val_parts = sb("valparts", [P, NT, 3, 2 * HEADS], BF16)
        part_sums = sb("partsums", [P, NT, 3, GW], F32)
        parts = sb("parts", [P, GS, 3, GW], BF16)
        early = parts[:].rearrange("p i k n -> p (i k n)").bitcast(F32)
        views, at = [], 0
        for count in (BL * HEADS * P, (GS + NT) * HEADS, GS * 2 * HEADS, 2 * HEADS * P):
            views.append(early[:, at:at + count])
            at += count
        spread_score = views[0].rearrange("p (i h n) -> p i h n", i=BL, h=HEADS)
        z2 = views[1].rearrange("p (i h) -> p i h", h=HEADS)
        end = views[2].rearrange("p (i k) -> p i k", k=2 * HEADS)
        top2 = views[3].rearrange("p (i h n) -> p i h n", i=2, h=HEADS)
        z = sb("z", [P, GS + NT, HEADS], F32)
        sums = sb("sums", [P, NT, GW], F32)
        tmp = sb("tmp", [P, NT, HW], F32)
        mean, var = sb("mean", [P, NT], F32), sb("var", [P, NT], F32)
        b_gat, gamma, beta = (sb(n, [P, HW], F32) for n in ("bgat", "gamma", "beta"))
        first, second = sb("first", [P, NT, NE1], F32), sb("second", [P, NT, NE1], F32)
        topv = sb("topv", [P, NT, 2], F32)
        psB = ctx.enter_context(nc.psum_tensor("gt_psB", [P, 2, 1024], BF16))
        psT = ctx.enter_context(nc.psum_tensor("gt_psT", [P, BL, P], F32))
        psE = ctx.enter_context(nc.psum_tensor("gt_psE", [P, 2, 512], F32))
        psO = ctx.enter_context(nc.psum_tensor("gt_psO", [P, 512], F32))
        block = ctx.enter_context(nc.Block())
        zs = z[:, GS:GS + NT, :]
        own = S.gat_sb

        @block.sync
        def _(sp):
            for dst, name in ((b_gat, "b_gat"), (gamma, "ln_gamma"), (beta, "ln_beta")):
                sp.dma_start(dst[:], A[name].unsqueeze(0).to_broadcast([P, HW])).then_inc(loaded, 16)

        @block.gpsimd
        def _(pool):
            total = pool.value_load(S.granges[0:1, NT:NT + 1], min_val=0, max_val=GBLOCKS)
            with pool.Fori(0, total) as g:
                c = slot_of(nc, pool, g, GBLOCKS)
                for i in range(BL):
                    pool.wait_ge(kept, g * BL + i + 1)
                    pool.wait_ge(spread_done, g * BL + i + 2)
                    nc.gpsimd.tensor_copy(idx[:, i:i + 1], S.rec_sb[:, bass.ds(c + i, 1), 0:1].rearrange("p a b -> p (a b)")
                                          ).then_inc(indexed, 1)
                    count = pool.snap(g * BL + i + 1)
                    pool.wait_ge(indexed, 1)
                    pool.wait_ge(indexed, count)
                    pool.indirect_dma_start(land[:, i, :], None, S.table_gat,
                                            bass.IndirectOffsetOnAxis(ap=idx[:, i:i + 1], axis=0)).then_inc(gathered[i], 16)

        @block.vector
        def _(v):
            def split(whole, into):
                for k in range(3):
                    nc.vector.tensor_copy(into[:, :, k, :], whole)
                    v.drain()
                    if k < 2:
                        nc.vector.tensor_tensor(whole, whole, into[:, :, k, :], ALU.subtract)
                        v.drain()

            nc.vector.memset(rows[:], 0.0)
            nc.vector.memset(end[:], 0.0)
            v.drain().then_inc(cleared, 1)
            v.sem_inc(hot_t, 2)
            v.sem_inc(added, BL)
            v.sem_inc(maxed, 2)
            v.sem_inc(end_read, 1)
            nc.vector.memset(lane[:, GS:GS + BL], 0.0)
            nc.vector.tensor_copy(lane[:, 0:GS], S.rec_sb[:, :, 1])
            v.drain()
            def mask_block(g):
                c = nc.s_assert_within(g * BL, 0, GS, skip_runtime_bounds_check_because="one block more than there are")
                at = v.snap(g % 2 * BL)
                v.wait_ge(spread_done, g * BL + 1)
                for i in range(BL):
                    nc.vector.tensor_scalar(nb[:, bass.ds(at + i, 1), :].rearrange("p a n -> p (a n)"), S.iotab[:],
                                            lane[:, bass.ds(c + i, 1)], -BIG, ALU.not_equal, ALU.mult).then_inc(masked, 1)

            mask_block(0)
            start = v.alloc_register("gt_start_v")
            v.reg_mov(start, 0)
            with v.Fori(0, NT) as t:
                g1 = v.value_load(S.granges[0:1, bass.ds(t + 1, 1)], min_val=0, max_val=GBLOCKS)
                nc.vector.memset(top2[:], -BIG)
                v.drain()
                with v.Fori(start, g1) as g:
                    mask_block(g + 1)
                    for a in range(2):
                        v.wait_ge(spread_done, g * BL + BL + 2 * a + 3)
                        nc.vector.tensor_tensor(top2[:], top2[:], spread_score[:, 2 * a:2 * a + 2, :, :], ALU.max).then_inc(maxed, 1)
                        v.drain()
                v.drain()
                nc.vector.tensor_tensor(top[:], top2[:, 0, :, :], top2[:, 1, :, :], ALU.max)
                v.reg_mov(start, g1)
                v.drain().then_inc(best, 1)
                v.wait_ge(best_t, t + 1)
                nc.vector.tensor_reduce(ms[:, bass.ds(t, 1), :], psT[:].unsqueeze(1), AX.X, ALU.max).then_inc(evac, 1)
            v.drain()
            src_own, dst_own = own[:, :, HW:HW + HEADS], own[:, :, GW:GW + HEADS]
            nc.vector.tensor_tensor(ms[:], ms[:], src_own, ALU.max)
            v.drain()
            nc.vector.tensor_tensor(ms[:], ms[:], dst_own, ALU.add)
            nc.vector.tensor_tensor(zs, src_own, dst_own, ALU.add)
            v.drain()
            nc.vector.tensor_copy(val[:, :, 0:HEADS], dst_own)
            nc.vector.scalar_tensor_tensor(val[:, :, HEADS:2 * HEADS], ms[:], 0.2, ms[:], ALU.mult, ALU.max)
            v.drain()
            nc.vector.tensor_copy(ms[:], val[:, :, HEADS:2 * HEADS])
            v.drain()
            split(val[:], val_parts)
            v.drain().then_inc(vals, 1)
            total = v.value_load(S.granges[0:1, NT:NT + 1], min_val=0, max_val=GBLOCKS)
            def one_hots(g):
                c = slot_of(nc, v, g, GBLOCKS)
                v.wait_ge(hot_t, 2 * g + 2)
                nc.vector.tensor_tensor(onehotb[:], S.iota[:, 0:P].unsqueeze(1).to_broadcast([P, BL, P]),
                                        lane[:, bass.ds(c, BL)].unsqueeze(2).to_broadcast([P, BL, P]), ALU.is_equal
                                        ).then_inc(hot, 1)

            def keep_ends(g):
                c = slot_of(nc, v, g, GBLOCKS)
                v.wait_ge(ends, g + 1)
                nc.vector.tensor_copy(end[:, bass.ds(c, BL), :].rearrange("p (a i) k -> p a (i k)", a=2),
                                      psE[:, :, 0:BL * HEADS]).then_inc(end_read, 1)

            one_hots(0)
            with v.Fori(1, total) as g:
                one_hots(g)
                keep_ends(g - 1)
            with v.Fori(total - 1, total) as g:
                keep_ends(g)
            v.drain()
            nc.vector.tensor_tensor(z[:, 0:GS, :], rows[:, :, HW:GW], end[:, :, 0:HEADS], ALU.add)
            v.drain()
            nc.vector.scalar_tensor_tensor(z2[:], z[:], 0.2, z[:], ALU.mult, ALU.max)
            v.drain()
            nc.vector.tensor_tensor(z2[:, 0:GS, :], z2[:, 0:GS, :], end[:, :, HEADS:2 * HEADS], ALU.subtract)
            nc.vector.tensor_tensor(z2[:, GS:GS + NT, :], z2[:, GS:GS + NT, :], ms[:], ALU.subtract)
            v.drain()
            nc.vector.tensor_scalar(z2[:], z2[:], 0.0, None, ALU.min).then_inc(logit, 1)
            v.wait_ge(expd, 1)
            spread4 = z[:, 0:GS, :].unsqueeze(3).to_broadcast([P, GS, HEADS, HC])
            by_head = rows[:, :, 0:HW].rearrange("p i (h k) -> p i h k", h=HEADS)
            nc.vector.tensor_tensor(by_head, by_head, spread4, ALU.mult)
            nc.vector.tensor_copy(rows[:, :, HW:GW], z[:, 0:GS, :])
            v.drain()
            split(rows[:], parts)
            v.drain().then_inc(weighed, 1)
            with v.Fori(0, total) as g:
                c = slot_of(nc, v, g, GBLOCKS)
                for i in range(BL):
                    v.wait_ge(added, g * BL + i + 1)
                    nc.vector.tensor_scalar(onehot[:, i, :], S.iotab[:], lane[:, bass.ds(c + i, 1)], None, ALU.is_equal
                                            ).then_inc(hot2, 1)
            v.wait_ge(closed_read, NT + 1)
            nc.vector.tensor_tensor(sums[:], part_sums[:, :, 1, :], part_sums[:, :, 2, :], ALU.add)
            v.drain()
            nc.vector.tensor_tensor(sums[:], sums[:], part_sums[:, :, 0, :], ALU.add)
            v.drain()
            heads = lambda a: a.rearrange("p t (h k) -> p t h k", h=HEADS)
            spread = lambda a: a.unsqueeze(3).to_broadcast([P, NT, HEADS, HC])
            row = lambda r: r[:].unsqueeze(1).to_broadcast([P, NT, HW])
            nc.vector.tensor_tensor(heads(tmp[:]), heads(own[:, :, 0:HW]), spread(zs), ALU.mult)
            v.drain()
            nc.vector.tensor_tensor(zs, zs, sums[:, :, HW:GW], ALU.add)
            v.drain()
            nc.vector.tensor_tensor(tmp[:], tmp[:], sums[:, :, 0:HW], ALU.add)
            nc.vector.tensor_scalar(zs, zs, 1e-16, None, ALU.add)
            v.drain()
            nc.vector.reciprocal(zs, zs)
            v.drain()
            nc.vector.tensor_tensor(heads(tmp[:]), heads(tmp[:]), spread(zs), ALU.mult)
            v.drain()
            v.wait_ge(loaded, 48)
            nc.vector.tensor_tensor(tmp[:], tmp[:], row(b_gat), ALU.add)
            v.drain()
            nc.vector.tensor_reduce(mean[:], tmp[:], AX.X, ALU.add)
            v.drain()
            nc.vector.tensor_scalar(mean[:], mean[:], 1.0 / HW, None, ALU.mult)
            v.drain()
            nc.vector.tensor_tensor(tmp[:], tmp[:], mean[:].unsqueeze(2).to_broadcast([P, NT, HW]), ALU.subtract)
            v.drain()
            nc.vector.tensor_tensor(sums[:, :, 0:HW], tmp[:], tmp[:], ALU.mult)
            v.drain()
            nc.vector.tensor_reduce(var[:], sums[:, :, 0:HW], AX.X, ALU.add)
            v.drain()
            nc.vector.tensor_scalar(var[:], var[:], 1.0 / HW, LNEPS, ALU.mult, ALU.add).then_inc(var_in, 1)
            v.wait_ge(rooted, 1)
            nc.vector.reciprocal(var[:], var[:])
            v.drain()
            nc.vector.tensor_tensor(tmp[:], tmp[:], var[:].unsqueeze(2).to_broadcast([P, NT, HW]), ALU.mult)
            v.drain()
            nc.vector.tensor_tensor(tmp[:], tmp[:], row(gamma), ALU.mult)
            v.drain()
            nc.vector.tensor_tensor(tmp[:], tmp[:], row(beta), ALU.add)
            v.drain()
            nc.vector.tensor_reduce(S.gate1[:], tmp[:].rearrange("p t (h k) -> p t k h", h=HEADS), AX.X, ALU.add)
            v.drain()
            nc.vector.tensor_scalar(S.gate1[:], S.gate1[:], 1.0 / HEADS, None, ALU.mult)
            v.drain()
            choose_two(nc, v, S, S.gate1, NE1, first, second, mean, topv)
            nc.vector.tensor_tensor(topv[:, :, 1], topv[:, :, 1], topv[:, :, 0], ALU.subtract).then_inc(dz, 1)
            v.wait_ge(de, 1)
            nc.vector.tensor_scalar(topv[:, :, 0], topv[:, :, 1], 1.0, None, ALU.add)
            v.drain()
            nc.vector.reciprocal(topv[:, :, 0], topv[:, :, 0])
            v.drain()
            nc.vector.tensor_tensor(topv[:, :, 1], topv[:, :, 1], topv[:, :, 0], ALU.mult)
            v.drain()
            nc.vector.tensor_tensor(first[:], first[:], topv[:, :, 0:1].to_broadcast([P, NT, NE1]), ALU.mult)
            nc.vector.tensor_tensor(second[:], second[:], topv[:, :, 1:2].to_broadcast([P, NT, NE1]), ALU.mult)
            v.drain()
            nc.vector.tensor_tensor(S.gate1[:], first[:], second[:], ALU.add)
            v.drain()

        @block.scalar
        def _(act):
            nc.scalar.preload_act_table(ACT.Exp)
            total = act.value_load(S.granges[0:1, NT:NT + 1], min_val=0, max_val=GBLOCKS)
            act.sem_inc(kept, BL)
            act.sem_inc(spread_done, BL + 1)
            act.sem_inc(hot_tc, 2)
            act.sem_inc(closed_read, 1)
            act.wait_ge(cleared, 1)
            with act.Fori(0, total) as g:
                c = slot_of(nc, act, g, GBLOCKS)
                mine = act.snap(g % 2 * BL)
                for i in range(BL):
                    act.wait_ge(gathered[i], g * 16 + 16)
                    nc.scalar.copy(rows[:, bass.ds(c + i, 1), :], land[:, i:i + 1, :]).then_inc(kept, 1)
                    act.wait_ge(masked, g * BL + i + 1)
                    act.wait_ge(maxed, g * 2 + i // 2 + 1)
                    for h in range(HEADS):
                        ins = nc.scalar.activation(spread_score[:, i, h:h + 1, :], nb[:, bass.ds(mine + i, 1), :], ACT.Identity,
                                                   bias=land[:, i, HW + h:HW + h + 1])
                    ins.then_inc(spread_done, 1)
            with act.Fori(0, total) as g:
                for a in range(2):
                    act.wait_ge(hot_t, 2 * g + a + 3)
                    nc.scalar.copy(onehot_t[:, 2 * a:2 * a + 2, :].rearrange("p i n -> p (i n)"), psB[:, a, 0:2 * P]).then_inc(hot_tc, 1)
            act.wait_ge(logit, 1)
            nc.scalar.activation(z[:], z2[:], ACT.Exp).then_inc(expd, 1)
            with act.Fori(0, NT) as t:
                act.wait_ge(closed, t + 1)
                nc.scalar.copy(part_sums[:, bass.ds(t, 1), :, :].rearrange("p a k n -> p (a k n)"), psO[:, 0:3 * GW]).then_inc(closed_read, 1)
            act.wait_ge(var_in, 1)
            nc.scalar.activation(var[:], var[:], ACT.Sqrt).then_inc(rooted, 1)
            act.wait_ge(dz, 1)
            nc.scalar.activation(topv[:, :, 1], topv[:, :, 1], ACT.Exp).then_inc(de, 1)

        @block.tensor
        def _(pe):
            with pe.Fori(0, NT) as t:
                pe.wait_ge(best, t + 1)
                for h in range(HEADS):
                    ins = nc.tensor.transpose(psT[:, h, :], top[:, h, :], S.ident[:])
                ins.then_inc(best_t, 1)
            pe.wait_ge(vals, 1)
            start = pe.alloc_register("gt_start_pe")
            pe.reg_mov(start, 0)
            with pe.Fori(0, NT) as t:
                g1 = pe.value_load(S.granges[0:1, bass.ds(t + 1, 1)], min_val=0, max_val=GBLOCKS)
                with pe.Fori(start, g1) as g:
                    for a in range(2):
                        if a == 0:
                            pe.wait_ge(hot, g + 1)
                        pe.wait_ge(hot_tc, 2 * g + a + 1)
                        for i in range(2):
                            ins = nc.tensor.transpose(psB[:, a, i * P:(i + 1) * P], onehotb[:, 2 * a + i, :], S.identb[:])
                        ins.then_inc(hot_t, 1)
                    pe.wait_ge(end_read, g + 1)
                    for a in range(2):
                        pe.wait_ge(hot_tc, 2 * g + a + 3)
                        for i in range(2):
                            for k in range(3):
                                ins = nc.tensor.matmul(psE[:, a, i * 2 * HEADS:(i + 1) * 2 * HEADS], onehot_t[:, 2 * a + i, :],
                                                       val_parts[:, bass.ds(t, 1), k, :].rearrange("p a n -> p (a n)"),
                                                       start=(k == 0), stop=(k == 2))
                    ins.then_inc(ends, 1)
                pe.reg_mov(start, g1)
            pe.wait_ge(weighed, 1)
            pe.reg_mov(start, 0)
            with pe.Fori(0, NT) as t:
                g1 = pe.value_load(S.granges[0:1, bass.ds(t + 1, 1)], min_val=0, max_val=GBLOCKS)
                pe.wait_ge(closed_read, t + 1)
                nc.tensor.matmul(psO[:, 0:3 * GW], S.zeros[0:1, 0:P], S.iota[0:1, 0:3 * GW], start=True, stop=False)
                with pe.Fori(start, g1) as g:
                    c = slot_of(nc, pe, g, GBLOCKS)
                    for i in range(BL):
                        pe.wait_ge(hot2, g * BL + i + 1)
                        nc.tensor.matmul(psO[:, 0:3 * GW], onehot[:, i, :],
                                         parts[:, bass.ds(c + i, 1), :, :].rearrange("p a k n -> p (a k n)"),
                                         start=False, stop=False).then_inc(added, 1)
                pe.reg_mov(start, g1)
                nc.tensor.matmul(psO[:, 0:3 * GW], S.zeros[0:1, 0:P], S.iota[0:1, 0:3 * GW], start=False, stop=True).then_inc(closed, 1)


class _Shared:
    pass


def build_kernel(nc, A, out):
    with ExitStack() as ctx:
        S = _Shared()
        taken = []

        def sem(name):
            taken.append(nc.alloc_semaphore(name=name))
            return taken[-1]

        def end_stage():
            nc.clear_and_free_semaphores(taken)
            nc.all_engine_barrier()
            taken.clear()

        S.sem = sem

        def sb(n, s, d, c=ctx):
            return c.enter_context(nc.sbuf_tensor("k_" + n, s, d))

        def dram(n, s, d):
            return nc.dram_tensor(n, s, d, kind="Internal").ap()

        S.x = sb("x", [P, NT * D], F32)
        S.iota = sb("iota", [P, NP], F32)
        S.lane = sb("lane", [P, 1], F32)
        S.ident, S.tri, S.zeros, S.ones = (sb(n, [P, P], F32) for n in ("ident", "tri", "zeros", "ones"))
        S.identb, S.iotab = sb("identb", [P, P], BF16), sb("iotab", [P, P], BF16)
        S.countdown = sb("countdown", [P, NE0], F32)
        S.src = sb("src", [P, NCP], I32)
        S.dstf, S.ew, S.score, S.srct = (sb(n, [P, NCP], F32) for n in ("dstf", "ew", "score", "srct"))
        S.ranges = sb("ranges", [P, NT], I32)
        S.granges = sb("granges", [P, NT + 1], I32)
        S.rec_sb = sb("rec", [P, GS, 2], I32)
        S.erec_sb = sb("erec", [P, ES, 3], I32)
        S.esource, S.elane, S.eweight = sb("esource", [P, ES], I32), sb("elane", [P, ES], F32), sb("eweight", [P, ES], F32)
        S.eranges = sb("eranges", [P, NT + 1], I32)
        S.gate0, S.gate1 = sb("gate0", [P, NT, NE0], F32), sb("gate1", [P, NT, NE1], F32)
        S.lane_row = dram("lane_row", [NC * P], BF16)
        recg = sb("recg", [P, GC + 1, 3], I32)
        rec_dram = dram("records", [P * GS, 2], I32)
        erec_dram = dram("erecords", [P * ES, 3], I32)
        table = dram("table", [NP, TW], F32)
        S.table_gat = dram("table_gat", [NP, GW], F32)

        with ExitStack() as stage:
            S.table_sb = sb("tbl0", [P, NT, TW], F32, stage)
            S.w_aug = sb("w_aug", [P, KD, D + 4], F32, stage)
            S.bn_row = sb("bn_row", [P, D], F32, stage)
            S.we_attn, S.bias_attn = sb("we_attn", [P, 1], F32, stage), sb("bias_attn", [P, 1], F32, stage)
            S.hs = sb("hs", [P, NT], F32, stage)
            S.src_tile = sb("src_tile", [P, NC, NT], BF16, stage)
            emit_setup(nc, S, A)

            def rows_and_score(v, o, i, ps):
                nc.vector.tensor_tensor(S.table_sb[:, bass.ds(o * U + i, 1), 0:D], ps[:, 0:D].unsqueeze(1),
                                        S.bn_row[:].unsqueeze(1), ALU.add)
                nc.vector.tensor_copy(S.hs[:, bass.ds(o * U + i, 1)], ps[:, D:D + 1])

            emit_layernorm_project(nc, S, "l0", S.w_aug, D + 1, False, rows_and_score, table, S.table_sb)
            emit_rank_edges(nc, S, "so", GC, BL, A["gsrc"], A["gdst"], None, GS, recg, rec_dram, S.granges)
            emit_edge_scores(nc, S, A, Scatter(nc, S, "sa", recg, rec_dram, 0, EARLY, stage=stage))
        emit_aggregate(nc, S, "a0", table, True)
        end_stage()

        with ExitStack() as stage:
            rece = sb("rece", [P, NC + 1, 4], I32, stage)
            emit_rank_edges(nc, S, "se", NC, BG, A["dst_pc"][:, 0:NC], A["src_pc"][:, 0:NC], S.ew[:, 0:NC], ES, rece, erec_dram,
                            S.eranges)
            S.xnT = sb("xnT0", [P, KD, NP], F32, stage)
            wg = sb("wg", [P, KD, NE0], F32, stage)
            bg = sb("bg", [P, NE0], F32, stage)
            wg_in = S.sem("wg_in")

            def load_gate(v):
                v.wait_ge(wg_in, 32)

            with nc.Block() as block:
                @block.sync
                def _(sp):
                    sp.dma_start(wg[:], A["Wg"].rearrange("(k p) e -> p k e", p=P)).then_inc(wg_in, 16)
                    sp.dma_start(bg[:], A["bg"].unsqueeze(0).to_broadcast([P, NE0])).then_inc(wg_in, 16)
                    sp.wait_ge(wg_in, 32)

            def gate_scores(v, o, i, ps):
                nc.vector.tensor_tensor(S.gate0[:, bass.ds(o * U + i, 1), :], ps.unsqueeze(1), bg[:].unsqueeze(1), ALU.add)

            emit_layernorm_project(nc, S, "l1", wg, NE0, True, gate_scores)
            emit_top2_mask(nc, S)
            beside = (Scatter(nc, S, "sb", recg, rec_dram, EARLY, GC, S.rec_sb, stage),
                      Scatter(nc, S, "sc", rece, erec_dram, 0, NC, S.erec_sb, stage))
            emit_experts(nc, S, "f0", A, NE0, S.gate0, beside)
        end_stage()

        with ExitStack() as stage:
            w_in = S.sem("w1_in")
            with ExitStack() as inner:
                S.table_sb = sb("tbl1", [P, NT, TW], F32, inner)
                w = sb("w_gcn", [P, KD, D], F32, inner)
                with nc.Block() as block:
                    @block.sync
                    def _(sp):
                        sp.dma_start(w[:], A["gcn_W"].rearrange("(k p) o -> p k o", p=P)).then_inc(w_in, 16)
                        sp.wait_ge(w_in, 16)

                    @block.vector
                    def _(v):
                        nc.vector.memset(S.table_sb[:, :, D:TW], 0.0)
                        nc.vector.tensor_copy(S.esource[:], S.erec_sb[:, :, 0])
                        nc.vector.tensor_copy(S.elane[:], S.erec_sb[:, :, 1])
                        nc.vector.tensor_copy(S.eweight[:], S.erec_sb[:, :, 2].bitcast(F32))
                        v.drain()

                def rows(v, o, i, ps):
                    nc.vector.tensor_copy(S.table_sb[:, bass.ds(o * U + i, 1), 0:D], ps.unsqueeze(1))

                emit_layernorm_project(nc, S, "l2", w, D, False, rows, table, S.table_sb)
            S.agg = sb("agg", [P, NT * D], F32, stage)
            S.bias_row = sb("bias_row", [P, D], F32, stage)
            bias_in = S.sem("bias_in")
            with nc.Block() as block:
                @block.sync
                def _(sp):
                    sp.dma_start(S.bias_row[:], A["gcn_bias"].unsqueeze(0).to_broadcast([P, D])).then_inc(bias_in, 16)
                    sp.wait_ge(bias_in, 16)
            emit_aggregate(nc, S, "a1", table, False)
            emit_batchnorm(nc, S, A)
        end_stage()

        with ExitStack() as stage:
            S.xnT = sb("xnT1", [P, KD, NP], F32, stage)
            with ExitStack() as inner:
                S.gat_sb = sb("gat", [P, NT, GW + HEADS], F32, inner)
                wgat = sb("wgat", [P, KD, HW], F32, inner)
                att = sb("att", [P, 2, HW], F32, inner)
                wgat_in = S.sem("wgat_in")
                with nc.Block() as block:
                    @block.sync
                    def _(sp):
                        sp.dma_start(wgat[:], A["W_gat"].rearrange("(k p) o -> p k o", p=P)).then_inc(wgat_in, 16)
                        sp.dma_start(att[:, 0, :], A["att_src"].unsqueeze(0).to_broadcast([P, HW])).then_inc(wgat_in, 16)
                        sp.dma_start(att[:, 1, :], A["att_dst"].unsqueeze(0).to_broadcast([P, HW])).then_inc(wgat_in, 16)
                        sp.wait_ge(wgat_in, 48)

                def rows(v, o, i, ps):
                    nc.vector.tensor_copy(S.gat_sb[:, bass.ds(o * U + i, 1), 0:HW], ps.unsqueeze(1))

                emit_layernorm_project(nc, S, "l3", wgat, HW, True, rows)
                prod = sb("prod", [P, NT, HW], F32, inner)
                tabled = S.sem("gat_tabled")
                stored = S.sem("gat_stored")
                with nc.Block() as block:
                    @block.vector
                    def _(v):
                        for k in range(2):
                            nc.vector.tensor_tensor(prod[:], S.gat_sb[:, :, 0:HW], att[:, k, :].unsqueeze(1).to_broadcast([P, NT, HW]), ALU.mult)
                            v.drain()
                            nc.vector.tensor_reduce(S.gat_sb[:, :, HW + k * HEADS:HW + (k + 1) * HEADS],
                                                    prod[:].rearrange("p t (h k) -> p t h k", h=HEADS), AX.X, ALU.add)
                            v.drain()
                        v.drain().then_inc(tabled, 1)

                    @block.sync
                    def _(sp):
                        sp.wait_ge(tabled, 1)
                        sp.dma_start(S.table_gat.rearrange("(t p) d -> p t d", p=P), S.gat_sb[:, :, 0:GW]).then_inc(stored, 16)
                        sp.wait_ge(stored, 16)
                emit_routing(nc, S, A)
            emit_experts(nc, S, "f1", A, NE1, S.gate1)

        done = S.sem("out_done")
        with nc.Block() as block:
            @block.sync
            def _(sp):
                rows = (NT - 1) * P
                x3 = S.x[:].rearrange("p (t d) -> p t d", d=D)
                sp.dma_start(out[0:rows, :].rearrange("(t p) d -> p t d", p=P), x3[:, 0:NT - 1, :]).then_inc(done, 16)
                sp.dma_start(out[rows:N, :], x3[0:N - rows, NT - 1, :]).then_inc(done, 16)
                sp.wait_ge(done, 32)
        end_stage()


def kernel(x, src, dst, edge_attr_128, edge_weight, L0_gnn_Wn, L0_gnn_bn, L0_gnn_We, L0_gnn_be, L0_gnn_attn, L0_ffn_Wg,
           L0_ffn_bg, L0_ffn_W1, L0_ffn_b1, L0_ffn_W2, L0_ffn_b2, L1_gnn_W, L1_gnn_bias, L1_gnn_gamma, L1_gnn_beta,
           L1_ffn_W_gat, L1_ffn_att_src, L1_ffn_att_dst, L1_ffn_b_gat, L1_ffn_ln_gamma, L1_ffn_ln_beta, L1_ffn_W1,
           L1_ffn_b1, L1_ffn_W2, L1_ffn_b2, L1_ffn_edge_index):
    import concourse.bacc as bacc
    from concourse.bass_utils import run_bass_kernel_spmd

    def padded(a, rows, value):
        a = np.asarray(a)
        return np.concatenate([a, np.full((rows - a.shape[0],) + a.shape[1:], value, a.dtype)])

    def chunks(a, n_chunks, value=0):
        return np.ascontiguousarray(padded(a, n_chunks * P, value).reshape(n_chunks, P).T)

    ge = np.asarray(L1_ffn_edge_index)
    arrays = {
        "x": padded(x, NP, 0), "src_pc": chunks(src, NCP), "dst_pc": chunks(dst, NCP, NP - 1),
        "src_pj": padded(src, NC * P, 0).reshape(P, NC), "ew_pc": chunks(edge_weight, NCP),
        "eaT": np.ascontiguousarray(padded(edge_attr_128, NC * P, 0).T),
        "Wn": L0_gnn_Wn, "WnT": np.ascontiguousarray(np.asarray(L0_gnn_Wn).T), "We": L0_gnn_We, "bn": L0_gnn_bn,
        "be": L0_gnn_be, "attn": np.asarray(L0_gnn_attn).reshape(-1),
        "Wg": L0_ffn_Wg, "bg": L0_ffn_bg, "f0_W1": L0_ffn_W1, "f0_b1": L0_ffn_b1, "f0_W2": L0_ffn_W2, "f0_b2": L0_ffn_b2,
        "gcn_W": L1_gnn_W, "gcn_bias": L1_gnn_bias, "bn_gamma": L1_gnn_gamma, "bn_beta": L1_gnn_beta,
        "W_gat": L1_ffn_W_gat, "att_src": np.asarray(L1_ffn_att_src).reshape(-1),
        "att_dst": np.asarray(L1_ffn_att_dst).reshape(-1), "b_gat": L1_ffn_b_gat, "ln_gamma": L1_ffn_ln_gamma,
        "ln_beta": L1_ffn_ln_beta, "f1_W1": L1_ffn_W1, "f1_b1": L1_ffn_b1, "f1_W2": L1_ffn_W2, "f1_b2": L1_ffn_b2,
        "gsrc": chunks(ge[0], GC), "gdst": chunks(ge[1], GC),
    }
    arrays = {"in_" + k: np.ascontiguousarray(v) for k, v in arrays.items()}
    nc = bacc.Bacc("TRN2", target_bir_lowering=False, num_devices=1)
    aps = {k[3:]: nc.dram_tensor(k, v.shape, mybir.dt.from_np(v.dtype), kind="ExternalInput").ap()
           for k, v in arrays.items()}
    out = nc.dram_tensor("out_x", (N, D), F32, kind="ExternalOutput").ap()
    build_kernel(nc, aps, out)
    r = run_bass_kernel_spmd(nc, [arrays], core_ids=[0])
    return r.results[0]["out_x"]
```
